# Optimizing a Trainium2 kernel written in Bass

```python
import numpy as np
import jax
import jax.numpy as jnp

def _softmax(x, axis=-1):
    return jax.nn.softmax(x, axis=axis)

def _gelu(x):
    return jax.nn.gelu(x, approximate=True)

def _silu(x):
    return jax.nn.silu(x)

def _sigmoid(x):
    return jax.nn.sigmoid(x)

def _layernorm(x, axis=-1, eps=1e-05):
    m = jnp.mean(x, axis=axis, keepdims=True)
    v = jnp.var(x, axis=axis, keepdims=True)
    return (x - m) / jnp.sqrt(v + eps)

def _scatter_add(tgt, idx, src, axis=0):
    return tgt.at[idx].add(src)

def _segment_sum(src, seg, n):
    return jax.ops.segment_sum(src, seg, n)
kernel_name = 'mk_flamingo_gated_d2_seqx_r4_67c017'

def setup_inputs(seed: int=0):
    np.random.seed(seed)
    _w = jnp.asarray

    def _rec_inputs():
        import jax
        import jax.numpy as jnp
        _rk = jax.random.key(seed)
        x = -0.0002928 + 1 * jax.random.normal(jax.random.fold_in(_rk, 1), (4, 512, 512), jnp.float32)
        _lenS = 512 - jax.random.randint(jax.random.fold_in(_rk, 7), (4,), 0, max(1, 512 // 4) + 1, jnp.int32)
        _lenS2 = 512 - jax.random.randint(jax.random.fold_in(_rk, 8), (4,), 0, max(1, 512 // 4) + 1, jnp.int32)
        _ctx_512P = jax.random.normal(jax.random.fold_in(_rk, 11), (4, 16, 128), jnp.float32)
        _ctx_512c = jax.random.dirichlet(jax.random.fold_in(_rk, 511), 0.3 * jnp.ones((16,), jnp.float32), (4, 512))
        _ctx_512t = jnp.einsum('bsk,bkd->bsd', _ctx_512c, _ctx_512P)
        _ctx_512t = _ctx_512t * jax.lax.rsqrt(jnp.mean(jnp.square(_ctx_512t)) + 1e-12) * 0.953939
        ctx_512 = 0.000227908 + 0.99994 * (_ctx_512t + 0.3 * jax.random.normal(jax.random.fold_in(_rk, 611), (4, 512, 128), jnp.float32))
        _g = jax.random.normal(jax.random.fold_in(_rk, 9001), (2, 2), jnp.float32)
        _g = jnp.sign(_g) * jnp.maximum(jnp.abs(_g), 1.0) + (_g == 0) * 1.0
        g_xattn = _g[0]
        g_ffn = _g[1]
        return (x, ctx_512, g_xattn, g_ffn)
    x, ctx_512, g_xattn, g_ffn = _rec_inputs()

    def _L0_xattn_setup():
        import jax, jax.numpy as jnp
        import numpy as np
        B, S, L = (2, 256, 256)
        DIM_Q, H, K, D_C, D_CQ, R = (512, 16, 128, 128, 384, 64)

        def _rope_tables(length, dim):
            inv = 1.0 / 10000.0 ** (jnp.arange(0, dim, 2, dtype=jnp.float32) / dim)
            f = jnp.arange(length, dtype=jnp.float32)[:, None] * inv[None, :]
            sin = jnp.repeat(jnp.sin(f), 2, axis=-1)
            cos = jnp.repeat(jnp.cos(f), 2, axis=-1)
            return (sin, cos)

        def _rotate_half(x):
            half = x.shape[-1] // 2
            return jnp.concatenate([-x[..., half:], x[..., :half]], axis=-1)

        def _apply_rope(x, sin, cos):
            return x * cos + _rotate_half(x) * sin
        key = jax.random.key(seed)
        ks = jax.random.split(key, 8)
        return {'hidden_q': jax.random.normal(ks[0], (B, S, DIM_Q), jnp.float32), 'kv_c': jax.random.normal(ks[1], (B, L, D_C), jnp.float32), 'Wq': jax.random.normal(ks[2], (H * K, DIM_Q), jnp.float32) / np.sqrt(DIM_Q).astype(np.float32), 'w_kc_q': jax.random.normal(ks[3], (H, K, D_CQ), jnp.float32) / np.sqrt(K).astype(np.float32), 'w_kc_kv': jax.random.normal(ks[4], (H, K, D_C), jnp.float32) / np.sqrt(K).astype(np.float32), 'W_qr': jax.random.normal(ks[5], (H, D_CQ, R), jnp.float32) / np.float32(np.sqrt(D_CQ) * np.sqrt(R)), 'W_kr': jax.random.normal(ks[6], (H, D_C, R), jnp.float32) / np.sqrt(D_C).astype(np.float32), 'Wo': jax.random.normal(ks[7], (DIM_Q, H * K), jnp.float32) / np.sqrt(H * K).astype(np.float32)}
    _L0_xattn_all = _L0_xattn_setup()
    _L0_xattn_in = {k: v for k, v in _L0_xattn_all.items() if k in ('Wq', 'w_kc_q', 'w_kc_kv', 'W_qr', 'W_kr', 'Wo')}
    del _L0_xattn_all

    def _L0_ffn_setup():
        import jax, jax.numpy as jnp
        import numpy as np
        HIDDEN = 512
        INTER = 1376
        LUT_SIZE = 16

        def _ghost_linear(x, idx, lut):
            w = lut[idx]
            return jnp.einsum('bsh,oh->bso', x, w)
        key = jax.random.key(seed)
        k_x, k_lut, k_g, k_u, k_d = jax.random.split(key, 5)
        x = jax.random.normal(k_x, (2, 1024, HIDDEN), dtype=jnp.float32)
        lut = jax.random.normal(k_lut, (LUT_SIZE,), dtype=jnp.float32) * 0.02
        gate_idx = jax.random.randint(k_g, (INTER, HIDDEN), 0, LUT_SIZE, dtype=jnp.int32)
        up_idx = jax.random.randint(k_u, (INTER, HIDDEN), 0, LUT_SIZE, dtype=jnp.int32)
        down_idx = jax.random.randint(k_d, (HIDDEN, INTER), 0, LUT_SIZE, dtype=jnp.int32)
        return {'x': x, 'lut': lut, 'gate_idx': gate_idx, 'up_idx': up_idx, 'down_idx': down_idx}
    _L0_ffn_all = _L0_ffn_setup()
    _L0_ffn_in = {k: v for k, v in _L0_ffn_all.items() if k in ('lut', 'gate_idx', 'up_idx', 'down_idx')}
    del _L0_ffn_all

    def _L1_xattn_setup():
        import jax, jax.numpy as jnp
        import numpy as np
        B, N, D = (16, 512, 128)
        H = 4
        TOP_K_RATIO = 0.3
        key = jax.random.key(seed)
        k1, k2, k3, k4 = jax.random.split(key, 4)
        h = jax.random.normal(k1, (B, N, D), dtype=jnp.float32)
        adj_raw = jax.random.uniform(k2, (B, N, N), dtype=jnp.float32)
        lim = 1.0 / np.sqrt(D)
        Wq = jax.random.uniform(k3, (D, D), minval=-lim, maxval=lim, dtype=jnp.float32)
        Wk = jax.random.uniform(k4, (D, D), minval=-lim, maxval=lim, dtype=jnp.float32)
        gamma_raw = jnp.float32(-0.85)
        return {'h': h, 'adj_raw': adj_raw, 'Wq': Wq, 'Wk': Wk, 'gamma_raw': gamma_raw}
    _L1_xattn_all = _L1_xattn_setup()
    _L1_xattn_in = {k: v for k, v in _L1_xattn_all.items() if k in ('Wq', 'Wk', 'gamma_raw')}
    del _L1_xattn_all

    def _L1_ffn_setup():
        import jax, jax.numpy as jnp
        import numpy as np
        B, S, D = (2, 512, 512)
        F = 256
        E = 64
        K = 8
        C = 256
        NORM_TOPK = False

        def _moe(x, gate_w, w_gate, w_up, w_down):
            b, s, d = x.shape
            T = b * s
            x2 = x.reshape(T, d)
            logits = x2 @ gate_w.T
            probs = jax.nn.softmax(logits.astype(jnp.float32), axis=-1)
            top_w, top_i = jax.lax.top_k(probs, K)
            if NORM_TOPK:
                top_w = top_w / jnp.sum(top_w, axis=-1, keepdims=True)
            top_w = top_w.astype(x.dtype)
            flat_e = top_i.reshape(-1)
            flat_w = top_w.reshape(-1)
            tok = jnp.arange(T * K) // K
            onehot = jax.nn.one_hot(flat_e, E, dtype=jnp.int32)
            pos = jnp.sum(jnp.cumsum(onehot, axis=0) * onehot, axis=-1) - 1
            valid = pos < C
            loc = flat_e * C + jnp.minimum(pos, C - 1)
            flat_w = jnp.where(valid, flat_w, 0.0)
            safe_loc = jnp.where(valid, loc, E * C)
            xg = jnp.zeros((E * C + 1, d), dtype=x.dtype).at[safe_loc].set(x2[tok])[:E * C]
            xg = xg.reshape(E, C, d)
            h = jax.nn.silu(jnp.einsum('ecd,edf->ecf', xg, w_gate)) * jnp.einsum('ecd,edf->ecf', xg, w_up)
            y = jnp.einsum('ecf,efd->ecd', h, w_down).reshape(E * C, d)
            y_tok = y[loc] * flat_w[:, None]
            out = jnp.zeros((T, d), dtype=x.dtype).at[tok].add(y_tok)
            return out.reshape(b, s, d)
        key = jax.random.key(seed)
        ks = jax.random.split(key, 5)
        scale = 0.02
        return {'hidden_states': jax.random.normal(ks[0], (B, S, D), dtype=jnp.float32), 'gate_w': jax.random.normal(ks[1], (E, D), dtype=jnp.float32) * scale, 'w_gate': jax.random.normal(ks[2], (E, D, F), dtype=jnp.float32) * scale, 'w_up': jax.random.normal(ks[3], (E, D, F), dtype=jnp.float32) * scale, 'w_down': jax.random.normal(ks[4], (E, F, D), dtype=jnp.float32) * scale}
    _L1_ffn_all = _L1_ffn_setup()
    _L1_ffn_in = {k: v for k, v in _L1_ffn_all.items() if k in ('gate_w', 'w_gate', 'w_up', 'w_down')}
    del _L1_ffn_all
    return {'x': x, 'ctx_512': ctx_512, 'g_xattn': g_xattn, 'g_ffn': g_ffn, 'L0_xattn_Wq': _L0_xattn_in['Wq'], 'L0_xattn_w_kc_q': _L0_xattn_in['w_kc_q'], 'L0_xattn_w_kc_kv': _L0_xattn_in['w_kc_kv'], 'L0_xattn_W_qr': _L0_xattn_in['W_qr'], 'L0_xattn_W_kr': _L0_xattn_in['W_kr'], 'L0_xattn_Wo': _L0_xattn_in['Wo'], 'L0_ffn_lut': _L0_ffn_in['lut'], 'L0_ffn_gate_idx': _L0_ffn_in['gate_idx'], 'L0_ffn_up_idx': _L0_ffn_in['up_idx'], 'L0_ffn_down_idx': _L0_ffn_in['down_idx'], 'L1_xattn_Wq': _L1_xattn_in['Wq'], 'L1_xattn_Wk': _L1_xattn_in['Wk'], 'L1_xattn_gamma_raw': _L1_xattn_in['gamma_raw'], 'L1_ffn_gate_w': _L1_ffn_in['gate_w'], 'L1_ffn_w_gate': _L1_ffn_in['w_gate'], 'L1_ffn_w_up': _L1_ffn_in['w_up'], 'L1_ffn_w_down': _L1_ffn_in['w_down']}

def reference(x, ctx_512, g_xattn, g_ffn, L0_xattn_Wq, L0_xattn_w_kc_q, L0_xattn_w_kc_kv, L0_xattn_W_qr, L0_xattn_W_kr, L0_xattn_Wo, L0_ffn_lut, L0_ffn_gate_idx, L0_ffn_up_idx, L0_ffn_down_idx, L1_xattn_Wq, L1_xattn_Wk, L1_xattn_gamma_raw, L1_ffn_gate_w, L1_ffn_w_gate, L1_ffn_w_up, L1_ffn_w_down):
    import jax
    import jax.numpy as jnp

    def _L0_xattn_ref(hidden_q, kv_c, Wq, w_kc_q, w_kc_kv, W_qr, W_kr, Wo):
        import jax, jax.numpy as jnp
        import numpy as np
        B, S, L = (2, 256, 256)
        DIM_Q, H, K, D_C, D_CQ, R = (512, 16, 128, 128, 384, 64)

        def _rope_tables(length, dim):
            inv = 1.0 / 10000.0 ** (jnp.arange(0, dim, 2, dtype=jnp.float32) / dim)
            f = jnp.arange(length, dtype=jnp.float32)[:, None] * inv[None, :]
            sin = jnp.repeat(jnp.sin(f), 2, axis=-1)
            cos = jnp.repeat(jnp.cos(f), 2, axis=-1)
            return (sin, cos)

        def _rotate_half(x):
            half = x.shape[-1] // 2
            return jnp.concatenate([-x[..., half:], x[..., :half]], axis=-1)

        def _apply_rope(x, sin, cos):
            return x * cos + _rotate_half(x) * sin
        Bv, Sv, _ = hidden_q.shape
        _, Lv, _ = kv_c.shape
        q_hk = (hidden_q @ Wq.T).reshape(Bv, Sv, H, K)
        q_big = jnp.einsum('bshk,hkq->bshq', q_hk, w_kc_q)
        sin_q, cos_q = _rope_tables(Sv, D_CQ)
        q_big = _apply_rope(q_big, sin_q[None, :, None, :], cos_q[None, :, None, :])
        sin_k, cos_k = _rope_tables(Lv, D_C)
        kv_r = _apply_rope(kv_c, sin_k[None], cos_k[None])
        q_r = jnp.einsum('bshq,hqr->bhsr', q_big, W_qr)
        k_r = jnp.einsum('bld,hdr->bhlr', kv_r, W_kr)
        scores = jnp.einsum('bhsr,bhlr->bhsl', q_r, k_r)
        attn = jax.nn.softmax(scores, axis=-1)
        ctx_c = jnp.einsum('bhsl,bld->bhsd', attn, kv_r)
        ctx_lat = jnp.einsum('bhsd,hkd->bhsk', ctx_c, w_kc_kv)
        ctx = ctx_lat.transpose(0, 2, 1, 3).reshape(Bv, Sv, H * K)
        return ctx @ Wo.T

    def _L0_ffn_ref(x, lut, gate_idx, up_idx, down_idx):
        import jax, jax.numpy as jnp
        import numpy as np
        HIDDEN = 512
        INTER = 1376
        LUT_SIZE = 16

        def _ghost_linear(x, idx, lut):
            w = lut[idx]
            return jnp.einsum('bsh,oh->bso', x, w)
        gate = _ghost_linear(x, gate_idx, lut)
        up = _ghost_linear(x, up_idx, lut)
        h = jax.nn.silu(gate) * up
        return _ghost_linear(h, down_idx, lut)

    def _L1_xattn_ref(h, adj_raw, Wq, Wk, gamma_raw):
        import jax, jax.numpy as jnp
        import numpy as np
        B, N, D = (16, 512, 128)
        H = 4
        TOP_K_RATIO = 0.3
        b, n, dm = h.shape
        d = dm // H
        Q = (h @ Wq.T).reshape(b, n, H, d).transpose(0, 2, 1, 3)
        K = (h @ Wk.T).reshape(b, n, H, d).transpose(0, 2, 1, 3)
        sim = jnp.einsum('bhnd,bhmd->bnm', Q, K) / (jnp.sqrt(jnp.float32(d)) * H)
        k = max(1, int(n * TOP_K_RATIO))
        topk_vals = jax.lax.top_k(sim, k)[0]
        threshold = topk_vals[:, :, -1:]
        sparse_mask = (sim >= threshold).astype(sim.dtype)
        A_learned = jax.nn.sigmoid(sim) * sparse_mask
        A_learned = (A_learned + jnp.swapaxes(A_learned, -1, -2)) * 0.5
        gamma = jax.nn.sigmoid(gamma_raw)
        return (1.0 - gamma) * adj_raw + gamma * A_learned

    def _L1_ffn_ref(hidden_states, gate_w, w_gate, w_up, w_down):
        import jax, jax.numpy as jnp
        import numpy as np
        B, S, D = (2, 512, 512)
        F = 256
        E = 64
        K = 8
        C = 256
        NORM_TOPK = False

        def _moe(x, gate_w, w_gate, w_up, w_down):
            b, s, d = x.shape
            T = b * s
            x2 = x.reshape(T, d)
            logits = x2 @ gate_w.T
            probs = jax.nn.softmax(logits.astype(jnp.float32), axis=-1)
            top_w, top_i = jax.lax.top_k(probs, K)
            if NORM_TOPK:
                top_w = top_w / jnp.sum(top_w, axis=-1, keepdims=True)
            top_w = top_w.astype(x.dtype)
            flat_e = top_i.reshape(-1)
            flat_w = top_w.reshape(-1)
            tok = jnp.arange(T * K) // K
            onehot = jax.nn.one_hot(flat_e, E, dtype=jnp.int32)
            pos = jnp.sum(jnp.cumsum(onehot, axis=0) * onehot, axis=-1) - 1
            valid = pos < C
            loc = flat_e * C + jnp.minimum(pos, C - 1)
            flat_w = jnp.where(valid, flat_w, 0.0)
            safe_loc = jnp.where(valid, loc, E * C)
            xg = jnp.zeros((E * C + 1, d), dtype=x.dtype).at[safe_loc].set(x2[tok])[:E * C]
            xg = xg.reshape(E, C, d)
            h = jax.nn.silu(jnp.einsum('ecd,edf->ecf', xg, w_gate)) * jnp.einsum('ecd,edf->ecf', xg, w_up)
            y = jnp.einsum('ecf,efd->ecd', h, w_down).reshape(E * C, d)
            y_tok = y[loc] * flat_w[:, None]
            out = jnp.zeros((T, d), dtype=x.dtype).at[tok].add(y_tok)
            return out.reshape(b, s, d)
        return _moe(hidden_states, gate_w, w_gate, w_up, w_down)
    x = x + jnp.tanh(g_xattn[0]) * _L0_xattn_ref(_layernorm(x, axis=-1), ctx_512, L0_xattn_Wq, L0_xattn_w_kc_q, L0_xattn_w_kc_kv, L0_xattn_W_qr, L0_xattn_W_kr, L0_xattn_Wo)
    x = x + jnp.tanh(g_ffn[0]) * _L0_ffn_ref(_layernorm(x, axis=-1), L0_ffn_lut, L0_ffn_gate_idx, L0_ffn_up_idx, L0_ffn_down_idx)
    x = x + jnp.tanh(g_xattn[1]) * _L1_xattn_ref(ctx_512, _layernorm(x, axis=-1), L1_xattn_Wq, L1_xattn_Wk, L1_xattn_gamma_raw)
    x = x + jnp.tanh(g_ffn[1]) * _L1_ffn_ref(_layernorm(x, axis=-1), L1_ffn_gate_w, L1_ffn_w_gate, L1_ffn_w_up, L1_ffn_w_down)
    return x

_drawn_inputs = setup_inputs


def setup_inputs(seed=0):
    import zlib

    import numpy as np

    out = dict(_drawn_inputs(seed))
    spreads = {'g_ffn': (-1.0, 0.6)}
    factors = {'L1_ffn_gate_w': 5.178,
     'L1_ffn_w_gate': 4.015,
     'L1_ffn_w_up': 3.955,
     'L1_ffn_w_down': 3.897}
    for name, (base, spread) in spreads.items():
        noise = np.random.default_rng([zlib.crc32(name.encode()), seed]).standard_normal(out[name].shape)
        drawn = base * np.exp(spread * noise) if base else spread * noise
        out[name] = jnp.asarray(drawn.astype(out[name].dtype))
    for name, factor in factors.items():
        out[name] = (out[name] * factor).astype(out[name].dtype)
    return out
```

```python
from contextlib import ExitStack

import numpy as np
import concourse.bass as bass
from concourse import mybir

ALU = mybir.AluOpType
ACT = mybir.ActivationFunctionType
F32 = mybir.dt.float32
BF16 = mybir.dt.bfloat16
I32 = mybir.dt.int32
U32 = mybir.dt.uint32
AX = mybir.AxisListType.X

P = 128
BATCH, SEQ, DIM = 4, 512, 512
T = BATCH * SEQ
TILES = T // P
KT = DIM // P
SEQ_T = SEQ // P
HEADS, HK, D_C, D_CQ, ROT = 16, 128, 128, 384, 64
QT = D_CQ // P
UNITS = HEADS * BATCH
INTER = 1376
FT = (INTER + P - 1) // P
F_LAST = INTER - (FT - 1) * P
LUT = 16
PICKS = 4
GU_W = KT * INTER
LUT_W = 2 * GU_W + FT * DIM
LUT_CHUNK = LUT_W // HEADS
TOP = int(SEQ * 0.3)
ROUNDS = (TOP - 1) // 8
AFF_SCALE = 1.0 / (float(np.sqrt(np.float32(32))) * 4)
EXPERTS, CHOSEN, CAP, FE = 64, 8, 256, 256
FET = FE // P
HALVES = CAP // P
EPS = 1e-5
LOWEST = -3.0e38
assert LUT_CHUNK * HEADS == LUT_W and 8 * ROUNDS < TOP <= 8 * ROUNDS + 8


def need(eng, sem, n):
    if isinstance(n, int) and n <= 0:
        return
    eng.wait_ge(sem, n)


def stand(eng):
    eng.nop(nofuse=True)


class Chain:

    def __init__(self, eng, sem, base=0):
        self.eng, self.sem, self.base, self.n = eng, sem, base, 0

    def add(self, ins):
        ins.then_inc(self.sem, 1)
        self.n += 1
        return self.n

    def now(self):
        self.eng.wait_ge(self.sem, self.base + self.n)

    def link(self, ins):
        self.add(ins)
        self.now()


def scoped(nc, stack):
    def sb(name, shape, dt=F32):
        return stack.enter_context(nc.sbuf_tensor(name, shape, dt))

    def banks(name, n):
        return [stack.enter_context(nc.psum_tensor(f"{name}{i}", [P, 512], F32)) for i in range(n)]

    def sem(name):
        return stack.enter_context(nc.semaphore(name))

    return sb, banks, sem


def norm_stats(dve, ch, tiles, stats, mv, ve):
    n = len(tiles)
    for j, x in enumerate(tiles):
        ch.add(dve.bn_stats(stats[:, j, :], x))
    ch.now()
    stand(dve)
    for j in range(n):
        ch.add(dve.bn_aggr(mv[:, j, :], stats[:, j, :]))
    ch.now()
    return dve.tensor_scalar(ve[:, 0:n], mv[:, 0:n, 1], EPS, None, ALU.add)


def phase_prepare(nc, a, x_sb, g):
    with ExitStack() as stack:
        sb, banks, sem = scoped(nc, stack)
        ctxT = sb("ctxT", [P, T])
        qaT = sb("qaT", [P, T])
        kaT = sb("kaT", [P, T])
        wqa = sb("wqa", [P, P])
        wka = sb("wka", [P, P])
        wqrT = sb("wqrT", [ROT, 2, D_CQ])
        wkrT = sb("wkrT", [ROT, 2, D_C])
        wkc = sb("wkc", [P, 2, D_C])
        woT = sb("woT", [P, 2, DIM])
        w1o = sb("w1o", [P, 2, D_CQ])
        w2o = sb("w2o", [P, 2, DIM])
        affo = sb("affo", [P, 2, SEQ])
        ps = banks("prep", 8)

        s_gate = sem("s_gate")
        s_tanh = sem("s_tanh")
        s_gsm = sem("s_gsm")
        s_ctx = sem("s_ctx")
        s_qk = sem("s_qk")
        s_qkc = sem("s_qkc")
        s_aff = sem("s_aff")
        s_affc = sem("s_affc")
        s_affo = [sem(f"s_affo{j}") for j in range(2)]
        s_win = [sem(f"s_win{j}") for j in range(2)]
        s_fold = sem("s_fold")
        s_foldc = sem("s_foldc")
        s_fout = [sem(f"s_fout{j}") for j in range(2)]
        block = stack.enter_context(nc.Block())

        @block.sync
        def _(sp):
            for src, dst in ((a["g_xattn"], g["raw"][:, 0:2]), (a["g_ffn"], g["raw"][:, 2:4]),
                             (a["gamma"], g["raw"][:, 4:5])):
                sp.dma_start(dst, src.partition_broadcast(P)).then_inc(s_gate, 16)
            sp.dma_start(g["lut"][:, :], a["lut"].partition_broadcast(P)).then_inc(s_gate, 16)
            sp.dma_start(ctxT[:, :], a["ctxT"]).then_inc(s_ctx, 16)
            sp.dma_start(wqa[:, :], a["wqa"]).then_inc(s_ctx, 16)
            sp.dma_start(wka[:, :], a["wka"]).then_inc(s_ctx, 16)
            for t in range(TILES):
                sp.wait_ge(s_affc, t + 1)
                sp.dma_start(a["aff"][t], affo[:, t % 2, :]).then_inc(s_affo[t % 2], 16)
            for j in range(2):
                sp.wait_ge(s_affo[j], 16 * TILES // 2)
            sp.wait_ge(s_gate, 64)

        @block.gpsimd
        def _(pool):
            with pool.Fori(0, HEADS // 2) as i:
                for j in range(2):
                    h = i * 2 + j
                    pool.wait_ge(s_fold, i * 4 + 0 + 2 * j)
                    for src, dst in ((a["wqrT"], wqrT), (a["wkrT"], wkrT), (a["wkc"], wkc), (a["woT"], woT)):
                        pool.dma_start(dst[:, j, :], src[bass.ds(h, 1), :, :].rearrange("o p n -> p (o n)"))\
                            .then_inc(s_win[j], 16)

        @block.tensor
        def _(pe):
            with pe.Fori(0, HEADS // 2) as i:
                for j in range(2):
                    pe.wait_ge(s_win[j], i * 64 + 64)
                    pe.wait_ge(s_foldc, i * 4 + 2 * j)
                    for t in range(QT):
                        mm = pe.matmul(ps[2 * j][:, t * P:(t + 1) * P], wqrT[:, j, t * P:(t + 1) * P],
                                       wkrT[:, j, :], start=True, stop=True)
                    mm.then_inc(s_fold, 1)
                    pe.matmul(ps[2 * j + 1][:, :], wkc[:, j, :], woT[:, j, :], start=True, stop=True)\
                        .then_inc(s_fold, 1)
            pe.wait_ge(s_ctx, 48)
            for n in range(BATCH):
                for m, w in enumerate((wqa, wka)):
                    k = 2 * n + m
                    if k >= 4:
                        pe.wait_ge(s_qkc, k - 3)
                    pe.matmul(ps[4 + k % 4][:, :], w[:, :], ctxT[:, n * SEQ:(n + 1) * SEQ], start=True, stop=True)\
                        .then_inc(s_qk, 1)
            for t in range(TILES):
                b = t // SEQ_T
                pe.wait_ge(s_qkc, 2 * b + 2)
                if t >= 4:
                    pe.wait_ge(s_affc, t - 3)
                else:
                    pe.wait_ge(s_qkc, 2 * BATCH)
                pe.matmul(ps[4 + t % 4][:, :], qaT[:, t * P:(t + 1) * P], kaT[:, b * SEQ:(b + 1) * SEQ],
                          start=True, stop=True).then_inc(s_aff, 1)

        @block.scalar
        def _(act):
            with act.Fori(0, HEADS // 2) as i:
                for j in range(2):
                    h = i * 2 + j
                    act.wait_ge(s_fout[j], i * 32)
                    act.wait_ge(s_fold, i * 4 + 2 * j + 1)
                    act.activation(w1o[:, j, :], ps[2 * j][:, 0:D_CQ], ACT.Copy).then_inc(s_foldc, 1)
                    act.wait_ge(s_fold, i * 4 + 2 * j + 2)
                    act.activation(w2o[:, j, :], ps[2 * j + 1][:, :], ACT.Copy).then_inc(s_foldc, 1)
                    act.wait_ge(s_foldc, i * 4 + 2 * j + 2)
                    act.dma_start(a["w1"][bass.ds(h, 1), :, :].rearrange("o p n -> p (o n)"), w1o[:, j, :])\
                        .then_inc(s_fout[j], 16)
                    act.dma_start(a["w2"][bass.ds(h, 1), :, :].rearrange("o p n -> p (o n)"), w2o[:, j, :])\
                        .then_inc(s_fout[j], 16)
            for j in range(2):
                act.wait_ge(s_fout[j], 32 * HEADS // 2)
            act.wait_ge(s_gate, 64)
            act.activation(g["th"][:, 0:4], g["raw"][:, 0:4], ACT.Tanh).then_inc(s_tanh, 1)
            act.activation(g["th"][:, 4:5], g["raw"][:, 4:5], ACT.Tanh, scale=0.5).then_inc(s_tanh, 1)

        @block.vector
        def _(dve):
            for k in range(2 * BATCH):
                dve.wait_ge(s_qk, k + 1)
                n, dst = k // 2, (qaT, kaT)[k % 2]
                dve.tensor_copy(dst[:, n * SEQ:(n + 1) * SEQ], ps[4 + k % 4][:, :]).then_inc(s_qkc, 1)
            for t in range(TILES):
                dve.wait_ge(s_aff, t + 1)
                if t >= 2:
                    dve.wait_ge(s_affo[t % 2], 16 * (t // 2))
                dve.tensor_copy(affo[:, t % 2, :], ps[4 + t % 4][:, :]).then_inc(s_affc, 1)
            ch = Chain(dve, s_gsm)
            dve.wait_ge(s_tanh, 2)
            ch.link(dve.tensor_scalar(g["tmp"][:, 0:1], g["th"][:, 4:5], 0.5, 0.5, ALU.mult, ALU.add))
            ch.link(dve.tensor_scalar(g["tmp"][:, 1:2], g["tmp"][:, 0:1], -1.0, 1.0, ALU.mult, ALU.add))
            ch.add(dve.tensor_tensor(g["mix"][:, 0:1], g["tmp"][:, 1:2], g["th"][:, 1:2], ALU.mult))
            ch.link(dve.tensor_tensor(g["tmp"][:, 2:3], g["tmp"][:, 0:1], g["th"][:, 1:2], ALU.mult))
            ch.add(dve.tensor_scalar(g["mix"][:, 1:2], g["tmp"][:, 2:3], 0.25, None, ALU.mult))


def phase_norm_transpose(nc, name, x_sb, xT, ident, load=None):
    with ExitStack() as stack:
        sb, banks, sem = scoped(nc, stack)
        stats = sb(name + "stats", [P, TILES, 6])
        mv = sb(name + "mv", [P, TILES, 2])
        ve = sb(name + "ve", [P, TILES])
        half = sb(name + "half", [P, SEQ_T])
        rstd = sb(name + "rstd", [P, TILES])
        xn = sb(name + "xn", [P, 4, DIM])
        ps = banks(name + "ps", 4)
        s_x = [sem(f"{name}x{b}") for b in range(BATCH)]
        s_half = sem(name + "half")
        s_var = sem(name + "var")
        s_rstd = sem(name + "rstd")
        s_ch = sem(name + "ch")
        s_xn = sem(name + "xn")
        s_tr = sem(name + "tr")
        s_out = sem(name + "out")
        block = stack.enter_context(nc.Block())

        if load is not None:
            @block.sync
            def _(sp):
                for b in range(BATCH):
                    sp.dma_start(x_sb[:, b * SEQ_T:(b + 1) * SEQ_T, :],
                                 load[b * SEQ:(b + 1) * SEQ, :].rearrange("(i p) d -> p i d", p=P))\
                        .then_inc(s_x[b], 16)

        @block.vector
        def _(dve):
            ch = Chain(dve, s_ch)
            for b in range(BATCH):
                if load is not None:
                    dve.wait_ge(s_x[b], 16)
                lo = b * SEQ_T
                norm_stats(dve, ch, [x_sb[:, lo + j, :] for j in range(SEQ_T)], stats[:, lo:lo + SEQ_T, :],
                           mv[:, lo:lo + SEQ_T, :], ve[:, lo:lo + SEQ_T]).then_inc(s_var, 1)
                dve.wait_ge(s_rstd, b + 1)
                for t in range(lo, lo + SEQ_T):
                    if t >= 4:
                        dve.wait_ge(s_tr, t - 3)
                    dve.tensor_scalar(xn[:, t % 4, :], x_sb[:, t, :], mv[:, t, 0:1], rstd[:, t:t + 1],
                                      ALU.subtract, ALU.mult).then_inc(s_xn, 1)

        @block.gpsimd
        def _(pool):
            pool.memset(half[:, :], -0.5).then_inc(s_half, 1)
            pool.wait_ge(s_half, 1)
            for b in range(BATCH):
                pool.wait_ge(s_var, b + 1)
                lo = b * SEQ_T
                pool.tensor_tensor(rstd[:, lo:lo + SEQ_T], ve[:, lo:lo + SEQ_T], half[:, :], ALU.pow)\
                    .then_inc(s_rstd, 1)

        @block.tensor
        def _(pe):
            for t in range(TILES):
                pe.wait_ge(s_xn, t + 1)
                if t >= 4:
                    pe.wait_ge(s_out, t - 3)
                for k in range(KT):
                    tr = pe.transpose(ps[t % 4][:, k * P:(k + 1) * P], xn[:, t % 4, k * P:(k + 1) * P], ident[:, :])
                tr.then_inc(s_tr, 1)

        @block.scalar
        def _(act):
            for t in range(TILES):
                act.wait_ge(s_tr, t + 1)
                act.activation(xT[:, :, t * P:(t + 1) * P], ps[t % 4][:, :].rearrange("p (k c) -> p k c", k=KT),
                               ACT.Copy).then_inc(s_out, 1)


def phase_attention(nc, a, x_sb, xT, ident, g):
    with ExitStack() as stack:
        sb, banks, sem = scoped(nc, stack)
        rot = sb("rot", [P, 2 * QT, SEQ])
        kvT = sb("kvT", [P, T])
        kv = sb("kv", [P, TILES, D_C])
        wq = sb("wq", [P, KT, HK])
        wc = sb("wc", [P, 4 * P])
        w1 = sb("w1", [P, D_CQ])
        w2 = sb("w2", [P, DIM])
        qT = sb("qT", [P, SEQ])
        prod = sb("prod", [P, 6, SEQ])
        qrot = sb("qrot", [P, QT, SEQ])
        qp = sb("qp", [P, SEQ])
        attn = sb("attn", [P, 2, SEQ_T, SEQ])
        attnT = sb("attnT", [P, SEQ_T, SEQ])
        ctx = sb("ctx", [P, SEQ])
        nmax = sb("nmax", [P, 2, SEQ_T])
        esum = sb("esum", [P, 2, SEQ_T])
        rsum = sb("rsum", [P, 2, SEQ_T])
        aff = sb("affin", [P, SEQ])
        left = sb("left", [P, SEQ])
        tanh = sb("tanh", [P, SEQ])
        kept = sb("kept", [P, SEQ])
        top8 = sb("top8", [P, 8])
        idx = sb("idx", [P, LUT_CHUNK], I32)
        pick = sb("pick", [P, PICKS, LUT_CHUNK])
        wsum = sb("wsum", [P, LUT_CHUNK])

        ps_q, = banks("ps_q", 1)
        ps_r = banks("ps_r", 2)
        ps_s = banks("ps_s", 2)
        ps_t = banks("ps_t", 3)

        names = """rot_in kv_in kv_mul kv_add
            wq_in wc_in w1_in w2_in aff_in idx_in
            q_full ab_full cc_full qp_full s_full t_full ctx_full o_full
            q_evac qp_evac exp_done t_evac ctx_evac tanh_done
            max_done ab_mul cc_mul c_add o_add recip topk kept_made picked
            ab_add normed pick_added wsum_zero aff_out w_out""".split()
        s = {n: sem("a_" + n) for n in names}
        block = stack.enter_context(nc.Block())
        TOPK_OPS = 2 * ROUNDS + 2

        flat = attn[:, :, :, :].rearrange("p a b c -> p (a b c)")
        straight, swapped = flat[:, 0:T], flat[:, T:2 * T]
        tok = attnT[:, :, :].rearrange("p a (b c) -> p (a b) c", c=D_C)
        tmp = prod[:, 0:4, :].rearrange("p a (b c) -> p (a b) c", c=D_C)
        ktab = qrot[:, 0:2, :]
        ttab = aff[:, :].rearrange("p (i d) -> p i d", i=SEQ_T)
        stab = left[:, :].rearrange("p (i d) -> p i d", i=SEQ_T)

        def loop(eng, body):
            body(0)
            with eng.Fori(1, HEADS - 1) as i:
                body(i)
            body(HEADS - 1)

        @block.sync
        def _(sp):
            sp.dma_start(rot[:, :, :], a["rot"]).then_inc(s["rot_in"], 16)

            def load(dst, src, h, what):
                sp.dma_start(dst, src[bass.ds(h, 1), :, :].rearrange("o p n -> p (o n)"))\
                    .then_inc(s[what], 16)

            wq_f = wq[:, :, :].rearrange("p k n -> p (k n)")

            def weights(h):
                need(sp, s["q_full"], h * 4)
                load(wq_f, a["wq"], h, "wq_in")
                need(sp, s["cc_full"], h * 4)
                load(wc[:, :], a["wc"], h, "wc_in")
                need(sp, s["qp_full"], h * 4)
                load(w1[:, :], a["w1"], h, "w1_in")
                need(sp, s["kept_made"], h)
                need(sp, s["tanh_done"], h)
                load(aff[:, :], a["aff"], h, "aff_in")
                need(sp, s["picked"], h * LUT)
                load(idx[:, :], a["idx"], h, "idx_in")
                need(sp, s["o_full"], h * 16)
                load(w2[:, :], a["w2"], h, "w2_in")

            for lo, hi in ((0, P // 2), (P // 2, P)):
                sp.dma_start(swapped[lo:hi, :], a["ctxT"][P // 2 - lo:P - lo, :]).then_inc(s["kv_in"], 16)
            for dst, src in ((straight, a["ctxT"]), (ktab, a["ktab"]), (ttab, a["ttab"]), (stab, a["stab"]),
                             (tok, a["ctx"].rearrange("(i p) d -> p i d", p=P))):
                sp.dma_start(dst, src).then_inc(s["kv_in"], 16)

            def body(h):
                if isinstance(h, int) and h == 0:
                    sp.wait_ge(s["kv_add"], 2)
                weights(h)

            loop(sp, body)

        @block.gpsimd
        def _(pool):
            def ab_add(u):
                pool.wait_ge(s["ab_mul"], u + 1)
                need(pool, s["qp_full"], u)
                pool.tensor_tensor(qrot[:, 0, :], prod[:, 0, :], prod[:, 1, :], ALU.add)
                pool.tensor_tensor(qrot[:, 1, :], prod[:, 2, :], prod[:, 3, :], ALU.add)\
                    .then_inc(s["ab_add"], 1)

            def norm(u, b):
                pool.wait_ge(s["recip"], u + 1)
                stand(pool)
                for j in range(SEQ_T):
                    pool.tensor_scalar(attn[:, b % 2, j, :], attn[:, b % 2, j, :], rsum[:, b % 2, j:j + 1], 1.0,
                                       ALU.mult, ALU.mult).then_inc(s["normed"], 1)

            def pick_add(h, k):
                pool.wait_ge(s["picked"], h * LUT + k + 1)
                if k == 0:
                    need(pool, s["w_out"], h * 16)
                    stand(pool)
                    pool.tensor_copy(wsum[:, :], pick[:, 0, :]).then_inc(s["pick_added"], 1)
                else:
                    pool.wait_ge(s["pick_added"], h * LUT + k)
                    pool.tensor_tensor(wsum[:, :], wsum[:, :], pick[:, k % PICKS, :], ALU.add)\
                        .then_inc(s["pick_added"], 1)

            ab_add(0)

            def body(h):
                for b in range(BATCH):
                    u = h * 4 + b
                    if not (isinstance(h, int) and u == UNITS - 1):
                        ab_add(u + 1)
                    norm(u, b)
                    for k in range(4 * b, 4 * b + 4):
                        pick_add(h, k)

            loop(pool, body)

        @block.scalar
        def _(act):
            def evac_q(u):
                act.wait_ge(s["q_full"], u + 1)
                need(act, s["cc_full"], u)
                act.activation(qT[:, :], ps_q[:, :], ACT.Copy).then_inc(s["q_evac"], 1)

            def evac_qp(u):
                act.wait_ge(s["qp_full"], u + 1)
                act.activation(qp[:, :], ps_q[:, :], ACT.Copy).then_inc(s["qp_evac"], 1)

            def exps(u, b, js):
                for j in js:
                    act.wait_ge(s["max_done"], u * 4 + j + 1)
                    if j == 0:
                        need(act, s["t_full"], u * 4 - 4)
                    act.activation(attn[:, b % 2, j, :], ps_s[j % 2][:, :], ACT.Exp, bias=nmax[:, b % 2, j:j + 1],
                                   accum_out=esum[:, b % 2, j:j + 1]).then_inc(s["exp_done"], 1)

            def evac_back(u):
                for j in range(SEQ_T):
                    act.wait_ge(s["t_full"], u * 4 + j + 1)
                    if j == 0:
                        need(act, s["ctx_full"], u)
                    act.activation(attnT[:, :, j * P:(j + 1) * P],
                                   ps_t[j % 3][:, :].rearrange("p (l c) -> p l c", l=SEQ_T), ACT.Copy)\
                        .then_inc(s["t_evac"], 1)

            def evac_ctx(u):
                act.wait_ge(s["ctx_full"], u + 1)
                need(act, s["o_full"], u * 4)
                act.activation(ctx[:, :], ps_t[1][:, :], ACT.Copy).then_inc(s["ctx_evac"], 1)

            def store(h):
                act.wait_ge(s["kept_made"], h + 1)
                act.dma_start(a["kept"][bass.ds(h, 1), :, :].rearrange("o p n -> p (o n)"), kept[:, :])\
                    .then_inc(s["aff_out"], 16)
                act.wait_ge(s["pick_added"], h * LUT + LUT)
                act.dma_start(a["lutw"][bass.ds(h, 1), :, :].rearrange("o p n -> p (o n)"), wsum[:, :])\
                    .then_inc(s["w_out"], 16)

            evac_q(0)
            evac_qp(0)

            def body(h):
                for b in range(BATCH):
                    u = h * 4 + b
                    first = isinstance(h, int) and u == 0
                    last = isinstance(h, int) and u == UNITS - 1
                    if not first:
                        evac_back(u - 1)
                    exps(u, b, (0, 1))
                    if not first:
                        evac_ctx(u - 1)
                    if not last:
                        evac_q(u + 1)
                    exps(u, b, (2, 3))
                    if b == 1:
                        act.wait_ge(s["aff_in"], h * 16 + 16)
                        need(act, s["kept_made"], h)
                        act.activation(tanh[:, :], aff[:, :], ACT.Tanh, scale=0.5 * AFF_SCALE)\
                            .then_inc(s["tanh_done"], 1)
                    if not last:
                        evac_qp(u + 1)
                    if b == 0 and not first:
                        store(h - 1)

            loop(act, body)
            evac_back(UNITS - 1)
            evac_ctx(UNITS - 1)
            store(HEADS - 1)
            act.wait_ge(s["aff_out"], 16 * HEADS)
            act.wait_ge(s["w_out"], 16 * HEADS)

        @block.tensor
        def _(pe):
            def q_heads(u, b, h):
                if b == 0:
                    pe.wait_ge(s["wq_in"], h * 16 + 16)
                need(pe, s["qp_evac"], u)
                for k in range(KT):
                    mm = pe.matmul(ps_q[:, :], wq[:, k, :], xT[:, k, b * SEQ:(b + 1) * SEQ],
                                   start=(k == 0), stop=(k == KT - 1))
                mm.then_inc(s["q_full"], 1)

            def latent(u, b, h, which):
                if which == 0:
                    if b == 0:
                        pe.wait_ge(s["wc_in"], h * 16 + 16)
                    pe.wait_ge(s["q_evac"], u + 1)
                    need(pe, s["cc_mul"], u)
                else:
                    pe.wait_ge(s["ab_mul"], u + 1)
                for r in range(2):
                    c = (2 * which + r) * P
                    mm = pe.matmul(ps_r[r][:, :], wc[:, c:c + P], qT[:, :], start=True, stop=True)
                mm.then_inc(s["ab_full" if which == 0 else "cc_full"], 1)

            def query(u, b, h):
                if b == 0:
                    pe.wait_ge(s["w1_in"], h * 16 + 16)
                pe.wait_ge(s["ab_add"], u + 1)
                pe.wait_ge(s["c_add"], u + 1)
                for t in range(QT):
                    mm = pe.matmul(ps_q[:, :], w1[:, t * P:(t + 1) * P], qrot[:, t, :],
                                   start=(t == 0), stop=(t == QT - 1))
                mm.then_inc(s["qp_full"], 1)

            def scores(u, b, j):
                if j == 0:
                    pe.wait_ge(s["qp_evac"], u + 1)
                need(pe, s["exp_done"], u * 4 + j - 1)
                pe.matmul(ps_s[j % 2][:, :], qp[:, j * P:(j + 1) * P], kvT[:, b * SEQ:(b + 1) * SEQ],
                          start=True, stop=True).then_inc(s["s_full"], 1)

            def turn(u, b, j):
                pe.wait_ge(s["normed"], u * 4 + j + 1)
                if j < 3:
                    need(pe, s["o_add"], u * 4 - 2 + j)
                else:
                    pe.wait_ge(s["t_evac"], u * 4 + 1)
                for l in range(SEQ_T):
                    tr = pe.transpose(ps_t[j % 3][:, l * P:(l + 1) * P], attn[:, b % 2, j, l * P:(l + 1) * P],
                                      ident[:, :])
                tr.then_inc(s["t_full"], 1)

            def context(u, b):
                pe.wait_ge(s["t_evac"], u * 4 + 4)
                for l in range(SEQ_T):
                    mm = pe.matmul(ps_t[1][:, :], kv[:, b * SEQ_T + l, :], attnT[:, l, :],
                                   start=(l == 0), stop=(l == SEQ_T - 1))
                mm.then_inc(s["ctx_full"], 1)

            def output(u, b, h, j):
                if j == 0:
                    if b == 0:
                        pe.wait_ge(s["w2_in"], h * 16 + 16)
                    pe.wait_ge(s["ctx_evac"], u + 1)
                if j == 3:
                    pe.wait_ge(s["o_add"], u * 4 + 1)
                pe.matmul(ps_t[(2 + j) % 3][:, :], ctx[:, j * P:(j + 1) * P], w2[:, :], start=True, stop=True)\
                    .then_inc(s["o_full"], 1)

            def front(u, b, h, part):
                (lambda: q_heads(u, b, h), lambda: latent(u, b, h, 0), lambda: latent(u, b, h, 1),
                 lambda: query(u, b, h))[part]()

            for part in range(4):
                front(0, 0, 0, part)
            pe.wait_ge(s["kv_add"], 2)

            def body(h):
                for b in range(BATCH):
                    u = h * 4 + b
                    first = isinstance(h, int) and u == 0
                    last = isinstance(h, int) and u == UNITS - 1
                    pb, ph = (b - 1) % 4, h if b else h - 1
                    nb, nh = (b + 1) % 4, h if b < 3 else h + 1
                    if not first:
                        for j in range(SEQ_T):
                            turn(u - 1, pb, j)
                    scores(u, b, 0)
                    scores(u, b, 1)
                    if not first:
                        context(u - 1, pb)
                    if not last:
                        front(u + 1, nb, nh, 0)
                    scores(u, b, 2)
                    if not last:
                        front(u + 1, nb, nh, 1)
                    scores(u, b, 3)
                    if not first:
                        output(u - 1, pb, ph, 0)
                        output(u - 1, pb, ph, 1)
                    if not last:
                        front(u + 1, nb, nh, 2)
                    if not first:
                        output(u - 1, pb, ph, 2)
                        output(u - 1, pb, ph, 3)
                    if not last:
                        front(u + 1, nb, nh, 3)

            loop(pe, body)
            for j in range(SEQ_T):
                turn(UNITS - 1, 3, j)
            context(UNITS - 1, 3)
            for j in range(SEQ_T):
                output(UNITS - 1, 3, HEADS - 1, j)

        @block.vector
        def _(dve):
            def rope_ab(u):
                dve.wait_ge(s["ab_full"], u + 1)
                need(dve, s["ab_add"], u)
                for t, (src, tab) in enumerate(((0, 0), (1, QT), (1, 1), (0, QT + 1))):
                    ins = dve.tensor_tensor(prod[:, t, :], ps_r[src][:, :], rot[:, tab, :], ALU.mult)
                ins.then_inc(s["ab_mul"], 1)

            def rope_cc(u):
                dve.wait_ge(s["cc_full"], u + 1)
                need(dve, s["c_add"], u)
                for t in range(2):
                    ins = dve.tensor_tensor(prod[:, 4 + t, :], ps_r[t][:, :], rot[:, 2 + QT * t, :], ALU.mult)
                ins.then_inc(s["cc_mul"], 1)
                dve.wait_ge(s["cc_mul"], u + 1)
                need(dve, s["qp_full"], u)
                dve.tensor_tensor(qrot[:, 2, :], prod[:, 4, :], prod[:, 5, :], ALU.add).then_inc(s["c_add"], 1)

            def maxes(u, b, js):
                for j in js:
                    dve.wait_ge(s["s_full"], u * 4 + j + 1)
                    dve.tensor_reduce(nmax[:, b % 2, j:j + 1], ps_s[j % 2][:, :], AX, ALU.max, negate=True)\
                        .then_inc(s["max_done"], 1)

            def add_out(u, b, js):
                for j in js:
                    dve.wait_ge(s["o_full"], u * 4 + j + 1)
                    need(dve, s["o_add"], u * 4 - 12 + j)
                    xt = x_sb[:, b * SEQ_T + j, :]
                    dve.scalar_tensor_tensor(xt, ps_t[(2 + j) % 3][:, :], g["th"][:, 0:1], xt, ALU.mult, ALU.add)\
                        .then_inc(s["o_add"], 1)

            def sums(u, b):
                dve.wait_ge(s["exp_done"], u * 4 + 4)
                dve.reciprocal(rsum[:, b % 2, :], esum[:, b % 2, :]).then_inc(s["recip"], 1)

            def topk(h, b):
                base = h * TOPK_OPS
                lo, hi = ROUNDS * b // 4, ROUNDS * (b + 1) // 4
                for r in range(lo, hi):
                    if r == 0:
                        dve.wait_ge(s["aff_in"], h * 16 + 16)
                        need(dve, s["kept_made"], h)
                    src = aff if r == 0 else left
                    need(dve, s["topk"], base + 2 * r)
                    stand(dve)
                    dve.max(top8[:, :], src[:, :]).then_inc(s["topk"], 1)
                    dve.wait_ge(s["topk"], base + 2 * r + 1)
                    stand(dve)
                    dve.match_replace(left[:, :], top8[:, :], src[:, :], LOWEST).then_inc(s["topk"], 1)
                if b == 3:
                    dve.wait_ge(s["topk"], base + 2 * ROUNDS)
                    stand(dve)
                    dve.max(top8[:, :], left[:, :]).then_inc(s["topk"], 1)
                    dve.wait_ge(s["topk"], base + 2 * ROUNDS + 1)
                    k = TOP - 8 * ROUNDS - 1
                    need(dve, s["aff_out"], h * 16)
                    dve.tensor_scalar(left[:, :], aff[:, :], top8[:, k:k + 1], None, ALU.is_ge)\
                        .then_inc(s["topk"], 1)
                    dve.wait_ge(s["topk"], base + 2 * ROUNDS + 2)
                    dve.wait_ge(s["tanh_done"], h + 1)
                    dve.scalar_tensor_tensor(kept[:, :], tanh[:, :], 1.0, left[:, :], ALU.add, ALU.mult)\
                        .then_inc(s["kept_made"], 1)

            def picks(h, b):
                for k in range(4 * b, 4 * b + 4):
                    if k == 0:
                        dve.wait_ge(s["idx_in"], h * 16 + 16)
                    need(dve, s["pick_added"], h * LUT + k + 1 - PICKS)
                    dve.tensor_scalar(pick[:, k % PICKS, :], idx[:, :], float(k), g["lut"][:, k:k + 1], ALU.is_equal,
                                      ALU.mult).then_inc(s["picked"], 1)

            dve.wait_ge(s["kv_in"], 16 * 7)
            for b in range(BATCH):
                c = slice(b * SEQ, (b + 1) * SEQ)
                dve.tensor_tensor(kvT[:, c], straight[:, c], ktab[:, 0, :], ALU.mult)
                ins = dve.tensor_tensor(swapped[:, c], swapped[:, c], ktab[:, 1, :], ALU.mult)
            ins.then_inc(s["kv_mul"], 1)
            dve.wait_ge(s["kv_mul"], 1)
            dve.tensor_tensor(kvT[:, :], kvT[:, :], swapped[:, :], ALU.add).then_inc(s["kv_add"], 1)
            H = D_C // 2
            for b in range(BATCH):
                r = slice(b * SEQ_T, (b + 1) * SEQ_T)
                dve.tensor_tensor(kv[:, r, :], tok[:, r, :], ttab, ALU.mult)
                dve.tensor_tensor(tmp[:, r, 0:H], tok[:, r, H:], stab[:, :, 0:H], ALU.mult)
                ins = dve.tensor_tensor(tmp[:, r, H:], tok[:, r, 0:H], stab[:, :, H:], ALU.mult)
            ins.then_inc(s["kv_mul"], 1)
            dve.wait_ge(s["kv_mul"], 2)
            dve.tensor_tensor(kv[:, :, :], kv[:, :, :], tmp, ALU.add).then_inc(s["kv_add"], 1)
            dve.wait_ge(s["kv_add"], 2)
            dve.wait_ge(s["rot_in"], 16)
            rope_ab(0)
            rope_cc(0)

            def body(h):
                for b in range(BATCH):
                    u = h * 4 + b
                    first = isinstance(h, int) and u == 0
                    last = isinstance(h, int) and u == UNITS - 1
                    maxes(u, b, (0, 1))
                    maxes(u, b, (2,))
                    if not last:
                        rope_ab(u + 1)
                    maxes(u, b, (3,))
                    if not first:
                        add_out(u - 1, (b - 1) % 4, (0, 1))
                    if not last:
                        rope_cc(u + 1)
                    sums(u, b)
                    if not first:
                        add_out(u - 1, (b - 1) % 4, (2, 3))
                    picks(h, b)
                    topk(h, b)

            loop(dve, body)
            add_out(UNITS - 1, 3, range(4))


def phase_swiglu(nc, a, x_sb, xT, g):
    with ExitStack() as stack:
        sb, banks, sem = scoped(nc, stack)
        lw = sb("lw", [P, LUT_W])
        w_gate = lw[:, 0:GU_W].rearrange("p (k f) -> p k f", k=KT)
        w_up = lw[:, GU_W:2 * GU_W].rearrange("p (k f) -> p k f", k=KT)
        w_down = lw[:, 2 * GU_W:LUT_W].rearrange("p (f n) -> p f n", f=FT)
        th = sb("th", [P, 2, SEQ])
        u = sb("u", [P, 2, SEQ])
        hT = sb("hT", [P, FT, SEQ])
        ps_g = banks("ps_g", 2)
        ps_u = banks("ps_u", 2)
        ps_o = banks("ps_o", 4)
        s = {n: sem("f_" + n) for n in "w_in g_full u_full tanh_done u_made h_made o_full o_add".split()}
        block = stack.enter_context(nc.Block())

        def width(f):
            return P if f < FT - 1 else F_LAST

        @block.sync
        def _(sp):
            sp.dma_start(lw[:, :].rearrange("p (h n) -> p h n", h=HEADS), a["lutw"].rearrange("h p n -> p h n"))\
                .then_inc(s["w_in"], 16)
            sp.wait_ge(s["w_in"], 16)

        @block.tensor
        def _(pe):
            pe.wait_ge(s["w_in"], 16)
            with pe.Fori(0, BATCH) as b:
                for f in range(FT):
                    n = b * FT + f
                    M = width(f)
                    for w, ps, full in ((w_gate, ps_g, "g_full"), (w_up, ps_u, "u_full")):
                        if f >= 2:
                            pe.wait_ge(s["h_made"], n - 1)
                        else:
                            pe.wait_ge(s["h_made"], b * FT)
                        for k in range(KT):
                            mm = pe.matmul(ps[f % 2][0:M, :], w[:, k, f * P:f * P + M],
                                           xT[:, k, bass.ds(b * SEQ, SEQ)], start=(k == 0), stop=(k == KT - 1))
                        mm.then_inc(s[full], 1)
                pe.wait_ge(s["h_made"], b * FT + FT)
                for j in range(SEQ_T):
                    pe.wait_ge(s["o_add"], b * SEQ_T)
                    for f in range(FT):
                        M = width(f)
                        mm = pe.matmul(ps_o[j][:, :], hT[0:M, f, j * P:(j + 1) * P], w_down[0:M, f, :],
                                       start=(f == 0), stop=(f == FT - 1))
                    mm.then_inc(s["o_full"], 1)

        @block.scalar
        def _(act):
            with act.Fori(0, BATCH) as b:
                for f in range(FT):
                    n = b * FT + f
                    M = width(f)
                    act.wait_ge(s["g_full"], n + 1)
                    if f >= 2:
                        act.wait_ge(s["u_made"], n - 1)
                    else:
                        act.wait_ge(s["u_made"], b * FT)
                    act.activation(th[0:M, f % 2, :], ps_g[f % 2][0:M, :], ACT.Tanh, scale=0.5)\
                        .then_inc(s["tanh_done"], 1)

        @block.vector
        def _(dve):
            with dve.Fori(0, BATCH) as b:
                dve.wait_ge(s["o_full"], b * SEQ_T)
                for f in range(FT):
                    n = b * FT + f
                    M = width(f)
                    dve.wait_ge(s["tanh_done"], n + 1)
                    dve.wait_ge(s["h_made"], n - 1 if f >= 2 else b * FT)
                    dve.scalar_tensor_tensor(u[0:M, f % 2, :], th[0:M, f % 2, :], 1.0, ps_g[f % 2][0:M, :],
                                             ALU.add, ALU.mult).then_inc(s["u_made"], 1)
                    dve.wait_ge(s["u_full"], n + 1)
                    dve.wait_ge(s["u_made"], n + 1)
                    dve.scalar_tensor_tensor(hT[0:M, f, :], u[0:M, f % 2, :], 0.5, ps_u[f % 2][0:M, :],
                                             ALU.mult, ALU.mult).then_inc(s["h_made"], 1)
                for j in range(SEQ_T):
                    dve.wait_ge(s["o_full"], b * SEQ_T + j + 1)
                    xt = x_sb[:, bass.ds(b * SEQ_T + j, 1), :].rearrange("p o d -> p (o d)")
                    dve.scalar_tensor_tensor(xt, ps_o[j][:, :], g["th"][:, 2:3], xt, ALU.mult, ALU.add)\
                        .then_inc(s["o_add"], 1)


def phase_mix_route(nc, a, x_sb, ident, g, r):
    with ExitStack() as stack:
        sb, banks, sem = scoped(nc, stack)
        kept = sb("kept_m", [P, 2, SEQ_T, SEQ])
        stats = sb("stats", [P, SEQ_T, 6])
        mv = sb("mv", [P, SEQ_T, 2])
        ve = sb("ve", [P, SEQ_T])
        half = sb("half", [P, SEQ_T])
        rstd = sb("rstd", [P, SEQ_T])
        scl = sb("scl", [P, SEQ_T])
        shift = sb("shift", [P, SEQ_T])
        xn = sb("xn", [P, SEQ_T, DIM])
        xnT = sb("xnT", [P, SEQ_T, DIM])
        gw = sb("gw", [P, KT, EXPERTS])
        logit = sb("logit", [P, SEQ_T, EXPERTS])
        rest = sb("rest", [P, SEQ_T, EXPERTS])
        top8 = sb("rtop8", [P, SEQ_T, 8])
        nmax = sb("rnmax", [P, SEQ_T])
        prob = sb("prob", [P, SEQ_T, EXPERTS])
        psum_e = sb("psum_e", [P, SEQ_T])
        rden = sb("rden", [P, SEQ_T])
        sel = sb("sel", [P, SEQ_T, EXPERTS])
        selb = sb("selb", [P, SEQ_T, EXPERTS], BF16)
        valid = sb("valid", [P, SEQ_T, EXPERTS])
        taken = sb("taken", [P, EXPERTS])
        takenb = sb("takenb", [P, EXPERTS], BF16)
        count = sb("count", [P, EXPERTS])
        posp = sb("posp", [P, SEQ_T, EXPERTS])
        w = sb("rw", [P, SEQ_T, EXPERTS])
        before = sb("before", [P, P], BF16)
        ones = sb("ones", [P, P], BF16)
        zeros = sb("zeros", [P, DIM])
        ps_a = banks("ps_a", 2)
        ps_x = banks("ps_x", 4)
        ps_l, ps_p = banks("ps_l", 2)
        s_kept = [sem(f"m_kept{j}") for j in range(2)]
        s = {n: sem("m_" + n) for n in """gw_in const consts a_full a_used var rstd ch x_new xn_made xn_out acc_out xt_full
            xt_evac l_full nmax prob_done selb_made p_full stage moe_const zero_out""".split()}
        block = stack.enter_context(nc.Block())

        def x_tile(b, j):
            return x_sb[:, bass.ds(b * SEQ_T + j, 1), :].rearrange("p o d -> p (o d)")

        @block.sync
        def _(sp):
            sp.dma_start(gw[:, :, :], a["gw"]).then_inc(s["gw_in"], 16)
            with sp.Fori(0, BATCH // 2) as i:
                for j in range(2):
                    sp.wait_ge(s["x_new"], i * 2 * SEQ_T)
                    sp.dma_start(kept[:, j, :, :],
                                 a["kept"][bass.ds((i * 2 + j) * SEQ_T, SEQ_T), :, :].rearrange("i p n -> p i n"))\
                        .then_inc(s_kept[j], 16)
                for j in range(2):
                    b = i * 2 + j
                    sp.wait_ge(s["x_new"], b * SEQ_T + SEQ_T)
                    sp.dma_start(a["acc"][bass.ds(b * SEQ, SEQ), :].rearrange("(i p) d -> p i d", p=P),
                                 x_sb[:, bass.ds(b * SEQ_T, SEQ_T), :]).then_inc(s["acc_out"], 16)
                    sp.wait_ge(s["xn_made"], b * SEQ_T + SEQ_T)
                    sp.dma_start(a["xn"][bass.ds(b * SEQ, SEQ), :].rearrange("(i p) d -> p i d", p=P),
                                 xn[:, :, :]).then_inc(s["xn_out"], 16)
            sp.wait_ge(s["consts"], 5)
            for k in range(HALVES):
                sp.dma_start(a["acc"][T + k * P:T + (k + 1) * P, :], zeros[:, :]).then_inc(s["zero_out"], 16)
            sp.wait_ge(s["zero_out"], 16 * HALVES)
            sp.wait_ge(s["acc_out"], 16 * BATCH)
            sp.wait_ge(s["xn_out"], 16 * BATCH)

        @block.gpsimd
        def _(pool):
            pool.memset(half[:, :], -0.5).then_inc(s["consts"], 1)
            pool.memset(zeros[:, :], 0.0).then_inc(s["consts"], 1)
            pool.memset(ones[:, :], 1.0).then_inc(s["consts"], 1)
            pool.memset(takenb[:, :], 0.0).then_inc(s["consts"], 1)
            pool.memset(taken[:, :], 0.0).then_inc(s["consts"], 1)
            pool.wait_ge(s["consts"], 5)
            pool.affine_select(out=before[:, :], in_=ones[:, :], compare_op=ALU.is_gt, fill=0.0, base=0,
                               pattern=[[1, P]], channel_multiplier=-1).then_inc(s["consts"], 1)
            with pool.Fori(0, BATCH) as b:
                for n in range(2):
                    pool.wait_ge(s["var"], b * 2 + n + 1)
                    pool.tensor_tensor(rstd[:, :], ve[:, :], half[:, :], ALU.pow).then_inc(s["rstd"], 1)

        @block.tensor
        def _(pe):
            pe.wait_ge(s["gw_in"], 16)
            pe.wait_ge(s["consts"], 6)
            with pe.Fori(0, BATCH // 2) as i:
                for slot in range(2):
                    b = i * 2 + slot
                    pe.wait_ge(s_kept[slot], i * 16 + 16)
                    for j in range(SEQ_T):
                        if j < 2:
                            pe.wait_ge(s["a_used"], b * SEQ_T)
                        else:
                            pe.wait_ge(s["a_used"], b * SEQ_T + j - 1)
                        for k in range(SEQ_T):
                            tr = pe.transpose(ps_a[j % 2][:, k * P:(k + 1) * P], kept[:, slot, k, j * P:(j + 1) * P],
                                              ident[:, :])
                        tr.then_inc(s["a_full"], 1)
                    for j in range(SEQ_T):
                        pe.wait_ge(s["xn_made"], b * SEQ_T + j + 1)
                        pe.wait_ge(s["xt_evac"], b * SEQ_T)
                        for k in range(KT):
                            tr = pe.transpose(ps_x[j][:, k * P:(k + 1) * P], xn[:, j, k * P:(k + 1) * P], ident[:, :])
                        tr.then_inc(s["xt_full"], 1)
                    for j in range(SEQ_T):
                        pe.wait_ge(s["xt_evac"], b * SEQ_T + j + 1)
                        for k in range(KT):
                            mm = pe.matmul(ps_l[:, j * EXPERTS:(j + 1) * EXPERTS], xnT[:, j, k * P:(k + 1) * P],
                                           gw[:, k, :], start=(k == 0), stop=(k == KT - 1))
                        mm.then_inc(s["l_full"], 1)
                    pe.wait_ge(s["selb_made"], b + 1)
                    for j in range(SEQ_T):
                        out = ps_p[:, j * EXPERTS:(j + 1) * EXPERTS]
                        pe.matmul(out, before[:, :], selb[:, j, :], start=True, stop=False)
                        for k in range(j):
                            pe.matmul(out, ones[:, :], selb[:, k, :], start=False, stop=False)
                        mm = pe.matmul(out, ones[:, :], takenb[:, :], start=False, stop=True)
                    mm.then_inc(s["p_full"], 1)

        @block.scalar
        def _(act):
            with act.Fori(0, BATCH) as b:
                for j in range(SEQ_T):
                    act.wait_ge(s["xt_full"], b * SEQ_T + j + 1)
                    act.activation(xnT[:, j, :], ps_x[j][:, :], ACT.Copy).then_inc(s["xt_evac"], 1)
                for j in range(SEQ_T):
                    act.wait_ge(s["nmax"], b + 1)
                    act.activation(prob[:, j, :], logit[:, j, :], ACT.Exp, bias=nmax[:, j:j + 1],
                                   accum_out=psum_e[:, j:j + 1]).then_inc(s["prob_done"], 1)

        @block.vector
        def _(dve):
            PER = 50
            with dve.Fori(0, BATCH // 2) as i:
                for slot in range(2):
                    b = i * 2 + slot
                    ch = Chain(dve, s["ch"], b * PER)
                    tiles = [x_tile(b, j) for j in range(SEQ_T)]
                    norm_stats(dve, ch, tiles, stats, mv, ve).then_inc(s["var"], 1)
                    dve.wait_ge(s["rstd"], b * 2 + 1)
                    ch.link(dve.tensor_scalar(shift[:, :], rstd[:, :], g["mix"][:, 0:1], None, ALU.mult))
                    ch.link(dve.tensor_scalar(scl[:, :], shift[:, :], 1.0, None, ALU.add))
                    ch.link(dve.scalar_tensor_tensor(shift[:, :], shift[:, :], -1.0, mv[:, :, 0], ALU.mult, ALU.mult))
                    for j in range(SEQ_T):
                        ch.add(dve.tensor_scalar(tiles[j], tiles[j], scl[:, j:j + 1], shift[:, j:j + 1],
                                                 ALU.mult, ALU.add))
                    ch.now()
                    for j in range(SEQ_T):
                        dve.wait_ge(s["a_full"], b * SEQ_T + j + 1)
                        dve.scalar_tensor_tensor(tiles[j], ps_a[j % 2][:, :], g["mix"][:, 1:2], tiles[j],
                                                 ALU.mult, ALU.add).then_inc(s["a_used"], 1)
                    for j in range(SEQ_T):
                        dve.wait_ge(s["a_used"], b * SEQ_T + j + 1)
                        dve.scalar_tensor_tensor(tiles[j], kept[:, slot, j, :], g["mix"][:, 1:2], tiles[j],
                                                 ALU.mult, ALU.add).then_inc(s["x_new"], 1)
                    dve.wait_ge(s["x_new"], b * SEQ_T + SEQ_T)
                    stand(dve)
                    norm_stats(dve, ch, tiles, stats, mv, ve).then_inc(s["var"], 1)
                    dve.wait_ge(s["rstd"], b * 2 + 2)
                    dve.wait_ge(s["xn_out"], b * 16)
                    for j in range(SEQ_T):
                        dve.tensor_scalar(xn[:, j, :], tiles[j], mv[:, j, 0:1], rstd[:, j:j + 1],
                                          ALU.subtract, ALU.mult).then_inc(s["xn_made"], 1)
                    dve.wait_ge(s["l_full"], b * SEQ_T + SEQ_T)
                    ch.link(dve.tensor_copy(logit[:, :, :], ps_l[:, 0:SEQ_T * EXPERTS]
                                            .rearrange("p (j e) -> p j e", j=SEQ_T)))
                    stand(dve)
                    for j in range(SEQ_T):
                        ch.add(dve.max(top8[:, j, :], logit[:, j, :]))
                    ch.now()
                    dve.tensor_scalar(nmax[:, :], top8[:, :, 0], -1.0, None, ALU.mult).then_inc(s["nmax"], 1)
                    for j in range(SEQ_T):
                        ch.add(dve.match_replace(rest[:, j, :], top8[:, j, :], logit[:, j, :], LOWEST))
                    ch.now()
                    ch.link(dve.tensor_tensor(sel[:, :, :], rest[:, :, :], logit[:, :, :], ALU.not_equal))
                    dve.tensor_copy(selb[:, :, :], sel[:, :, :]).then_inc(s["selb_made"], 1)
                    dve.wait_ge(s["p_full"], b + 1)
                    places = ps_p[:, 0:SEQ_T * EXPERTS].rearrange("p (j e) -> p j e", j=SEQ_T)
                    ch.link(dve.scalar_tensor_tensor(valid[:, :, :], places, float(CAP), sel[:, :, :],
                                                     ALU.is_lt, ALU.mult))
                    ch.link(dve.scalar_tensor_tensor(posp[:, :, :], places, 1.0, valid[:, :, :], ALU.add, ALU.mult))
                    ch.add(dve.tensor_scalar(r["place"][:, bass.ds(b * SEQ_T, SEQ_T), :], posp[:, :, :], -1.0, None,
                                             ALU.add))
                    ch.link(dve.tensor_reduce(count[:, :], sel[:, :, :].rearrange("p j e -> p e j"), AX, ALU.add))
                    ch.link(dve.tensor_tensor(taken[:, :], taken[:, :], count[:, :], ALU.add))
                    ch.link(dve.tensor_copy(takenb[:, :], taken[:, :]))
                    dve.wait_ge(s["prob_done"], b * SEQ_T + SEQ_T)
                    ch.link(dve.reciprocal(rden[:, :], psum_e[:, :]))
                    ch.link(dve.tensor_scalar(rden[:, :], rden[:, :], g["th"][:, 3:4], None, ALU.mult))
                    for j in range(SEQ_T):
                        ch.add(dve.scalar_tensor_tensor(w[:, j, :], prob[:, j, :], rden[:, j:j + 1], valid[:, j, :],
                                                        ALU.mult, ALU.mult))
                    ch.now()
                    for part in range(3):
                        dst = r["parts"][:, bass.ds(b * SEQ_T, SEQ_T), part, :]
                        ch.link(dve.tensor_copy(dst, w[:, :, :]))
                        if part < 2:
                            ch.link(dve.tensor_tensor(w[:, :, :], w[:, :, :], dst, ALU.subtract))
                    assert ch.n == PER, ch.n


def phase_experts(nc, a, ident, g, r, out):
    with ExitStack() as stack:
        sb, banks, sem = scoped(nc, stack)
        GROUP = 4
        wg = sb("wg", [P, 2, KT, FE])
        wu = sb("wu", [P, 2, KT, FE])
        wd = sb("wd", [P, 2, FET, DIM])
        slots = sb("slots", [P, CAP])
        slotsb = sb("slotsb", [P, CAP], BF16)
        spare = sb("spare", [P, HALVES])
        cur = sb("cur", [P, 2, TILES])
        pick = sb("pick_e", [P, 2, TILES, CAP], BF16)
        vals = sb("vals", [P, 2, TILES, 6], BF16)
        table = sb("table", [P, HALVES, 6])
        wsum = sb("wsum_e", [P, HALVES])
        weight = sb("weight", [P, GROUP, HALVES])
        tokf = sb("tokf", [P, HALVES])
        empty = sb("empty", [P, HALVES])
        src_row = sb("src_row", [P, GROUP, HALVES], U32)
        dst_row = sb("dst_row", [P, GROUP, HALVES], U32)
        xg = sb("xg", [P, 2, HALVES, DIM])
        xgT = sb("xgT", [P, KT, CAP])
        th = sb("th_e", [P, FET * CAP])
        u = sb("u_e", [P, FET * CAP])
        hT = sb("hT_e", [P, FET, CAP])
        y = sb("y_e", [P, 2, HALVES, DIM])
        ps_tab, ps_g, ps_u = banks("ps_tgu", 3)
        ps_x = banks("ps_xg", 2)
        ps_y = banks("ps_y", 2)
        s_w = [sem(f"e_w{j}") for j in range(2)]
        s_gat = [sem(f"e_gat{j}") for j in range(2)]
        s = {n: sem("e_" + n) for n in """const slots cur_made pick_made tab_full tab_read ch tabled xt_full xt_evac
            gu_full tanh_done u_made h_made y_full y_evac scat out""".split()}
        block = stack.enter_context(nc.Block())

        def loop(eng, body):
            body(0)
            with eng.Fori(1, EXPERTS // GROUP - 1) as i:
                body(i)
            body(EXPERTS // GROUP - 1)

        def last_group(i):
            return isinstance(i, int) and i > 0

        def count2(i, q, ahead=0):
            return i * (GROUP // 2) + (q + ahead) // 2 + 1

        @block.sync
        def _(sp):
            def body(i):
                for q in range(GROUP):
                    e, k = i * GROUP + q, q % 2
                    need(sp, s["y_full"], e * 2 - 2)
                    one = bass.ds(e, 1)
                    sp.dma_start(wg[:, k, :, :], a["w_gate"][one, :, :].rearrange("o (k p) f -> p (o k) f", p=P))\
                        .then_inc(s_w[k], 16)
                    sp.dma_start(wu[:, k, :, :], a["w_up"][one, :, :].rearrange("o (k p) f -> p (o k) f", p=P))\
                        .then_inc(s_w[k], 16)
                    sp.dma_start(wd[:, k, :, :], a["w_down"][one, :, :].rearrange("o (k p) f -> p (o k) f", p=P))\
                        .then_inc(s_w[k], 16)

            loop(sp, body)
            sp.wait_ge(s["scat"], 32 * EXPERTS)
            sp.dma_start(out, a["acc"][0:T, :]).then_inc(s["out"], 16)
            sp.wait_ge(s["out"], 16)

        @block.gpsimd
        def _(pool):
            pool.iota(slots[:, :], pattern=[[1, CAP]], base=0, channel_multiplier=0,
                      allow_small_or_imprecise_dtypes=True).then_inc(s["const"], 1)
            pool.iota(spare[:, :], pattern=[[P, HALVES]], base=T, channel_multiplier=1,
                      allow_small_or_imprecise_dtypes=True).then_inc(s["const"], 1)
            for k in range(2):
                pool.iota(vals[:, k, :, 3], pattern=[[1, TILES]], base=0, channel_multiplier=0,
                          allow_small_or_imprecise_dtypes=True).then_inc(s["const"], 1)
                pool.iota(vals[:, k, :, 4], pattern=[[0, TILES]], base=0, channel_multiplier=1,
                          allow_small_or_imprecise_dtypes=True).then_inc(s["const"], 1)
                pool.memset(vals[:, k, :, 5], 1.0).then_inc(s["const"], 1)

            def gather(i, q, ahead):
                e = i * GROUP + q + ahead
                qq = (q + ahead) % GROUP
                pool.wait_ge(s["tabled"], e + 1)
                need(pool, s["xt_full"], e * 2 - 2)
                stand(pool)
                for n in range(HALVES):
                    pool.indirect_dma_start(xg[:, qq % 2, n, :], None, a["xn"][:, :],
                                            bass.IndirectOffsetOnAxis(ap=src_row[:, qq, n:n + 1], axis=0))\
                        .then_inc(s_gat[qq % 2], 16)

            def scatter(i, q, back):
                e = i * GROUP + q - back
                qq = (q - back) % GROUP
                pool.wait_ge(s["y_evac"], e * 2 + 2)
                need(pool, s["scat"], e * 32)
                stand(pool)
                for n in range(HALVES):
                    pool.indirect_dma_start(a["acc"][:, :], bass.IndirectOffsetOnAxis(ap=dst_row[:, qq, n:n + 1], axis=0),
                                            y[:, qq % 2, n, :], None, compute_op=ALU.add)\
                        .then_inc(s["scat"], 16)

            gather(0, 0, 0)
            gather(0, 1, 0)

            def body(i):
                for q in range(GROUP):
                    if not (isinstance(i, int) and i == 0 and q == 0):
                        scatter(i, q, 1)
                    if not (last_group(i) and q >= GROUP - 2):
                        gather(i, q, 2)

            loop(pool, body)
            scatter(EXPERTS // GROUP - 1, GROUP, 1)

        @block.tensor
        def _(pe):
            def tabulate(i, q, ahead):
                e, k = i * GROUP + q + ahead, (q + ahead) % 2
                pe.wait_ge(s["pick_made"], e + 1)
                need(pe, s["tab_read"], e)
                for n in range(HALVES):
                    for t in range(TILES):
                        mm = pe.matmul(ps_tab[:, n * 6:(n + 1) * 6], pick[:, k, t, n * P:(n + 1) * P],
                                       vals[:, k, t, :], start=(t == 0), stop=(t == TILES - 1))
                mm.then_inc(s["tab_full"], 1)

            def turn(i, q, ahead):
                e, k = i * GROUP + q + ahead, (q + ahead) % 2
                pe.wait_ge(s_gat[k], count2(i, q, ahead) * 32)
                for n in range(HALVES):
                    need(pe, s["xt_evac"], e * 2 - 1 + n)
                    for c in range(KT):
                        tr = pe.transpose(ps_x[n][:, c * P:(c + 1) * P], xg[:, k, n, c * P:(c + 1) * P], ident[:, :])
                    tr.then_inc(s["xt_full"], 1)

            def gate_up(i, q):
                e, k = i * GROUP + q, q % 2
                pe.wait_ge(s_w[k], count2(i, q) * 48)
                pe.wait_ge(s["xt_evac"], e * 2 + 2)
                need(pe, s["h_made"], e)
                for w, ps in ((wg, ps_g), (wu, ps_u)):
                    for f in range(FET):
                        for c in range(KT):
                            mm = pe.matmul(ps[:, f * CAP:(f + 1) * CAP], w[:, k, c, f * P:(f + 1) * P], xgT[:, c, :],
                                           start=(c == 0), stop=(c == KT - 1))
                    mm.then_inc(s["gu_full"], 1)

            def down(i, q):
                e, k = i * GROUP + q, q % 2
                pe.wait_ge(s["h_made"], e + 1)
                for n in range(HALVES):
                    need(pe, s["y_evac"], e * 2 - 1 + n)
                    for f in range(FET):
                        mm = pe.matmul(ps_y[n][:, :], hT[:, f, n * P:(n + 1) * P], wd[:, k, f, :],
                                       start=(f == 0), stop=(f == FET - 1))
                    mm.then_inc(s["y_full"], 1)

            tabulate(0, 0, 0)
            tabulate(0, 1, 0)
            turn(0, 0, 0)

            def body(i):
                for q in range(GROUP):
                    gate_up(i, q)
                    if not (last_group(i) and q >= GROUP - 2):
                        tabulate(i, q, 2)
                    if not (last_group(i) and q == GROUP - 1):
                        turn(i, q, 1)
                    down(i, q)

            loop(pe, body)

        @block.scalar
        def _(act):
            def evac_x(i, q, ahead):
                e = i * GROUP + q + ahead
                for n in range(HALVES):
                    act.wait_ge(s["xt_full"], e * 2 + n + 1)
                    act.activation(xgT[:, :, n * P:(n + 1) * P], ps_x[n][:, :].rearrange("p (k c) -> p k c", k=KT),
                                   ACT.Copy).then_inc(s["xt_evac"], 1)

            evac_x(0, 0, 0)

            def body(i):
                for q in range(GROUP):
                    e = i * GROUP + q
                    act.wait_ge(s["gu_full"], e * 2 + 1)
                    need(act, s["u_made"], e)
                    act.activation(th[:, :], ps_g[:, :], ACT.Tanh, scale=0.5).then_inc(s["tanh_done"], 1)
                    if not (last_group(i) and q == GROUP - 1):
                        evac_x(i, q, 1)
                    need(act, s["scat"], e * 32 - 32)
                    for n in range(HALVES):
                        act.wait_ge(s["y_full"], e * 2 + n + 1)
                        act.activation(y[:, q % 2, n, :], ps_y[n][:, :], ACT.Copy, scale=weight[:, q, n:n + 1])\
                            .then_inc(s["y_evac"], 1)

            loop(act, body)

        @block.vector
        def _(dve):
            def make_pick(i, q, ahead):
                e, k = i * GROUP + q + ahead, (q + ahead) % 2
                need(dve, s["tab_full"], e - 1)
                one = bass.ds(e, 1)
                dve.tensor_copy(cur[:, k, :], r["place"][:, :, one].rearrange("p t o -> p (t o)"))\
                    .then_inc(s["cur_made"], 1)
                dve.tensor_copy(vals[:, k, :, 0:3], r["parts"][:, :, :, one].rearrange("p t c o -> p t (c o)"))\
                    .then_inc(s["cur_made"], 1)
                dve.wait_ge(s["cur_made"], e * 2 + 2)
                for t in range(TILES):
                    ins = dve.tensor_scalar(pick[:, k, t, :], slotsb[:, :], cur[:, k, t:t + 1], None, ALU.is_equal)
                ins.then_inc(s["pick_made"], 1)

            PER = 5

            def make_table(i, q, ahead):
                e, qq = i * GROUP + q + ahead, (q + ahead) % GROUP
                dve.wait_ge(s["tab_full"], e + 1)
                need(dve, s["tabled"], e)
                dve.tensor_copy(table[:, :, :], ps_tab[:, 0:HALVES * 6].rearrange("p (n c) -> p n c", n=HALVES))\
                    .then_inc(s["tab_read"], 1)
                dve.wait_ge(s["tab_read"], e + 1)
                need(dve, s["scat"], e * 32 - 96)
                ch = Chain(dve, s["ch"], e * PER)
                ch.add(dve.tensor_tensor(wsum[:, :], table[:, :, 2], table[:, :, 1], ALU.add))
                ch.add(dve.scalar_tensor_tensor(tokf[:, :], table[:, :, 3], float(P), table[:, :, 4],
                                                ALU.mult, ALU.add))
                ch.link(dve.tensor_tensor(empty[:, :], table[:, :, 5], spare[:, :], ALU.mult))
                ch.add(dve.tensor_tensor(weight[:, qq, :], wsum[:, :], table[:, :, 0], ALU.add))
                ch.link(dve.tensor_tensor(empty[:, :], spare[:, :], empty[:, :], ALU.subtract))
                dve.tensor_copy(src_row[:, qq, :], tokf[:, :])
                dve.tensor_tensor(dst_row[:, qq, :], tokf[:, :], empty[:, :], ALU.add).then_inc(s["tabled"], 1)
                assert ch.n == PER

            dve.wait_ge(s["const"], 8)
            dve.tensor_copy(slotsb[:, :], slots[:, :]).then_inc(s["slots"], 1)
            dve.wait_ge(s["slots"], 1)
            make_pick(0, 0, 0)
            make_pick(0, 1, 0)
            make_table(0, 0, 0)
            make_pick(0, 2, 0)
            make_table(0, 1, 0)

            def body(i):
                for q in range(GROUP):
                    e = i * GROUP + q
                    dve.wait_ge(s["tanh_done"], e + 1)
                    dve.scalar_tensor_tensor(u[:, :], th[:, :], 1.0, ps_g[:, :], ALU.add, ALU.mult)\
                        .then_inc(s["u_made"], 1)
                    dve.wait_ge(s["gu_full"], e * 2 + 2)
                    dve.wait_ge(s["u_made"], e + 1)
                    dve.scalar_tensor_tensor(hT[:, :, :].rearrange("p f c -> p (f c)"), u[:, :], 0.5, ps_u[:, :],
                                             ALU.mult, ALU.mult).then_inc(s["h_made"], 1)
                    if not (last_group(i) and q >= GROUP - 2):
                        make_table(i, q, 2)
                    if not (last_group(i) and q >= GROUP - 3):
                        make_pick(i, q, 3)

            loop(dve, body)


def build(nc, a, out):
    with ExitStack() as stack:
        def sb(name, shape, dt=F32):
            return stack.enter_context(nc.sbuf_tensor(name, shape, dt))

        ident = sb("ident", [P, P])
        r = {"place": sb("place", [P, TILES, EXPERTS]), "parts": sb("parts", [P, TILES, 3, EXPERTS], BF16)}
        g = {"raw": sb("g_raw", [P, 5]), "th": sb("g_th", [P, 5]), "tmp": sb("g_tmp", [P, 3]),
             "mix": sb("g_mix", [P, 2]), "lut": sb("g_lut", [P, LUT])}
        with nc.semaphore("s_ident") as s_ident, nc.Block() as block:
            @block.gpsimd
            def _(pool):
                pool.memset(ident[:, :], 0.0).then_inc(s_ident, 1)
                pool.wait_ge(s_ident, 1)
                pool.affine_select(out=ident[:, :], in_=ident[:, :], compare_op=ALU.not_equal, fill=1.0, base=0,
                                   pattern=[[-1, P]], channel_multiplier=1).then_inc(s_ident, 1)

        with nc.sbuf_tensor("x_sb", [P, TILES, DIM], F32) as x_sb:
            with nc.sbuf_tensor("xT", [P, KT, T], F32) as xT:
                phase_prepare(nc, a, x_sb, g)
                phase_norm_transpose(nc, "n1", x_sb, xT, ident, load=a["x"])
                phase_attention(nc, a, x_sb, xT, ident, g)
                phase_norm_transpose(nc, "n2", x_sb, xT, ident)
                phase_swiglu(nc, a, x_sb, xT, g)
            phase_mix_route(nc, a, x_sb, ident, g, r)
        phase_experts(nc, a, ident, g, r, out)


def rope(length, dim):
    inv = (1.0 / 10000.0 ** (np.arange(0, dim, 2, dtype=np.float32) / np.float32(dim))).astype(np.float32)
    f = np.arange(length, dtype=np.float32)[:, None] * inv[None, :]
    return np.repeat(np.sin(f), 2, axis=-1), np.repeat(np.cos(f), 2, axis=-1)


def tables():
    half = D_CQ // 2
    sin, cos = rope(SEQ, D_CQ)
    sign = np.where(np.arange(D_CQ) < half, -1.0, 1.0).astype(np.float32)
    cols = latent_columns()
    rot = np.stack([cos[:, c].T for c in cols[:3]] + [(sin * sign)[:, c].T for c in cols[:3]], 1)
    sin, cos = rope(SEQ, D_C)
    sin = sin * np.where(np.arange(D_C) < D_C // 2, -1.0, 1.0).astype(np.float32)
    by_token = [m.reshape(SEQ_T, P, D_C).transpose(1, 0, 2) for m in (cos, sin)]
    return {"rot": rot, "ktab": np.stack([cos.T, sin.T], 1), "ttab": by_token[0], "stab": by_token[1]}


def latent_columns():
    half = D_CQ // 2
    a, rest = np.arange(P), np.arange(P, half)
    return [a, a + half, np.concatenate([rest, rest + half]), np.concatenate([rest + half, rest])]


def kernel(**inputs):
    import concourse.bacc as bacc
    from concourse.bass_utils import run_bass_kernel_spmd

    v = {k: np.asarray(x) for k, x in inputs.items()}
    cols = latent_columns()
    by_part = lambda m: m.reshape(-1, P, m.shape[-1]).transpose(1, 0, 2).reshape(P, -1)
    down = v["L0_ffn_down_idx"].T
    down = np.concatenate([down, np.zeros((FT * P - INTER, DIM), down.dtype)])
    idx = np.concatenate([by_part(v["L0_ffn_gate_idx"].T), by_part(v["L0_ffn_up_idx"].T), by_part(down)], 1)
    ctx = v["ctx_512"].reshape(T, D_C)
    arrays = {
        "x": v["x"].reshape(T, DIM), "ctx": ctx, "ctxT": ctx.T,
        "g_xattn": v["g_xattn"], "g_ffn": v["g_ffn"], "gamma": v["L1_xattn_gamma_raw"].reshape(1),
        "lut": v["L0_ffn_lut"],
        "wqa": v["L1_xattn_Wq"].T, "wka": v["L1_xattn_Wk"].T,
        "wq": v["L0_xattn_Wq"].T.reshape(KT, P, HEADS, HK).transpose(2, 1, 0, 3).reshape(HEADS, P, KT * HK),
        "wc": v["L0_xattn_w_kc_q"][:, :, np.concatenate(cols)],
        "wqrT": v["L0_xattn_W_qr"][:, np.concatenate(cols[:3]), :].transpose(0, 2, 1),
        "wkrT": v["L0_xattn_W_kr"].transpose(0, 2, 1),
        "wkc": v["L0_xattn_w_kc_kv"],
        "woT": v["L0_xattn_Wo"].T.reshape(HEADS, HK, DIM),
        "idx": idx.reshape(P, HEADS, LUT_CHUNK).transpose(1, 0, 2),
        "gw": v["L1_ffn_gate_w"].T.reshape(KT, P, EXPERTS).transpose(1, 0, 2),
        "w_gate": v["L1_ffn_w_gate"], "w_up": v["L1_ffn_w_up"], "w_down": v["L1_ffn_w_down"],
        **tables(),
    }
    arrays = {"in_" + k: np.ascontiguousarray(x) for k, x in arrays.items()}
    nc = bacc.Bacc("TRN2", target_bir_lowering=False, num_devices=1)
    a = {k[3:]: nc.dram_tensor(k, x.shape, mybir.dt.from_np(x.dtype), kind="ExternalInput").ap()
         for k, x in arrays.items()}
    for name, shape in (("w1", (HEADS, P, D_CQ)), ("w2", (HEADS, P, DIM)), ("aff", (TILES, P, SEQ)),
                        ("kept", (TILES, P, SEQ)), ("lutw", (HEADS, P, LUT_CHUNK)), ("xn", (T, DIM)),
                        ("acc", (T + CAP, DIM))):
        a[name] = nc.dram_tensor("via_" + name, shape, F32).ap()
    out = nc.dram_tensor("out", (T, DIM), F32, kind="ExternalOutput").ap()
    build(nc, a, out)
    result = run_bass_kernel_spmd(nc, [arrays], core_ids=[0])
    return result.results[0]["out"].reshape(BATCH, SEQ, DIM)
```

```python
from contextlib import ExitStack

import numpy as np
import concourse.bass as bass
from concourse import mybir

ALU = mybir.AluOpType
ACT = mybir.ActivationFunctionType
F32 = mybir.dt.float32
F32R = mybir.dt.float32r
BF16 = mybir.dt.bfloat16
I32 = mybir.dt.int32
U32 = mybir.dt.uint32
AX = mybir.AxisListType.X

P = 128
BATCH, SEQ, DIM = 4, 512, 512
T = BATCH * SEQ
TILES = T // P
KT = DIM // P
SEQ_T = SEQ // P
HEADS, HK, D_C, D_CQ, ROT = 16, 128, 128, 384, 64
QT = D_CQ // P
UNITS = HEADS * BATCH
INTER = 1376
FT = (INTER + P - 1) // P
F_LAST = INTER - (FT - 1) * P
LUT = 16
PICKS = 4
GU_W = KT * INTER
LUT_W = 2 * GU_W + FT * DIM
LUT_CHUNK = LUT_W // HEADS
TOP = int(SEQ * 0.3)
ROUNDS = (TOP - 1) // 8
AFF_SCALE = 1.0 / (float(np.sqrt(np.float32(32))) * 4)
EXPERTS, CHOSEN, CAP, FE = 64, 8, 256, 256
FET = FE // P
HALVES = CAP // P
EPS = 1e-5
LOWEST = -3.0e38
assert LUT_CHUNK * HEADS == LUT_W and 8 * ROUNDS < TOP <= 8 * ROUNDS + 8


def need(eng, sem, n):
    if isinstance(n, int) and n <= 0:
        return
    eng.wait_ge(sem, n)


def stand(eng):
    eng.nop(nofuse=True)


class Chain:

    def __init__(self, eng, sem, base=0):
        self.eng, self.sem, self.base, self.n = eng, sem, base, 0

    def add(self, ins):
        ins.then_inc(self.sem, 1)
        self.n += 1
        return self.n

    def now(self):
        self.eng.wait_ge(self.sem, self.base + self.n)

    def link(self, ins):
        self.add(ins)
        self.now()


def scoped(nc, stack):
    def sb(name, shape, dt=F32):
        return stack.enter_context(nc.sbuf_tensor(name, shape, dt))

    def banks(name, n):
        return [stack.enter_context(nc.psum_tensor(f"{name}{i}", [P, 512], F32)) for i in range(n)]

    def sem(name):
        return stack.enter_context(nc.semaphore(name))

    return sb, banks, sem


def split_product(pe, out, a_parts, b_parts, start, stop, before_low=None):
    (a_hi, a_lo), (b_hi, b_lo) = a_parts, b_parts
    pe.matmul(out, a_hi, b_hi, start=start, stop=False)
    pe.matmul(out, a_lo, b_hi, start=False, stop=False)
    if before_low is not None:
        before_low()
    return pe.matmul(out, a_hi, b_lo, start=False, stop=stop)


def norm_stats(dve, ch, tiles, stats, mv, ve):
    n = len(tiles)
    for j, x in enumerate(tiles):
        ch.add(dve.bn_stats(stats[:, j, :], x))
    ch.now()
    stand(dve)
    for j in range(n):
        ch.add(dve.bn_aggr(mv[:, j, :], stats[:, j, :]))
    ch.now()
    return dve.tensor_scalar(ve[:, 0:n], mv[:, 0:n, 1], EPS, None, ALU.add)


def phase_prepare(nc, a, x_sb, xT, kvT, kv, ident, g):
    with ExitStack() as stack:
        sb, banks, sem = scoped(nc, stack)
        GROUP = HEADS // BATCH
        ctxT = sb("ctxT", [P, T])
        qaT = sb("qaT", [P, T])
        kaT = sb("kaT", [P, T])
        wqa = sb("wqa", [P, P])
        wka = sb("wka", [P, P])
        w1 = sb("fold1", [P, HEADS, D_CQ])
        wkrT = sb("wkrT", [ROT, HEADS, D_C])
        wkc = sb("wkc", [P, HEADS, D_C])
        w2 = sb("fold2", [P, HEADS, DIM])
        affo = sb("affo", [P, 2, SEQ])
        stats = sb("stats1", [P, TILES, 6])
        mv = sb("mv1", [P, TILES, 2])
        ve = sb("ve1", [P, TILES])
        half = sb("half1", [P, SEQ_T])
        rstd = sb("rstd1", [P, TILES])
        xn = sb("xn1", [P, 4, DIM])
        ps = banks("prep", 8)

        flat = xT[:, :, :].rearrange("p k t -> p (k t)")
        swapped = flat[:, 0:T]
        straight = flat[:, 2 * T:3 * T]
        tok = flat[:, T:2 * T].rearrange("p (i d) -> p i d", d=D_C)
        tmp = flat[:, 2 * T:3 * T].rearrange("p (i d) -> p i d", d=D_C)
        ktab = flat[:, 3 * T:3 * T + 2 * SEQ].rearrange("p (c t) -> p c t", c=2)
        ttab = flat[:, 3 * T + 2 * SEQ:3 * T + 3 * SEQ].rearrange("p (i d) -> p i d", d=D_C)
        stab = flat[:, 3 * T + 3 * SEQ:4 * T].rearrange("p (i d) -> p i d", d=D_C)

        s_gate = sem("s_gate")
        s_tanh = sem("s_tanh")
        s_gsm = sem("s_gsm")
        s_ctx = sem("s_ctx")
        s_kvT = sem("s_kvT")
        s_kv = sem("s_kv")
        s_rope = sem("s_rope")
        s_x = [sem(f"s_x{b}") for b in range(BATCH)]
        s_qk = sem("s_qk")
        s_qkc = sem("s_qkc")
        s_aff = sem("s_aff")
        s_affc = sem("s_affc")
        s_affo = [sem(f"s_affo{j}") for j in range(2)]
        s_win = [sem(f"s_win{j}") for j in range(BATCH)]
        s_fold = sem("s_fold")
        s_foldc = sem("s_foldc")
        s_fout = sem("s_fout")
        s_half = sem("s_half")
        s_var = sem("s_var")
        s_rstd = sem("s_rstd")
        s_ch = sem("s_ch")
        s_xn = sem("s_xn")
        s_tr = sem("s_tr")
        s_out = sem("s_out")
        block = stack.enter_context(nc.Block())

        @block.sync
        def _(sp):
            for dst, src in ((ctxT[:, :], a["ctxT"]), (wqa[:, :], a["wqa"]), (wka[:, :], a["wka"])):
                sp.dma_start(dst, src).then_inc(s_ctx, 16)
            for lo, hi in ((0, P // 2), (P // 2, P)):
                sp.dma_start(swapped[lo:hi, :], a["ctxT"][P // 2 - lo:P - lo, :]).then_inc(s_kvT, 16)
            sp.dma_start(ktab, a["ktab"]).then_inc(s_kvT, 16)
            for dst, src in ((ttab, a["ttab"]), (stab, a["stab"]),
                             (tok, a["ctx"].rearrange("(i p) d -> p i d", p=P))):
                sp.dma_start(dst, src).then_inc(s_kv, 16)
            for src, dst in ((a["g_xattn"], g["raw"][:, 0:2]), (a["g_ffn"], g["raw"][:, 2:4]),
                             (a["gamma"], g["raw"][:, 4:5])):
                sp.dma_start(dst, src.partition_broadcast(P)).then_inc(s_gate, 16)
            sp.dma_start(g["lut"][:, :], a["lut"].partition_broadcast(P)).then_inc(s_gate, 16)
            for b in range(BATCH):
                sp.dma_start(x_sb[:, b * SEQ_T:(b + 1) * SEQ_T, :],
                             a["x"][b * SEQ:(b + 1) * SEQ, :].rearrange("(i p) d -> p i d", p=P))\
                    .then_inc(s_x[b], 16)
            for t in range(TILES):
                sp.wait_ge(s_affc, t + 1)
                sp.dma_start(a["aff"][t], affo[:, t % 2, :]).then_inc(s_affo[t % 2], 16)
            for j in range(2):
                sp.wait_ge(s_affo[j], 16 * TILES // 2)
            for n in range(BATCH):
                heads = slice(n * GROUP, (n + 1) * GROUP)
                sp.wait_ge(s_foldc, (n + 1) * 2 * GROUP)
                sp.dma_start(a["w1"][heads].rearrange("h p n -> p h n"), w1[:, heads, :]).then_inc(s_fout, 16)
                sp.dma_start(a["w2"][heads].rearrange("h p n -> p h n"), w2[:, heads, :]).then_inc(s_fout, 16)
            sp.wait_ge(s_fout, 32 * BATCH)

        @block.gpsimd
        def _(pool):
            pool.memset(half[:, :], -0.5).then_inc(s_half, 1)
            pool.wait_ge(s_half, 1)
            for b in range(BATCH):
                pool.wait_ge(s_var, b + 1)
                lo = b * SEQ_T
                pool.tensor_tensor(rstd[:, lo:lo + SEQ_T], ve[:, lo:lo + SEQ_T], half[:, :], ALU.pow)\
                    .then_inc(s_rstd, 1)

        @block.tensor
        def _(pe):
            pe.wait_ge(s_ctx, 48)
            for n in range(BATCH):
                for m, w in enumerate((wqa, wka)):
                    k = 2 * n + m
                    if k >= 4:
                        pe.wait_ge(s_qkc, k - 3)
                    pe.matmul(ps[4 + k % 4][:, :], w[:, :], ctxT[:, n * SEQ:(n + 1) * SEQ], start=True, stop=True)\
                        .then_inc(s_qk, 1)
            for t in range(TILES):
                b = t // SEQ_T
                pe.wait_ge(s_qkc, 2 * BATCH)
                if t >= 4:
                    pe.wait_ge(s_affc, t - 3)
                pe.matmul(ps[4 + t % 4][:, :], qaT[:, t * P:(t + 1) * P], kaT[:, b * SEQ:(b + 1) * SEQ],
                          start=True, stop=True).then_inc(s_aff, 1)
            for n in range(BATCH):
                pe.wait_ge(s_win[n], 64)
                for h in range(n * GROUP, (n + 1) * GROUP):
                    j = h % 2
                    if h >= 2:
                        pe.wait_ge(s_foldc, 2 * h - 2)
                    for t in range(QT):
                        mm = pe.matmul(ps[2 * j][:, t * P:(t + 1) * P], w1[0:ROT, h, t * P:(t + 1) * P],
                                       wkrT[:, h, :], start=True, stop=True)
                    mm.then_inc(s_fold, 1)
                    pe.matmul(ps[2 * j + 1][:, :], wkc[:, h, :], w2[:, h, :], start=True, stop=True)\
                        .then_inc(s_fold, 1)
                for t in range(n * SEQ_T, (n + 1) * SEQ_T):
                    pe.wait_ge(s_xn, t + 1)
                    if t >= 4:
                        pe.wait_ge(s_out, t - 3)
                    else:
                        pe.wait_ge(s_affc, TILES - 3 + t)
                    for k in range(KT):
                        tr = pe.transpose(ps[4 + t % 4][:, k * P:(k + 1) * P], xn[:, t % 4, k * P:(k + 1) * P],
                                          ident[:, :])
                    tr.then_inc(s_tr, 1)

        @block.scalar
        def _(act):
            for n in range(BATCH):
                heads = slice(n * GROUP, (n + 1) * GROUP)
                for src, dst in ((a["wqrT"], w1[0:ROT, heads, :]), (a["wkrT"], wkrT[:, heads, :]),
                                 (a["wkc"], wkc[:, heads, :]), (a["woT"], w2[:, heads, :])):
                    act.dma_start(dst, src[heads].rearrange("h p n -> p h n")).then_inc(s_win[n], 16)
            for k in range(2 * BATCH):
                act.wait_ge(s_qk, k + 1)
                n, dst = k // 2, (qaT, kaT)[k % 2]
                act.activation(dst[:, n * SEQ:(n + 1) * SEQ], ps[4 + k % 4][:, :], ACT.Copy).then_inc(s_qkc, 1)
            for t in range(TILES):
                act.wait_ge(s_aff, t + 1)
                if t >= 2:
                    act.wait_ge(s_affo[t % 2], 16 * (t // 2))
                act.activation(affo[:, t % 2, :], ps[4 + t % 4][:, :], ACT.Copy).then_inc(s_affc, 1)
            act.wait_ge(s_gate, 64)
            act.activation(g["th"][:, 0:4], g["raw"][:, 0:4], ACT.Tanh).then_inc(s_tanh, 1)
            act.activation(g["th"][:, 4:5], g["raw"][:, 4:5], ACT.Tanh, scale=0.5).then_inc(s_tanh, 1)
            act.wait_ge(s_tanh, 2)
            for n in range(BATCH):
                for h in range(n * GROUP, (n + 1) * GROUP):
                    act.wait_ge(s_fold, 2 * h + 1)
                    act.activation(w1[:, h, :], ps[2 * (h % 2)][:, 0:D_CQ], ACT.Copy).then_inc(s_foldc, 1)
                    act.wait_ge(s_fold, 2 * h + 2)
                    act.activation(w2[:, h, :], ps[2 * (h % 2) + 1][:, :], ACT.Copy, scale=g["th"][:, 0:1])\
                        .then_inc(s_foldc, 1)
                for t in range(n * SEQ_T, (n + 1) * SEQ_T):
                    act.wait_ge(s_tr, t + 1)
                    act.activation(xT[:, :, t * P:(t + 1) * P],
                                   ps[4 + t % 4][:, :].rearrange("p (k c) -> p k c", k=KT), ACT.Copy)\
                        .then_inc(s_out, 1)

        @block.vector
        def _(dve):
            dve.wait_ge(s_ctx, 48)
            dve.wait_ge(s_kvT, 48)
            for b in range(BATCH):
                c = slice(b * SEQ, (b + 1) * SEQ)
                dve.tensor_tensor(straight[:, c], ctxT[:, c], ktab[:, 0, :], ALU.mult)
                ins = dve.tensor_tensor(swapped[:, c], swapped[:, c], ktab[:, 1, :], ALU.mult)
            ins.then_inc(s_rope, 1)
            dve.wait_ge(s_rope, 1)
            dve.tensor_tensor(swapped[:, :], straight[:, :], swapped[:, :], ALU.add).then_inc(s_rope, 1)
            dve.wait_ge(s_rope, 2)
            dve.tensor_copy(kvT[:, 0, :], swapped[:, :]).then_inc(s_rope, 1)
            dve.wait_ge(s_rope, 3)
            dve.tensor_tensor(kvT[:, 1, :], swapped[:, :], kvT[:, 0, :], ALU.subtract).then_inc(s_rope, 1)
            H = D_C // 2
            dve.wait_ge(s_kv, 48)
            for b in range(BATCH):
                r = slice(b * SEQ_T, (b + 1) * SEQ_T)
                dve.tensor_tensor(kv[:, r, :], tok[:, r, :], ttab, ALU.mult)
                dve.tensor_tensor(tmp[:, r, 0:H], tok[:, r, H:], stab[:, :, 0:H], ALU.mult)
                ins = dve.tensor_tensor(tmp[:, r, H:], tok[:, r, 0:H], stab[:, :, H:], ALU.mult)
            ins.then_inc(s_rope, 1)
            dve.wait_ge(s_rope, 5)
            dve.tensor_tensor(kv[:, :, :], kv[:, :, :], tmp, ALU.add).then_inc(s_rope, 1)
            ch = Chain(dve, s_ch)
            for b in range(BATCH):
                dve.wait_ge(s_x[b], 16)
                lo = b * SEQ_T
                norm_stats(dve, ch, [x_sb[:, lo + j, :] for j in range(SEQ_T)], stats[:, lo:lo + SEQ_T, :],
                           mv[:, lo:lo + SEQ_T, :], ve[:, lo:lo + SEQ_T]).then_inc(s_var, 1)
                dve.wait_ge(s_rstd, b + 1)
                if b == 0:
                    dve.wait_ge(s_rope, 6)
                for t in range(lo, lo + SEQ_T):
                    if t >= 4:
                        dve.wait_ge(s_tr, t - 3)
                    dve.tensor_scalar(xn[:, t % 4, :], x_sb[:, t, :], mv[:, t, 0:1], rstd[:, t:t + 1],
                                      ALU.subtract, ALU.mult).then_inc(s_xn, 1)
            ch = Chain(dve, s_gsm)
            dve.wait_ge(s_tanh, 2)
            ch.link(dve.tensor_scalar(g["tmp"][:, 0:1], g["th"][:, 4:5], 0.5, 0.5, ALU.mult, ALU.add))
            ch.link(dve.tensor_scalar(g["tmp"][:, 1:2], g["tmp"][:, 0:1], -1.0, 1.0, ALU.mult, ALU.add))
            ch.add(dve.tensor_tensor(g["mix"][:, 0:1], g["tmp"][:, 1:2], g["th"][:, 1:2], ALU.mult))
            ch.link(dve.tensor_tensor(g["tmp"][:, 2:3], g["tmp"][:, 0:1], g["th"][:, 1:2], ALU.mult))
            ch.add(dve.tensor_scalar(g["mix"][:, 1:2], g["tmp"][:, 2:3], 0.25, None, ALU.mult))


def phase_norm_transpose(nc, name, x_sb, xT, ident, fetch):
    with ExitStack() as stack:
        sb, banks, sem = scoped(nc, stack)
        stats = sb(name + "stats", [P, TILES, 6])
        mv = sb(name + "mv", [P, TILES, 2])
        ve = sb(name + "ve", [P, TILES])
        half = sb(name + "half", [P, SEQ_T])
        rstd = sb(name + "rstd", [P, TILES])
        xn = sb(name + "xn", [P, 4, DIM])
        ps = banks(name + "ps", 4)
        s_fetch = sem(name + "fetch")
        s_half = sem(name + "half")
        s_var = sem(name + "var")
        s_rstd = sem(name + "rstd")
        s_ch = sem(name + "ch")
        s_xn = sem(name + "xn")
        s_tr = sem(name + "tr")
        s_out = sem(name + "out")
        block = stack.enter_context(nc.Block())

        @block.sync
        def _(sp):
            sp.dma_start(*fetch).then_inc(s_fetch, 16)
            sp.wait_ge(s_fetch, 16)

        @block.vector
        def _(dve):
            ch = Chain(dve, s_ch)
            for b in range(BATCH):
                lo = b * SEQ_T
                norm_stats(dve, ch, [x_sb[:, lo + j, :] for j in range(SEQ_T)], stats[:, lo:lo + SEQ_T, :],
                           mv[:, lo:lo + SEQ_T, :], ve[:, lo:lo + SEQ_T]).then_inc(s_var, 1)
                dve.wait_ge(s_rstd, b + 1)
                for t in range(lo, lo + SEQ_T):
                    if t >= 4:
                        dve.wait_ge(s_tr, t - 3)
                    dve.tensor_scalar(xn[:, t % 4, :], x_sb[:, t, :], mv[:, t, 0:1], rstd[:, t:t + 1],
                                      ALU.subtract, ALU.mult).then_inc(s_xn, 1)

        @block.gpsimd
        def _(pool):
            pool.memset(half[:, :], -0.5).then_inc(s_half, 1)
            pool.wait_ge(s_half, 1)
            for b in range(BATCH):
                pool.wait_ge(s_var, b + 1)
                lo = b * SEQ_T
                pool.tensor_tensor(rstd[:, lo:lo + SEQ_T], ve[:, lo:lo + SEQ_T], half[:, :], ALU.pow)\
                    .then_inc(s_rstd, 1)

        @block.tensor
        def _(pe):
            for t in range(TILES):
                pe.wait_ge(s_xn, t + 1)
                if t >= 4:
                    pe.wait_ge(s_out, t - 3)
                for k in range(KT):
                    tr = pe.transpose(ps[t % 4][:, k * P:(k + 1) * P], xn[:, t % 4, k * P:(k + 1) * P], ident[:, :])
                tr.then_inc(s_tr, 1)

        @block.scalar
        def _(act):
            for t in range(TILES):
                act.wait_ge(s_tr, t + 1)
                act.activation(xT[:, :, t * P:(t + 1) * P], ps[t % 4][:, :].rearrange("p (k c) -> p k c", k=KT),
                               ACT.Copy).then_inc(s_out, 1)


def phase_attention(nc, a, x_sb, xT, kvT, kv, ident, g):
    with ExitStack() as stack:
        sb, banks, sem = scoped(nc, stack)
        rot = sb("rot", [P, 2 * QT, SEQ])
        wq = sb("wq", [P, KT, HK])
        wc_raw = sb("wc_raw", [P, 4 * P])
        w2_raw = sb("w2_raw", [P, DIM])
        wc = sb("wc", [P, 2, 4 * P], F32R)
        w1 = sb("w1", [P, D_CQ])
        w2 = sb("w2", [P, 2, DIM], F32R)
        qT = sb("qT", [P, 2, SEQ], F32R)
        prod = sb("prod", [P, 6, SEQ])
        qrot = sb("qrot", [P, QT, SEQ])
        qp = sb("qp", [P, 2, SEQ], F32R)
        attn = sb("attn", [P, 2, SEQ_T, SEQ])
        attnT = sb("attnT", [P, SEQ_T, SEQ])
        ctx = sb("ctx", [P, 2, SEQ], F32R)
        nmax = sb("nmax", [P, 2, SEQ_T])
        esum = sb("esum", [P, 2, SEQ_T])
        rsum = sb("rsum", [P, 2, SEQ_T])
        aff = sb("affin", [P, SEQ])
        left = sb("left", [P, SEQ])
        tanh = sb("tanh", [P, SEQ])
        kept = sb("kept", [P, SEQ])
        top8 = sb("top8", [P, 8])
        idx = sb("idx", [P, LUT_CHUNK], I32)
        pick = sb("pick", [P, PICKS, LUT_CHUNK])
        wsum = sb("wsum", [P, LUT_CHUNK])

        ps_q, = banks("ps_q", 1)
        ps_r = banks("ps_r", 2)
        ps_s = banks("ps_s", 2)
        ps_t = banks("ps_t", 3)
        out_bank = (ps_t[2], ps_t[0], ps_t[1], ps_q)

        names = """rot_in
            wq_in wc_in w1_in w2_in aff_in idx_in
            q_full ab_full cc_full qp_full s_full t_full ctx_full o_full
            q_evac qp_evac exp_done t_evac ctx_evac tanh_done
            max_done a_mul b_mul cc_mul c_add o_add recip topk kept_made picked
            ab_add pick_added aff_out w_out
            wc_hi wc_lo w2_hi w2_lo q_lo qp_lo ctx_lo""".split()
        s = {n: sem("a_" + n) for n in names}
        block = stack.enter_context(nc.Block())
        TOPK_OPS = 2 * ROUNDS + 2
        SHARES = (((0, 0), (0, 6)), ((0, 1), (6, 10)), ((1, 2), (10, 11))), \
                 (((2, 4), (11, 15)), ((4, 7), (15, 19)), ((7, 7), (19, 21))), \
                 (((7, 9), (21, 25)), ((9, 12), (25, 29)), ((12, 12), (29, 31))), \
                 (((12, 14), (31, 35)), ((14, 16), (35, 39)), ((16, 16), (39, 2 * ROUNDS + 3)))

        def loop(eng, body):
            body(0)
            with eng.Fori(1, HEADS - 1) as i:
                body(i)
            body(HEADS - 1)

        @block.sync
        def _(sp):
            def load(dst, src, h, what):
                sp.dma_start(dst, src[bass.ds(h, 1), :, :].rearrange("o p n -> p (o n)"))\
                    .then_inc(s[what], 16)

            wq_f = wq[:, :, :].rearrange("p k n -> p (k n)")

            def weights(h):
                need(sp, s["q_full"], h * 4)
                load(wq_f, a["wq"], h, "wq_in")
                need(sp, s["wc_hi"], h)
                need(sp, s["wc_lo"], h)
                load(wc_raw[:, :], a["wc"], h, "wc_in")
                if isinstance(h, int) and h == 0:
                    sp.dma_start(rot[:, :, :], a["rot"]).then_inc(s["rot_in"], 16)
                need(sp, s["w2_hi"], h)
                need(sp, s["w2_lo"], h)
                load(w2_raw[:, :], a["w2"], h, "w2_in")
                need(sp, s["qp_full"], h * 4)
                load(w1[:, :], a["w1"], h, "w1_in")
                need(sp, s["picked"], h * LUT)
                load(idx[:, :], a["idx"], h, "idx_in")
                need(sp, s["kept_made"], h)
                need(sp, s["tanh_done"], h)
                load(aff[:, :], a["aff"], h, "aff_in")

            def body(h):
                weights(h)

            loop(sp, body)

        @block.gpsimd
        def _(pool):
            def ab_add(u):
                pool.wait_ge(s["b_mul"], u + 1)
                need(pool, s["qp_full"], u)
                for t in range(2):
                    pool.tensor_tensor(qrot[:, t, :], prod[:, 2 * t, :], prod[:, 2 * t + 1, :], ALU.add)\
                        .then_inc(s["ab_add"], 1)

            def c_add(u):
                pool.wait_ge(s["cc_mul"], u + 1)
                pool.tensor_tensor(qrot[:, 2, :], prod[:, 4, :], prod[:, 5, :], ALU.add).then_inc(s["c_add"], 1)

            def pick_add(h, k):
                pool.wait_ge(s["picked"], h * LUT + k + 1)
                if k == 0:
                    need(pool, s["w_out"], h * 16)
                    stand(pool)
                    pool.tensor_copy(wsum[:, :], pick[:, 0, :]).then_inc(s["pick_added"], 1)
                else:
                    pool.wait_ge(s["pick_added"], h * LUT + k)
                    pool.tensor_tensor(wsum[:, :], wsum[:, :], pick[:, k % PICKS, :], ALU.add)\
                        .then_inc(s["pick_added"], 1)

            def low_part(w, raw, name, h):
                pool.wait_ge(s[name + "_in"], h * 16 + 16)
                pool.wait_ge(s[name + "_hi"], h + 1)
                pool.tensor_tensor(w[:, 1, :], raw[:, :], w[:, 0, :], ALU.subtract).then_inc(s[name + "_lo"], 1)

            low_part(wc, wc_raw, "wc", 0)
            ab_add(0)
            c_add(0)

            def body(h):
                for b in range(BATCH):
                    u = h * 4 + b
                    if b == 1:
                        low_part(w2, w2_raw, "w2", h)
                    if b == 3 and not (isinstance(h, int) and h == HEADS - 1):
                        low_part(wc, wc_raw, "wc", h + 1)
                    (k0, _), (_, k1) = SHARES[b][0][0], SHARES[b][2][0]
                    for k in range(k0, min(k1, k0 + 4)):
                        pick_add(h, k)
                    if not (isinstance(h, int) and u == UNITS - 1):
                        ab_add(u + 1)
                        c_add(u + 1)
                    for k in range(k0 + 4, k1):
                        pick_add(h, k)

            loop(pool, body)

        @block.scalar
        def _(act):
            def evac_q(u):
                act.wait_ge(s["q_full"], u + 1)
                need(act, s["cc_full"], u * 2)
                act.activation(qT[:, 0, :], ps_q[:, :], ACT.Copy).then_inc(s["q_evac"], 1)

            def evac_qp(u):
                act.wait_ge(s["qp_full"], u + 1)
                act.activation(qp[:, 0, :], ps_q[:, :], ACT.Copy).then_inc(s["qp_evac"], 1)

            def exps(u, b, js):
                for j in js:
                    act.wait_ge(s["max_done"], u * 4 + j + 1)
                    if j == 0:
                        need(act, s["t_full"], u * 4 - 4)
                    act.activation(attn[:, b % 2, j, :], ps_s[j % 2][:, :], ACT.Exp, bias=nmax[:, b % 2, j:j + 1],
                                   accum_out=esum[:, b % 2, j:j + 1]).then_inc(s["exp_done"], 1)

            def evac_back(u):
                for j in range(SEQ_T):
                    act.wait_ge(s["t_full"], u * 4 + j + 1)
                    if j == 0:
                        need(act, s["ctx_full"], u)
                    act.activation(attnT[:, :, j * P:(j + 1) * P],
                                   ps_t[j % 3][:, :].rearrange("p (l c) -> p l c", l=SEQ_T), ACT.Copy)\
                        .then_inc(s["t_evac"], 1)

            def evac_ctx(u):
                act.wait_ge(s["ctx_full"], u + 1)
                need(act, s["o_full"], u * 4)
                act.activation(ctx[:, 0, :], ps_t[1][:, :], ACT.Copy).then_inc(s["ctx_evac"], 1)

            def store(h):
                act.wait_ge(s["kept_made"], h + 1)
                act.dma_start(a["kept"][bass.ds(h, 1), :, :].rearrange("o p n -> p (o n)"), kept[:, :])\
                    .then_inc(s["aff_out"], 16)
                act.wait_ge(s["pick_added"], h * LUT + LUT)
                act.dma_start(a["lutw"][bass.ds(h, 1), :, :].rearrange("o p n -> p (o n)"), wsum[:, :])\
                    .then_inc(s["w_out"], 16)

            def high_part(w, raw, name, h, last_read, n):
                act.wait_ge(s[name + "_in"], h * 16 + 16)
                need(act, s[last_read], n)
                act.activation(w[:, 0, :], raw[:, :], ACT.Copy).then_inc(s[name + "_hi"], 1)

            high_part(wc, wc_raw, "wc", 0, "cc_full", 0)
            evac_q(0)

            def body(h):
                for b in range(BATCH):
                    u = h * 4 + b
                    first = isinstance(h, int) and u == 0
                    last = isinstance(h, int) and u == UNITS - 1
                    if b == 1:
                        high_part(w2, w2_raw, "w2", h, "o_full", h * 16)
                    if b == 3 and not last:
                        high_part(wc, wc_raw, "wc", h + 1, "cc_full", h * 8 + 8)
                    if not first:
                        evac_back(u - 1)
                    evac_qp(u)
                    if not first:
                        evac_ctx(u - 1)
                    exps(u, b, (0, 1))
                    if not last:
                        evac_q(u + 1)
                    exps(u, b, (2, 3))
                    if b == 1:
                        act.wait_ge(s["aff_in"], h * 16 + 16)
                        need(act, s["kept_made"], h)
                        act.activation(tanh[:, :], aff[:, :], ACT.Tanh, scale=0.5 * AFF_SCALE)\
                            .then_inc(s["tanh_done"], 1)
                    if b == 3:
                        store(h)

            loop(act, body)
            evac_back(UNITS - 1)
            evac_ctx(UNITS - 1)
            act.wait_ge(s["aff_out"], 16 * HEADS)
            act.wait_ge(s["w_out"], 16 * HEADS)

        @block.tensor
        def _(pe):
            def q_heads(u, b, h):
                if b == 0:
                    pe.wait_ge(s["wq_in"], h * 16 + 16)
                need(pe, s["qp_evac"], u)
                for k in range(KT):
                    mm = pe.matmul(ps_q[:, :], wq[:, k, :], xT[:, k, b * SEQ:(b + 1) * SEQ],
                                   start=(k == 0), stop=(k == KT - 1))
                mm.then_inc(s["q_full"], 1)

            def latent(u, b, h, which):
                if which == 0:
                    if b == 0:
                        pe.wait_ge(s["wc_hi"], h + 1)
                        pe.wait_ge(s["wc_lo"], h + 1)
                    pe.wait_ge(s["q_evac"], u + 1)
                    need(pe, s["cc_mul"], u)
                for r in range(2):
                    if which == 1:
                        pe.wait_ge(s["a_mul" if r == 0 else "b_mul"], u + 1)
                    c = (2 * which + r) * P
                    low = (lambda: pe.wait_ge(s["q_lo"], u + 1)) if which == 0 and r == 0 else None
                    mm = split_product(pe, ps_r[r][:, :], (wc[:, 0, c:c + P], wc[:, 1, c:c + P]),
                                       (qT[:, 0, :], qT[:, 1, :]), True, True, low)
                    mm.then_inc(s["ab_full" if which == 0 else "cc_full"], 1)

            def query(u, b, h):
                if b == 0:
                    pe.wait_ge(s["w1_in"], h * 16 + 16)
                need(pe, s["o_add"], u * 4 - 4)
                for t in range(QT):
                    if t < 2:
                        pe.wait_ge(s["ab_add"], u * 2 + t + 1)
                    else:
                        pe.wait_ge(s["c_add"], u + 1)
                    mm = pe.matmul(ps_q[:, :], w1[:, t * P:(t + 1) * P], qrot[:, t, :],
                                   start=(t == 0), stop=(t == QT - 1))
                mm.then_inc(s["qp_full"], 1)

            def scores(u, b, j):
                if j == 0:
                    pe.wait_ge(s["qp_lo"], u + 1)
                need(pe, s["exp_done"], u * 4 + j - 1)
                q, k = slice(j * P, (j + 1) * P), slice(b * SEQ, (b + 1) * SEQ)
                split_product(pe, ps_s[j % 2][:, :], (qp[:, 0, q], qp[:, 1, q]), (kvT[:, 0, k], kvT[:, 1, k]),
                              True, True).then_inc(s["s_full"], 1)

            def turn(u, b, j):
                pe.wait_ge(s["exp_done"], u * 4 + j + 1)
                if j < 3:
                    need(pe, s["o_add"], u * 4 - 4 + (2, 3, 1)[j])
                else:
                    pe.wait_ge(s["t_evac"], u * 4 + 1)
                for l in range(SEQ_T):
                    tr = pe.transpose(ps_t[j % 3][:, l * P:(l + 1) * P], attn[:, b % 2, j, l * P:(l + 1) * P],
                                      ident[:, :])
                tr.then_inc(s["t_full"], 1)

            def context(u, b):
                pe.wait_ge(s["t_evac"], u * 4 + 4)
                for l in range(SEQ_T):
                    mm = pe.matmul(ps_t[1][:, :], kv[:, b * SEQ_T + l, :], attnT[:, l, :],
                                   start=(l == 0), stop=(l == SEQ_T - 1))
                mm.then_inc(s["ctx_full"], 1)

            def output(u, b, h, j):
                if j == 0:
                    if b == 0:
                        pe.wait_ge(s["w2_hi"], h + 1)
                        pe.wait_ge(s["w2_lo"], h + 1)
                    pe.wait_ge(s["ctx_lo"], u + 1)
                q = slice(j * P, (j + 1) * P)
                split_product(pe, out_bank[j][:, :], (ctx[:, 0, q], ctx[:, 1, q]), (w2[:, 0, :], w2[:, 1, :]),
                              True, True)\
                    .then_inc(s["o_full"], 1)

            q_heads(0, 0, 0)
            latent(0, 0, 0, 0)
            latent(0, 0, 0, 1)

            def body(h):
                for b in range(BATCH):
                    u = h * 4 + b
                    first = isinstance(h, int) and u == 0
                    last = isinstance(h, int) and u == UNITS - 1
                    pb, ph = (b - 1) % 4, h if b else h - 1
                    nb, nh = (b + 1) % 4, h if b < 3 else h + 1
                    if not first:
                        for j in range(SEQ_T):
                            turn(u - 1, pb, j)
                    query(u, b, h)
                    if not first:
                        context(u - 1, pb)
                    scores(u, b, 0)
                    scores(u, b, 1)
                    if not last:
                        q_heads(u + 1, nb, nh)
                    scores(u, b, 2)
                    if not first:
                        output(u - 1, pb, ph, 0)
                    if not last:
                        latent(u + 1, nb, nh, 0)
                    scores(u, b, 3)
                    if not first:
                        output(u - 1, pb, ph, 1)
                        output(u - 1, pb, ph, 2)
                    if not last:
                        latent(u + 1, nb, nh, 1)
                    if not first:
                        output(u - 1, pb, ph, 3)

            loop(pe, body)
            for j in range(SEQ_T):
                turn(UNITS - 1, 3, j)
            context(UNITS - 1, 3)
            for j in range(SEQ_T):
                output(UNITS - 1, 3, HEADS - 1, j)

        @block.vector
        def _(dve):
            def rope_ab(u, r):
                dve.wait_ge(s["ab_full"], u * 2 + r + 1)
                need(dve, s["ab_add"], u * 2)
                for t, tab in (((0, 0), (3, QT + 1)), ((1, QT), (2, 1)))[r]:
                    ins = dve.tensor_tensor(prod[:, t, :], ps_r[r][:, :], rot[:, tab, :], ALU.mult)
                ins.then_inc(s["a_mul" if r == 0 else "b_mul"], 1)

            def rope_c(u):
                need(dve, s["c_add"], u)
                for t in range(2):
                    dve.wait_ge(s["cc_full"], u * 2 + t + 1)
                    ins = dve.tensor_tensor(prod[:, 4 + t, :], ps_r[t][:, :], rot[:, 2 + QT * t, :], ALU.mult)
                ins.then_inc(s["cc_mul"], 1)

            def maxes(u, b, js):
                for j in js:
                    dve.wait_ge(s["s_full"], u * 4 + j + 1)
                    dve.tensor_reduce(nmax[:, b % 2, j:j + 1], ps_s[j % 2][:, :], AX, ALU.max, negate=True)\
                        .then_inc(s["max_done"], 1)

            def add_out(u, b, js):
                dve.wait_ge(s["recip"], u + 1)
                for j in js:
                    dve.wait_ge(s["o_full"], u * 4 + j + 1)
                    need(dve, s["o_add"], u * 4 - 12 + j)
                    xt = x_sb[:, b * SEQ_T + j, :]
                    dve.scalar_tensor_tensor(xt, out_bank[j][:, :], rsum[:, b % 2, j:j + 1], xt, ALU.mult, ALU.add)\
                        .then_inc(s["o_add"], 1)

            def sums(u, b):
                dve.wait_ge(s["exp_done"], u * 4 + 4)
                dve.reciprocal(rsum[:, b % 2, :], esum[:, b % 2, :]).then_inc(s["recip"], 1)

            def topk(h, n):
                base = h * TOPK_OPS
                src = aff if n < 2 else left
                if n == 0:
                    dve.wait_ge(s["aff_in"], h * 16 + 16)
                    need(dve, s["kept_made"], h)
                if n < 2 * ROUNDS + 2:
                    need(dve, s["topk"], base + n)
                if n <= 2 * ROUNDS:
                    stand(dve)
                if n <= 2 * ROUNDS and n % 2 == 0:
                    dve.max(top8[:, :], src[:, :]).then_inc(s["topk"], 1)
                elif n < 2 * ROUNDS:
                    dve.match_replace(left[:, :], top8[:, :], src[:, :], LOWEST).then_inc(s["topk"], 1)
                elif n == 2 * ROUNDS + 1:
                    k = TOP - 8 * ROUNDS - 1
                    dve.tensor_scalar(left[:, :], aff[:, :], top8[:, k:k + 1], None, ALU.is_ge)\
                        .then_inc(s["topk"], 1)
                else:
                    dve.wait_ge(s["topk"], base + TOPK_OPS)
                    dve.wait_ge(s["tanh_done"], h + 1)
                    need(dve, s["aff_out"], h * 16)
                    dve.scalar_tensor_tensor(kept[:, :], tanh[:, :], 1.0, left[:, :], ALU.add, ALU.mult)\
                        .then_inc(s["kept_made"], 1)

            def pick_entry(h, k):
                if k == 0:
                    dve.wait_ge(s["idx_in"], h * 16 + 16)
                need(dve, s["pick_added"], h * LUT + k + 1 - PICKS)
                dve.tensor_scalar(pick[:, k % PICKS, :], idx[:, :], float(k), g["lut"][:, k:k + 1], ALU.is_equal,
                                  ALU.mult).then_inc(s["picked"], 1)

            def background(h, share):
                (k, k_end), (n, n_end) = share
                while k < k_end or n < n_end:
                    if n < n_end:
                        topk(h, n)
                        n += 1
                    if k < k_end:
                        pick_entry(h, k)
                        k += 1

            def low_part(pair, ps, name, u):
                dve.wait_ge(s[name + "_evac"], u + 1)
                dve.tensor_tensor(pair[:, 1, :], ps[:, :], pair[:, 0, :], ALU.subtract).then_inc(s[name + "_lo"], 1)

            low_part(qT, ps_q, "q", 0)
            dve.wait_ge(s["rot_in"], 16)
            rope_ab(0, 0)
            rope_ab(0, 1)
            rope_c(0)

            def body(h):
                for b in range(BATCH):
                    u = h * 4 + b
                    first = isinstance(h, int) and u == 0
                    last = isinstance(h, int) and u == UNITS - 1
                    background(h, SHARES[b][0])
                    low_part(qp, ps_q, "qp", u)
                    background(h, SHARES[b][1])
                    if not first:
                        low_part(ctx, ps_t[1], "ctx", u - 1)
                    maxes(u, b, (0, 1))
                    background(h, SHARES[b][2])
                    if not last:
                        low_part(qT, ps_q, "q", u + 1)
                    maxes(u, b, (2,))
                    if not last:
                        rope_ab(u + 1, 0)
                    maxes(u, b, (3,))
                    if not last:
                        rope_ab(u + 1, 1)
                    sums(u, b)
                    if not first:
                        add_out(u - 1, (b - 1) % 4, (0, 1, 2))
                    if not last:
                        rope_c(u + 1)
                    if not first:
                        add_out(u - 1, (b - 1) % 4, (3,))

            loop(dve, body)
            low_part(ctx, ps_t[1], "ctx", UNITS - 1)
            add_out(UNITS - 1, 3, range(4))


def phase_swiglu(nc, x_sb, xT, lw, g):
    with ExitStack() as stack:
        sb, banks, sem = scoped(nc, stack)
        w_gate = lw[:, 0:GU_W].rearrange("p (k f) -> p k f", k=KT)
        w_up = lw[:, GU_W:2 * GU_W].rearrange("p (k f) -> p k f", k=KT)
        w_down = lw[:, 2 * GU_W:LUT_W].rearrange("p (f n) -> p f n", f=FT)
        th = sb("th", [P, 2, SEQ])
        u = sb("u", [P, 2, SEQ])
        hT = sb("hT", [P, FT, SEQ])
        ps_g = banks("ps_g", 2)
        ps_u = banks("ps_u", 2)
        ps_o = banks("ps_o", 4)
        s = {n: sem("f_" + n) for n in "g_full u_full tanh_done u_made h_made o_full o_add".split()}
        block = stack.enter_context(nc.Block())

        def width(f):
            return P if f < FT - 1 else F_LAST

        @block.tensor
        def _(pe):
            with pe.Fori(0, BATCH) as b:
                for f in range(FT):
                    n = b * FT + f
                    M = width(f)
                    for w, ps, full in ((w_gate, ps_g, "g_full"), (w_up, ps_u, "u_full")):
                        if f >= 2:
                            pe.wait_ge(s["h_made"], n - 1)
                        else:
                            pe.wait_ge(s["h_made"], b * FT)
                        for k in range(KT):
                            mm = pe.matmul(ps[f % 2][0:M, :], w[:, k, f * P:f * P + M],
                                           xT[:, k, bass.ds(b * SEQ, SEQ)], start=(k == 0), stop=(k == KT - 1))
                        mm.then_inc(s[full], 1)
                pe.wait_ge(s["h_made"], b * FT + FT)
                for j in range(SEQ_T):
                    pe.wait_ge(s["o_add"], b * SEQ_T)
                    for f in range(FT):
                        M = width(f)
                        mm = pe.matmul(ps_o[j][:, :], hT[0:M, f, j * P:(j + 1) * P], w_down[0:M, f, :],
                                       start=(f == 0), stop=(f == FT - 1))
                    mm.then_inc(s["o_full"], 1)

        @block.scalar
        def _(act):
            with act.Fori(0, BATCH) as b:
                for f in range(FT):
                    n = b * FT + f
                    M = width(f)
                    act.wait_ge(s["g_full"], n + 1)
                    if f >= 2:
                        act.wait_ge(s["u_made"], n - 1)
                    else:
                        act.wait_ge(s["u_made"], b * FT)
                    act.activation(th[0:M, f % 2, :], ps_g[f % 2][0:M, :], ACT.Tanh, scale=0.5)\
                        .then_inc(s["tanh_done"], 1)

        @block.vector
        def _(dve):
            with dve.Fori(0, BATCH) as b:
                dve.wait_ge(s["o_full"], b * SEQ_T)
                for f in range(FT):
                    n = b * FT + f
                    M = width(f)
                    dve.wait_ge(s["tanh_done"], n + 1)
                    dve.wait_ge(s["h_made"], n - 1 if f >= 2 else b * FT)
                    dve.scalar_tensor_tensor(u[0:M, f % 2, :], th[0:M, f % 2, :], 1.0, ps_g[f % 2][0:M, :],
                                             ALU.add, ALU.mult).then_inc(s["u_made"], 1)
                    dve.wait_ge(s["u_full"], n + 1)
                    dve.wait_ge(s["u_made"], n + 1)
                    dve.scalar_tensor_tensor(hT[0:M, f, :], u[0:M, f % 2, :], 0.5, ps_u[f % 2][0:M, :],
                                             ALU.mult, ALU.mult).then_inc(s["h_made"], 1)
                for j in range(SEQ_T):
                    dve.wait_ge(s["o_full"], b * SEQ_T + j + 1)
                    xt = x_sb[:, bass.ds(b * SEQ_T + j, 1), :].rearrange("p o d -> p (o d)")
                    dve.scalar_tensor_tensor(xt, ps_o[j][:, :], g["th"][:, 2:3], xt, ALU.mult, ALU.add)\
                        .then_inc(s["o_add"], 1)


def phase_mix_route(nc, a, x_sb, ident, g, r):
    with ExitStack() as stack:
        sb, banks, sem = scoped(nc, stack)
        kept = sb("kept_m", [P, 2, SEQ_T, SEQ])
        stats = sb("stats", [P, SEQ_T, 6])
        mv = sb("mv", [P, SEQ_T, 2])
        ve = sb("ve", [P, SEQ_T])
        half = sb("half", [P, SEQ_T])
        rstd = sb("rstd", [P, SEQ_T])
        scl = sb("scl", [P, SEQ_T])
        shift = sb("shift", [P, SEQ_T])
        xn = sb("xn", [P, SEQ_T, DIM])
        xnT = sb("xnT", [P, SEQ_T, DIM])
        gw = sb("gw", [P, KT, EXPERTS])
        logit = sb("logit", [P, SEQ_T, EXPERTS])
        rest = sb("rest", [P, SEQ_T, EXPERTS])
        top8 = sb("rtop8", [P, SEQ_T, 8])
        nmax = sb("rnmax", [P, SEQ_T])
        prob = sb("prob", [P, SEQ_T, EXPERTS])
        psum_e = sb("psum_e", [P, SEQ_T])
        rden = sb("rden", [P, SEQ_T])
        sel = sb("sel", [P, SEQ_T, EXPERTS])
        selb = sb("selb", [P, SEQ_T, EXPERTS], BF16)
        valid = sb("valid", [P, SEQ_T, EXPERTS])
        taken = sb("taken", [P, EXPERTS])
        takenb = sb("takenb", [P, EXPERTS], BF16)
        count = sb("count", [P, EXPERTS])
        posp = sb("posp", [P, SEQ_T, EXPERTS])
        w = sb("rw", [P, SEQ_T, EXPERTS])
        before = sb("before", [P, P], BF16)
        ones = sb("ones", [P, P], BF16)
        zeros = sb("zeros", [P, DIM])
        ps_a = banks("ps_a", 2)
        ps_x = banks("ps_x", 4)
        ps_l, ps_p = banks("ps_l", 2)
        s_kept = [sem(f"m_kept{j}") for j in range(2)]
        s = {n: sem("m_" + n) for n in """gw_in const consts a_full a_used var rstd ch x_new xn_made xn_out acc_out xt_full
            xt_evac l_full nmax prob_done selb_made p_full stage moe_const zero_out""".split()}
        block = stack.enter_context(nc.Block())

        def x_tile(b, j):
            return x_sb[:, bass.ds(b * SEQ_T + j, 1), :].rearrange("p o d -> p (o d)")

        @block.sync
        def _(sp):
            sp.dma_start(gw[:, :, :], a["gw"]).then_inc(s["gw_in"], 16)
            with sp.Fori(0, BATCH // 2) as i:
                for j in range(2):
                    sp.wait_ge(s["x_new"], i * 2 * SEQ_T)
                    sp.dma_start(kept[:, j, :, :],
                                 a["kept"][bass.ds((i * 2 + j) * SEQ_T, SEQ_T), :, :].rearrange("i p n -> p i n"))\
                        .then_inc(s_kept[j], 16)
                for j in range(2):
                    b = i * 2 + j
                    sp.wait_ge(s["x_new"], b * SEQ_T + SEQ_T)
                    sp.dma_start(a["acc"][bass.ds(b * SEQ, SEQ), :].rearrange("(i p) d -> p i d", p=P),
                                 x_sb[:, bass.ds(b * SEQ_T, SEQ_T), :]).then_inc(s["acc_out"], 16)
                    sp.wait_ge(s["xn_made"], b * SEQ_T + SEQ_T)
                    sp.dma_start(a["xn"][bass.ds(b * SEQ, SEQ), :].rearrange("(i p) d -> p i d", p=P),
                                 xn[:, :, :]).then_inc(s["xn_out"], 16)
            sp.wait_ge(s["consts"], 5)
            for k in range(HALVES):
                sp.dma_start(a["acc"][T + k * P:T + (k + 1) * P, :], zeros[:, :]).then_inc(s["zero_out"], 16)
            sp.wait_ge(s["zero_out"], 16 * HALVES)
            sp.wait_ge(s["acc_out"], 16 * BATCH)
            sp.wait_ge(s["xn_out"], 16 * BATCH)

        @block.gpsimd
        def _(pool):
            pool.memset(half[:, :], -0.5).then_inc(s["consts"], 1)
            pool.memset(zeros[:, :], 0.0).then_inc(s["consts"], 1)
            pool.memset(ones[:, :], 1.0).then_inc(s["consts"], 1)
            pool.memset(takenb[:, :], 0.0).then_inc(s["consts"], 1)
            pool.memset(taken[:, :], 0.0).then_inc(s["consts"], 1)
            pool.wait_ge(s["consts"], 5)
            pool.affine_select(out=before[:, :], in_=ones[:, :], compare_op=ALU.is_gt, fill=0.0, base=0,
                               pattern=[[1, P]], channel_multiplier=-1).then_inc(s["consts"], 1)
            with pool.Fori(0, BATCH) as b:
                for n in range(2):
                    pool.wait_ge(s["var"], b * 2 + n + 1)
                    pool.tensor_tensor(rstd[:, :], ve[:, :], half[:, :], ALU.pow).then_inc(s["rstd"], 1)

        @block.tensor
        def _(pe):
            pe.wait_ge(s["gw_in"], 16)
            pe.wait_ge(s["consts"], 6)
            with pe.Fori(0, BATCH // 2) as i:
                for slot in range(2):
                    b = i * 2 + slot
                    pe.wait_ge(s_kept[slot], i * 16 + 16)
                    for j in range(SEQ_T):
                        if j < 2:
                            pe.wait_ge(s["a_used"], b * SEQ_T)
                        else:
                            pe.wait_ge(s["a_used"], b * SEQ_T + j - 1)
                        for k in range(SEQ_T):
                            tr = pe.transpose(ps_a[j % 2][:, k * P:(k + 1) * P], kept[:, slot, k, j * P:(j + 1) * P],
                                              ident[:, :])
                        tr.then_inc(s["a_full"], 1)
                    for j in range(SEQ_T):
                        pe.wait_ge(s["xn_made"], b * SEQ_T + j + 1)
                        pe.wait_ge(s["xt_evac"], b * SEQ_T)
                        for k in range(KT):
                            tr = pe.transpose(ps_x[j][:, k * P:(k + 1) * P], xn[:, j, k * P:(k + 1) * P], ident[:, :])
                        tr.then_inc(s["xt_full"], 1)
                    for j in range(SEQ_T):
                        pe.wait_ge(s["xt_evac"], b * SEQ_T + j + 1)
                        for k in range(KT):
                            mm = pe.matmul(ps_l[:, j * EXPERTS:(j + 1) * EXPERTS], xnT[:, j, k * P:(k + 1) * P],
                                           gw[:, k, :], start=(k == 0), stop=(k == KT - 1))
                        mm.then_inc(s["l_full"], 1)
                    pe.wait_ge(s["selb_made"], b + 1)
                    for j in range(SEQ_T):
                        out = ps_p[:, j * EXPERTS:(j + 1) * EXPERTS]
                        pe.matmul(out, before[:, :], selb[:, j, :], start=True, stop=False)
                        for k in range(j):
                            pe.matmul(out, ones[:, :], selb[:, k, :], start=False, stop=False)
                        mm = pe.matmul(out, ones[:, :], takenb[:, :], start=False, stop=True)
                    mm.then_inc(s["p_full"], 1)

        @block.scalar
        def _(act):
            with act.Fori(0, BATCH) as b:
                for j in range(SEQ_T):
                    act.wait_ge(s["xt_full"], b * SEQ_T + j + 1)
                    act.activation(xnT[:, j, :], ps_x[j][:, :], ACT.Copy).then_inc(s["xt_evac"], 1)
                for j in range(SEQ_T):
                    act.wait_ge(s["nmax"], b + 1)
                    act.activation(prob[:, j, :], logit[:, j, :], ACT.Exp, bias=nmax[:, j:j + 1],
                                   accum_out=psum_e[:, j:j + 1]).then_inc(s["prob_done"], 1)

        @block.vector
        def _(dve):
            PER = 50
            with dve.Fori(0, BATCH // 2) as i:
                for slot in range(2):
                    b = i * 2 + slot
                    ch = Chain(dve, s["ch"], b * PER)
                    tiles = [x_tile(b, j) for j in range(SEQ_T)]
                    norm_stats(dve, ch, tiles, stats, mv, ve).then_inc(s["var"], 1)
                    dve.wait_ge(s["rstd"], b * 2 + 1)
                    ch.link(dve.tensor_scalar(shift[:, :], rstd[:, :], g["mix"][:, 0:1], None, ALU.mult))
                    ch.link(dve.tensor_scalar(scl[:, :], shift[:, :], 1.0, None, ALU.add))
                    ch.link(dve.scalar_tensor_tensor(shift[:, :], shift[:, :], -1.0, mv[:, :, 0], ALU.mult, ALU.mult))
                    for j in range(SEQ_T):
                        ch.add(dve.tensor_scalar(tiles[j], tiles[j], scl[:, j:j + 1], shift[:, j:j + 1],
                                                 ALU.mult, ALU.add))
                    ch.now()
                    for j in range(SEQ_T):
                        dve.wait_ge(s["a_full"], b * SEQ_T + j + 1)
                        dve.scalar_tensor_tensor(tiles[j], ps_a[j % 2][:, :], g["mix"][:, 1:2], tiles[j],
                                                 ALU.mult, ALU.add).then_inc(s["a_used"], 1)
                    for j in range(SEQ_T):
                        dve.wait_ge(s["a_used"], b * SEQ_T + j + 1)
                        dve.scalar_tensor_tensor(tiles[j], kept[:, slot, j, :], g["mix"][:, 1:2], tiles[j],
                                                 ALU.mult, ALU.add).then_inc(s["x_new"], 1)
                    dve.wait_ge(s["x_new"], b * SEQ_T + SEQ_T)
                    stand(dve)
                    norm_stats(dve, ch, tiles, stats, mv, ve).then_inc(s["var"], 1)
                    dve.wait_ge(s["rstd"], b * 2 + 2)
                    dve.wait_ge(s["xn_out"], b * 16)
                    for j in range(SEQ_T):
                        dve.tensor_scalar(xn[:, j, :], tiles[j], mv[:, j, 0:1], rstd[:, j:j + 1],
                                          ALU.subtract, ALU.mult).then_inc(s["xn_made"], 1)
                    dve.wait_ge(s["l_full"], b * SEQ_T + SEQ_T)
                    ch.link(dve.tensor_copy(logit[:, :, :], ps_l[:, 0:SEQ_T * EXPERTS]
                                            .rearrange("p (j e) -> p j e", j=SEQ_T)))
                    stand(dve)
                    for j in range(SEQ_T):
                        ch.add(dve.max(top8[:, j, :], logit[:, j, :]))
                    ch.now()
                    dve.tensor_scalar(nmax[:, :], top8[:, :, 0], -1.0, None, ALU.mult).then_inc(s["nmax"], 1)
                    for j in range(SEQ_T):
                        ch.add(dve.match_replace(rest[:, j, :], top8[:, j, :], logit[:, j, :], LOWEST))
                    ch.now()
                    ch.link(dve.tensor_tensor(sel[:, :, :], rest[:, :, :], logit[:, :, :], ALU.not_equal))
                    dve.tensor_copy(selb[:, :, :], sel[:, :, :]).then_inc(s["selb_made"], 1)
                    dve.wait_ge(s["p_full"], b + 1)
                    places = ps_p[:, 0:SEQ_T * EXPERTS].rearrange("p (j e) -> p j e", j=SEQ_T)
                    ch.link(dve.scalar_tensor_tensor(valid[:, :, :], places, float(CAP), sel[:, :, :],
                                                     ALU.is_lt, ALU.mult))
                    ch.link(dve.scalar_tensor_tensor(posp[:, :, :], places, 1.0, valid[:, :, :], ALU.add, ALU.mult))
                    ch.add(dve.tensor_scalar(r["place"][:, bass.ds(b * SEQ_T, SEQ_T), :], posp[:, :, :], -1.0, None,
                                             ALU.add))
                    ch.link(dve.tensor_reduce(count[:, :], sel[:, :, :].rearrange("p j e -> p e j"), AX, ALU.add))
                    ch.link(dve.tensor_tensor(taken[:, :], taken[:, :], count[:, :], ALU.add))
                    ch.link(dve.tensor_copy(takenb[:, :], taken[:, :]))
                    dve.wait_ge(s["prob_done"], b * SEQ_T + SEQ_T)
                    ch.link(dve.reciprocal(rden[:, :], psum_e[:, :]))
                    ch.link(dve.tensor_scalar(rden[:, :], rden[:, :], g["th"][:, 3:4], None, ALU.mult))
                    for j in range(SEQ_T):
                        ch.add(dve.scalar_tensor_tensor(w[:, j, :], prob[:, j, :], rden[:, j:j + 1], valid[:, j, :],
                                                        ALU.mult, ALU.mult))
                    ch.now()
                    for part in range(3):
                        dst = r["parts"][:, bass.ds(b * SEQ_T, SEQ_T), part, :]
                        ch.link(dve.tensor_copy(dst, w[:, :, :]))
                        if part < 2:
                            ch.link(dve.tensor_tensor(w[:, :, :], w[:, :, :], dst, ALU.subtract))
                    assert ch.n == PER, ch.n


def phase_experts(nc, a, ident, g, r, out):
    with ExitStack() as stack:
        sb, banks, sem = scoped(nc, stack)
        GROUP = 4
        wg = sb("wg", [P, 2, KT, FE])
        wu = sb("wu", [P, 2, KT, FE])
        wd = sb("wd", [P, 2, FET, DIM])
        slots = sb("slots", [P, CAP])
        slotsb = sb("slotsb", [P, CAP], BF16)
        spare = sb("spare", [P, HALVES])
        cur = sb("cur", [P, 2, TILES])
        pick = sb("pick_e", [P, 2, TILES, CAP], BF16)
        vals = sb("vals", [P, 2, TILES, 6], BF16)
        table = sb("table", [P, HALVES, 6])
        wsum = sb("wsum_e", [P, HALVES])
        weight = sb("weight", [P, GROUP, HALVES])
        tokf = sb("tokf", [P, HALVES])
        empty = sb("empty", [P, HALVES])
        src_row = sb("src_row", [P, GROUP, HALVES], U32)
        dst_row = sb("dst_row", [P, GROUP, HALVES], U32)
        xg = sb("xg", [P, 2, HALVES, DIM])
        xgT = sb("xgT", [P, KT, CAP])
        th = sb("th_e", [P, FET * CAP])
        u = sb("u_e", [P, FET * CAP])
        hT = sb("hT_e", [P, FET, CAP])
        y = sb("y_e", [P, 2, HALVES, DIM])
        ps_tab, ps_g, ps_u = banks("ps_tgu", 3)
        ps_x = banks("ps_xg", 2)
        ps_y = banks("ps_y", 2)
        s_w = [sem(f"e_w{j}") for j in range(2)]
        s_gat = [sem(f"e_gat{j}") for j in range(2)]
        s = {n: sem("e_" + n) for n in """const slots cur_made pick_made tab_full tab_read ch tabled xt_full xt_evac
            gu_full tanh_done u_made h_made y_full y_evac scat out""".split()}
        block = stack.enter_context(nc.Block())

        def loop(eng, body):
            body(0)
            with eng.Fori(1, EXPERTS // GROUP - 1) as i:
                body(i)
            body(EXPERTS // GROUP - 1)

        def last_group(i):
            return isinstance(i, int) and i > 0

        def count2(i, q, ahead=0):
            return i * (GROUP // 2) + (q + ahead) // 2 + 1

        @block.sync
        def _(sp):
            def body(i):
                for q in range(GROUP):
                    e, k = i * GROUP + q, q % 2
                    need(sp, s["y_full"], e * 2 - 2)
                    one = bass.ds(e, 1)
                    sp.dma_start(wg[:, k, :, :], a["w_gate"][one, :, :].rearrange("o (k p) f -> p (o k) f", p=P))\
                        .then_inc(s_w[k], 16)
                    sp.dma_start(wu[:, k, :, :], a["w_up"][one, :, :].rearrange("o (k p) f -> p (o k) f", p=P))\
                        .then_inc(s_w[k], 16)
                    sp.dma_start(wd[:, k, :, :], a["w_down"][one, :, :].rearrange("o (k p) f -> p (o k) f", p=P))\
                        .then_inc(s_w[k], 16)

            loop(sp, body)
            sp.wait_ge(s["scat"], 32 * EXPERTS)
            sp.dma_start(out, a["acc"][0:T, :]).then_inc(s["out"], 16)
            sp.wait_ge(s["out"], 16)

        @block.gpsimd
        def _(pool):
            pool.iota(slots[:, :], pattern=[[1, CAP]], base=0, channel_multiplier=0,
                      allow_small_or_imprecise_dtypes=True).then_inc(s["const"], 1)
            pool.iota(spare[:, :], pattern=[[P, HALVES]], base=T, channel_multiplier=1,
                      allow_small_or_imprecise_dtypes=True).then_inc(s["const"], 1)
            for k in range(2):
                pool.iota(vals[:, k, :, 3], pattern=[[1, TILES]], base=0, channel_multiplier=0,
                          allow_small_or_imprecise_dtypes=True).then_inc(s["const"], 1)
                pool.iota(vals[:, k, :, 4], pattern=[[0, TILES]], base=0, channel_multiplier=1,
                          allow_small_or_imprecise_dtypes=True).then_inc(s["const"], 1)
                pool.memset(vals[:, k, :, 5], 1.0).then_inc(s["const"], 1)

            def gather(i, q, ahead):
                e = i * GROUP + q + ahead
                qq = (q + ahead) % GROUP
                pool.wait_ge(s["tabled"], e + 1)
                need(pool, s["xt_full"], e * 2 - 2)
                stand(pool)
                for n in range(HALVES):
                    pool.indirect_dma_start(xg[:, qq % 2, n, :], None, a["xn"][:, :],
                                            bass.IndirectOffsetOnAxis(ap=src_row[:, qq, n:n + 1], axis=0))\
                        .then_inc(s_gat[qq % 2], 16)

            def scatter(i, q, back):
                e = i * GROUP + q - back
                qq = (q - back) % GROUP
                pool.wait_ge(s["y_evac"], e * 2 + 2)
                need(pool, s["scat"], e * 32)
                stand(pool)
                for n in range(HALVES):
                    pool.indirect_dma_start(a["acc"][:, :], bass.IndirectOffsetOnAxis(ap=dst_row[:, qq, n:n + 1], axis=0),
                                            y[:, qq % 2, n, :], None, compute_op=ALU.add)\
                        .then_inc(s["scat"], 16)

            gather(0, 0, 0)
            gather(0, 1, 0)

            def body(i):
                for q in range(GROUP):
                    if not (isinstance(i, int) and i == 0 and q == 0):
                        scatter(i, q, 1)
                    if not (last_group(i) and q >= GROUP - 2):
                        gather(i, q, 2)

            loop(pool, body)
            scatter(EXPERTS // GROUP - 1, GROUP, 1)

        @block.tensor
        def _(pe):
            def tabulate(i, q, ahead):
                e, k = i * GROUP + q + ahead, (q + ahead) % 2
                pe.wait_ge(s["pick_made"], e + 1)
                need(pe, s["tab_read"], e)
                for n in range(HALVES):
                    for t in range(TILES):
                        mm = pe.matmul(ps_tab[:, n * 6:(n + 1) * 6], pick[:, k, t, n * P:(n + 1) * P],
                                       vals[:, k, t, :], start=(t == 0), stop=(t == TILES - 1))
                mm.then_inc(s["tab_full"], 1)

            def turn(i, q, ahead):
                e, k = i * GROUP + q + ahead, (q + ahead) % 2
                pe.wait_ge(s_gat[k], count2(i, q, ahead) * 32)
                for n in range(HALVES):
                    need(pe, s["xt_evac"], e * 2 - 1 + n)
                    for c in range(KT):
                        tr = pe.transpose(ps_x[n][:, c * P:(c + 1) * P], xg[:, k, n, c * P:(c + 1) * P], ident[:, :])
                    tr.then_inc(s["xt_full"], 1)

            def gate_up(i, q):
                e, k = i * GROUP + q, q % 2
                pe.wait_ge(s_w[k], count2(i, q) * 48)
                pe.wait_ge(s["xt_evac"], e * 2 + 2)
                need(pe, s["h_made"], e)
                for w, ps in ((wg, ps_g), (wu, ps_u)):
                    for f in range(FET):
                        for c in range(KT):
                            mm = pe.matmul(ps[:, f * CAP:(f + 1) * CAP], w[:, k, c, f * P:(f + 1) * P], xgT[:, c, :],
                                           start=(c == 0), stop=(c == KT - 1))
                    mm.then_inc(s["gu_full"], 1)

            def down(i, q):
                e, k = i * GROUP + q, q % 2
                pe.wait_ge(s["h_made"], e + 1)
                for n in range(HALVES):
                    need(pe, s["y_evac"], e * 2 - 1 + n)
                    for f in range(FET):
                        mm = pe.matmul(ps_y[n][:, :], hT[:, f, n * P:(n + 1) * P], wd[:, k, f, :],
                                       start=(f == 0), stop=(f == FET - 1))
                    mm.then_inc(s["y_full"], 1)

            tabulate(0, 0, 0)
            tabulate(0, 1, 0)
            turn(0, 0, 0)

            def body(i):
                for q in range(GROUP):
                    gate_up(i, q)
                    if not (last_group(i) and q >= GROUP - 2):
                        tabulate(i, q, 2)
                    if not (last_group(i) and q == GROUP - 1):
                        turn(i, q, 1)
                    down(i, q)

            loop(pe, body)

        @block.scalar
        def _(act):
            def evac_x(i, q, ahead):
                e = i * GROUP + q + ahead
                for n in range(HALVES):
                    act.wait_ge(s["xt_full"], e * 2 + n + 1)
                    act.activation(xgT[:, :, n * P:(n + 1) * P], ps_x[n][:, :].rearrange("p (k c) -> p k c", k=KT),
                                   ACT.Copy).then_inc(s["xt_evac"], 1)

            evac_x(0, 0, 0)

            def body(i):
                for q in range(GROUP):
                    e = i * GROUP + q
                    act.wait_ge(s["gu_full"], e * 2 + 1)
                    need(act, s["u_made"], e)
                    act.activation(th[:, :], ps_g[:, :], ACT.Tanh, scale=0.5).then_inc(s["tanh_done"], 1)
                    if not (last_group(i) and q == GROUP - 1):
                        evac_x(i, q, 1)
                    need(act, s["scat"], e * 32 - 32)
                    for n in range(HALVES):
                        act.wait_ge(s["y_full"], e * 2 + n + 1)
                        act.activation(y[:, q % 2, n, :], ps_y[n][:, :], ACT.Copy, scale=weight[:, q, n:n + 1])\
                            .then_inc(s["y_evac"], 1)

            loop(act, body)

        @block.vector
        def _(dve):
            def make_pick(i, q, ahead):
                e, k = i * GROUP + q + ahead, (q + ahead) % 2
                need(dve, s["tab_full"], e - 1)
                one = bass.ds(e, 1)
                dve.tensor_copy(cur[:, k, :], r["place"][:, :, one].rearrange("p t o -> p (t o)"))\
                    .then_inc(s["cur_made"], 1)
                dve.tensor_copy(vals[:, k, :, 0:3], r["parts"][:, :, :, one].rearrange("p t c o -> p t (c o)"))\
                    .then_inc(s["cur_made"], 1)
                dve.wait_ge(s["cur_made"], e * 2 + 2)
                for t in range(TILES):
                    ins = dve.tensor_scalar(pick[:, k, t, :], slotsb[:, :], cur[:, k, t:t + 1], None, ALU.is_equal)
                ins.then_inc(s["pick_made"], 1)

            PER = 5

            def make_table(i, q, ahead):
                e, qq = i * GROUP + q + ahead, (q + ahead) % GROUP
                dve.wait_ge(s["tab_full"], e + 1)
                need(dve, s["tabled"], e)
                dve.tensor_copy(table[:, :, :], ps_tab[:, 0:HALVES * 6].rearrange("p (n c) -> p n c", n=HALVES))\
                    .then_inc(s["tab_read"], 1)
                dve.wait_ge(s["tab_read"], e + 1)
                need(dve, s["scat"], e * 32 - 96)
                ch = Chain(dve, s["ch"], e * PER)
                ch.add(dve.tensor_tensor(wsum[:, :], table[:, :, 2], table[:, :, 1], ALU.add))
                ch.add(dve.scalar_tensor_tensor(tokf[:, :], table[:, :, 3], float(P), table[:, :, 4],
                                                ALU.mult, ALU.add))
                ch.link(dve.tensor_tensor(empty[:, :], table[:, :, 5], spare[:, :], ALU.mult))
                ch.add(dve.tensor_tensor(weight[:, qq, :], wsum[:, :], table[:, :, 0], ALU.add))
                ch.link(dve.tensor_tensor(empty[:, :], spare[:, :], empty[:, :], ALU.subtract))
                dve.tensor_copy(src_row[:, qq, :], tokf[:, :])
                dve.tensor_tensor(dst_row[:, qq, :], tokf[:, :], empty[:, :], ALU.add).then_inc(s["tabled"], 1)
                assert ch.n == PER

            dve.wait_ge(s["const"], 8)
            dve.tensor_copy(slotsb[:, :], slots[:, :]).then_inc(s["slots"], 1)
            dve.wait_ge(s["slots"], 1)
            make_pick(0, 0, 0)
            make_pick(0, 1, 0)
            make_table(0, 0, 0)
            make_pick(0, 2, 0)
            make_table(0, 1, 0)

            def body(i):
                for q in range(GROUP):
                    e = i * GROUP + q
                    dve.wait_ge(s["tanh_done"], e + 1)
                    dve.scalar_tensor_tensor(u[:, :], th[:, :], 1.0, ps_g[:, :], ALU.add, ALU.mult)\
                        .then_inc(s["u_made"], 1)
                    dve.wait_ge(s["gu_full"], e * 2 + 2)
                    dve.wait_ge(s["u_made"], e + 1)
                    dve.scalar_tensor_tensor(hT[:, :, :].rearrange("p f c -> p (f c)"), u[:, :], 0.5, ps_u[:, :],
                                             ALU.mult, ALU.mult).then_inc(s["h_made"], 1)
                    if not (last_group(i) and q >= GROUP - 2):
                        make_table(i, q, 2)
                    if not (last_group(i) and q >= GROUP - 3):
                        make_pick(i, q, 3)

            loop(dve, body)


def build(nc, a, out):
    with ExitStack() as stack:
        def sb(name, shape, dt=F32):
            return stack.enter_context(nc.sbuf_tensor(name, shape, dt))

        ident = sb("ident", [P, P])
        g = {"raw": sb("g_raw", [P, 5]), "th": sb("g_th", [P, 5]), "tmp": sb("g_tmp", [P, 3]),
             "mix": sb("g_mix", [P, 2]), "lut": sb("g_lut", [P, LUT])}
        with nc.semaphore("s_ident") as s_ident, nc.Block() as block:
            @block.gpsimd
            def _(pool):
                pool.memset(ident[:, :], 0.0).then_inc(s_ident, 1)
                pool.wait_ge(s_ident, 1)
                pool.affine_select(out=ident[:, :], in_=ident[:, :], compare_op=ALU.not_equal, fill=1.0, base=0,
                                   pattern=[[-1, P]], channel_multiplier=1).then_inc(s_ident, 1)

        with nc.sbuf_tensor("x_sb", [P, TILES, DIM], F32) as x_sb:
            with nc.sbuf_tensor("xT", [P, KT, T], F32) as xT:
                with nc.sbuf_tensor("kvT", [P, 2, T], F32R) as kvT, nc.sbuf_tensor("kv", [P, TILES, D_C], F32) as kv:
                    phase_prepare(nc, a, x_sb, xT, kvT, kv, ident, g)
                    phase_attention(nc, a, x_sb, xT, kvT, kv, ident, g)
                with nc.sbuf_tensor("lw", [P, LUT_W], F32) as lw:
                    fetch = (lw[:, :].rearrange("p (h n) -> p h n", h=HEADS), a["lutw"].rearrange("h p n -> p h n"))
                    phase_norm_transpose(nc, "n2", x_sb, xT, ident, fetch)
                    phase_swiglu(nc, x_sb, xT, lw, g)
            with nc.sbuf_tensor("place", [P, TILES, EXPERTS], F32) as place, \
                    nc.sbuf_tensor("parts", [P, TILES, 3, EXPERTS], BF16) as parts:
                r = {"place": place, "parts": parts}
                phase_mix_route(nc, a, x_sb, ident, g, r)
                phase_experts(nc, a, ident, g, r, out)


def rope(length, dim):
    inv = (1.0 / 10000.0 ** (np.arange(0, dim, 2, dtype=np.float32) / np.float32(dim))).astype(np.float32)
    f = np.arange(length, dtype=np.float32)[:, None] * inv[None, :]
    return np.repeat(np.sin(f), 2, axis=-1), np.repeat(np.cos(f), 2, axis=-1)


def tables():
    half = D_CQ // 2
    sin, cos = rope(SEQ, D_CQ)
    sign = np.where(np.arange(D_CQ) < half, -1.0, 1.0).astype(np.float32)
    cols = latent_columns()
    rot = np.stack([cos[:, c].T for c in cols[:3]] + [(sin * sign)[:, c].T for c in cols[:3]], 1)
    sin, cos = rope(SEQ, D_C)
    sin = sin * np.where(np.arange(D_C) < D_C // 2, -1.0, 1.0).astype(np.float32)
    by_token = [m.reshape(SEQ_T, P, D_C).transpose(1, 0, 2) for m in (cos, sin)]
    return {"rot": rot, "ktab": np.stack([cos.T, sin.T], 1), "ttab": by_token[0], "stab": by_token[1]}


def latent_columns():
    half = D_CQ // 2
    a, rest = np.arange(P), np.arange(P, half)
    return [a, a + half, np.concatenate([rest, rest + half]), np.concatenate([rest + half, rest])]


def kernel(**inputs):
    import concourse.bacc as bacc
    from concourse.bass_utils import run_bass_kernel_spmd

    v = {k: np.asarray(x) for k, x in inputs.items()}
    cols = latent_columns()
    by_part = lambda m: m.reshape(-1, P, m.shape[-1]).transpose(1, 0, 2).reshape(P, -1)
    down = v["L0_ffn_down_idx"].T
    down = np.concatenate([down, np.zeros((FT * P - INTER, DIM), down.dtype)])
    idx = np.concatenate([by_part(v["L0_ffn_gate_idx"].T), by_part(v["L0_ffn_up_idx"].T), by_part(down)], 1)
    ctx = v["ctx_512"].reshape(T, D_C)
    arrays = {
        "x": v["x"].reshape(T, DIM), "ctx": ctx, "ctxT": ctx.T,
        "g_xattn": v["g_xattn"], "g_ffn": v["g_ffn"], "gamma": v["L1_xattn_gamma_raw"].reshape(1),
        "lut": v["L0_ffn_lut"],
        "wqa": v["L1_xattn_Wq"].T, "wka": v["L1_xattn_Wk"].T,
        "wq": v["L0_xattn_Wq"].T.reshape(KT, P, HEADS, HK).transpose(2, 1, 0, 3).reshape(HEADS, P, KT * HK),
        "wc": v["L0_xattn_w_kc_q"][:, :, np.concatenate(cols)],
        "wqrT": v["L0_xattn_W_qr"][:, np.concatenate(cols[:3]), :].transpose(0, 2, 1),
        "wkrT": v["L0_xattn_W_kr"].transpose(0, 2, 1),
        "wkc": v["L0_xattn_w_kc_kv"],
        "woT": v["L0_xattn_Wo"].T.reshape(HEADS, HK, DIM),
        "idx": idx.reshape(P, HEADS, LUT_CHUNK).transpose(1, 0, 2),
        "gw": v["L1_ffn_gate_w"].T.reshape(KT, P, EXPERTS).transpose(1, 0, 2),
        "w_gate": v["L1_ffn_w_gate"], "w_up": v["L1_ffn_w_up"], "w_down": v["L1_ffn_w_down"],
        **tables(),
    }
    arrays = {"in_" + k: np.ascontiguousarray(x) for k, x in arrays.items()}
    nc = bacc.Bacc("TRN2", target_bir_lowering=False, num_devices=1)
    a = {k[3:]: nc.dram_tensor(k, x.shape, mybir.dt.from_np(x.dtype), kind="ExternalInput").ap()
         for k, x in arrays.items()}
    for name, shape in (("w1", (HEADS, P, D_CQ)), ("w2", (HEADS, P, DIM)), ("aff", (TILES, P, SEQ)),
                        ("kept", (TILES, P, SEQ)), ("lutw", (HEADS, P, LUT_CHUNK)), ("xn", (T, DIM)),
                        ("acc", (T + CAP, DIM))):
        a[name] = nc.dram_tensor("via_" + name, shape, F32).ap()
    out = nc.dram_tensor("out", (T, DIM), F32, kind="ExternalOutput").ap()
    build(nc, a, out)
    result = run_bass_kernel_spmd(nc, [arrays], core_ids=[0])
    return result.results[0]["out"].reshape(BATCH, SEQ, DIM)
```

```python
from contextlib import ExitStack

import numpy as np
import concourse.bass as bass
from concourse import mybir

ALU = mybir.AluOpType
ACT = mybir.ActivationFunctionType
F32 = mybir.dt.float32
F32R = mybir.dt.float32r
BF16 = mybir.dt.bfloat16
I32 = mybir.dt.int32
U32 = mybir.dt.uint32
AX = mybir.AxisListType.X

P = 128
BATCH, SEQ, DIM = 4, 512, 512
T = BATCH * SEQ
TILES = T // P
KT = DIM // P
SEQ_T = SEQ // P
HEADS, HK, D_C, D_CQ, ROT = 16, 128, 128, 384, 64
QT = D_CQ // P
UNITS = HEADS * BATCH
INTER = 1376
FT = (INTER + P - 1) // P
LUT = 16
PICKS = 4
GU_W = 2 * KT * P
F_W = GU_W + DIM
LUT_W = FT * F_W
LUT_CHUNK = LUT_W // HEADS
TOP = int(SEQ * 0.3)
ROUNDS = (TOP - 1) // 8
AFF_SCALE = 1.0 / (float(np.sqrt(np.float32(32))) * 4)
EXPERTS, CHOSEN, CAP, FE = 64, 8, 256, 256
FET = FE // P
HALVES = CAP // P
EPS = 1e-5
LOWEST = -3.0e38
assert LUT_CHUNK * HEADS == LUT_W and 8 * ROUNDS < TOP <= 8 * ROUNDS + 8


def need(eng, sem, n):
    if isinstance(n, int) and n <= 0:
        return
    eng.wait_ge(sem, n)


def stand(eng):
    eng.nop(nofuse=True)


class Chain:

    def __init__(self, eng, sem, base=0):
        self.eng, self.sem, self.base, self.n = eng, sem, base, 0

    def add(self, ins):
        ins.then_inc(self.sem, 1)
        self.n += 1
        return self.n

    def now(self):
        self.eng.wait_ge(self.sem, self.base + self.n)

    def link(self, ins):
        self.add(ins)
        self.now()


def scoped(nc, stack):
    def sb(name, shape, dt=F32):
        return stack.enter_context(nc.sbuf_tensor(name, shape, dt))

    def banks(name, n):
        return [stack.enter_context(nc.psum_tensor(f"{name}{i}", [P, 512], F32)) for i in range(n)]

    def sem(name):
        return stack.enter_context(nc.semaphore(name))

    return sb, banks, sem


def split_product(pe, out, a_parts, b_parts, start, stop, before_low=None):
    (a_hi, a_lo), (b_hi, b_lo) = a_parts, b_parts
    pe.matmul(out, a_hi, b_hi, start=start, stop=False)
    pe.matmul(out, a_lo, b_hi, start=False, stop=False)
    if before_low is not None:
        before_low()
    return pe.matmul(out, a_hi, b_lo, start=False, stop=stop)


def norm_stats(dve, ch, tiles, stats, mv, ve):
    n = len(tiles)
    for j, x in enumerate(tiles):
        ch.add(dve.bn_stats(stats[:, j, :], x))
    ch.now()
    stand(dve)
    for j in range(n):
        ch.add(dve.bn_aggr(mv[:, j, :], stats[:, j, :]))
    ch.now()
    return dve.tensor_scalar(ve[:, 0:n], mv[:, 0:n, 1], EPS, None, ALU.add)


def phase_prepare(nc, a, x_sb, xT, kvT, kv, ident, g):
    with ExitStack() as stack:
        sb, banks, sem = scoped(nc, stack)
        GROUP = HEADS // BATCH
        assert HEADS == TILES
        ctxT = sb("ctxT", [P, T])
        qaT = sb("qaT", [P, T])
        kaT = sb("kaT", [P, T])
        wqa = sb("wqa", [P, P])
        wka = sb("wka", [P, P])
        w1 = sb("fold1", [P, HEADS, D_CQ])
        wkrT = sb("wkrT", [ROT, HEADS, D_C])
        wkc = sb("wkc", [P, HEADS, D_C])
        w2 = sb("fold2", [P, HEADS, DIM])
        affo = sb("affo", [P, 2, SEQ])
        stats = sb("stats1", [P, TILES, 6])
        mv = sb("mv1", [P, TILES, 2])
        ve = sb("ve1", [P, TILES])
        half = sb("half1", [P, SEQ_T])
        rstd = sb("rstd1", [P, TILES])
        xn = sb("xn1", [P, 4, DIM])
        ps = banks("prep", 8)

        flat = xT[:, :, :].rearrange("p k t -> p (k t)")
        swapped = flat[:, 0:T]
        straight = flat[:, 2 * T:3 * T]
        tok = flat[:, T:2 * T].rearrange("p (i d) -> p i d", d=D_C)
        tmp = flat[:, 2 * T:3 * T].rearrange("p (i d) -> p i d", d=D_C)
        ktab = flat[:, 3 * T:3 * T + 2 * SEQ].rearrange("p (c t) -> p c t", c=2)
        ttab = flat[:, 3 * T + 2 * SEQ:3 * T + 3 * SEQ].rearrange("p (i d) -> p i d", d=D_C)
        stab = flat[:, 3 * T + 3 * SEQ:4 * T].rearrange("p (i d) -> p i d", d=D_C)

        s_gate = sem("s_gate")
        s_tanh = sem("s_tanh")
        s_gsm = sem("s_gsm")
        s_ctx = sem("s_ctx")
        s_kvT = sem("s_kvT")
        s_kv = sem("s_kv")
        s_rope = sem("s_rope")
        s_x = [sem(f"s_x{b}") for b in range(BATCH)]
        s_qk = sem("s_qk")
        s_qkc = sem("s_qkc")
        s_aff = sem("s_aff")
        s_affc = sem("s_affc")
        s_affo = [sem(f"s_affo{j}") for j in range(2)]
        s_win = [sem(f"s_win{j}") for j in range(BATCH)]
        s_fold = sem("s_fold")
        s_foldc = sem("s_foldc")
        s_fout = sem("s_fout")
        s_half = sem("s_half")
        s_var = sem("s_var")
        s_rstd = sem("s_rstd")
        s_ch = sem("s_ch")
        s_xn = sem("s_xn")
        s_tr = sem("s_tr")
        s_out = sem("s_out")
        block = stack.enter_context(nc.Block())

        @block.sync
        def _(sp):
            for dst, src in ((ctxT[:, :], a["ctxT"]), (wqa[:, :], a["wqa"]), (wka[:, :], a["wka"])):
                sp.dma_start(dst, src).then_inc(s_ctx, 16)
            for lo, hi in ((0, P // 2), (P // 2, P)):
                sp.dma_start(swapped[lo:hi, :], a["ctxT"][P // 2 - lo:P - lo, :]).then_inc(s_kvT, 16)
            sp.dma_start(ktab, a["ktab"]).then_inc(s_kvT, 16)
            for dst, src in ((ttab, a["ttab"]), (stab, a["stab"]),
                             (tok, a["ctx"].rearrange("(i p) d -> p i d", p=P))):
                sp.dma_start(dst, src).then_inc(s_kv, 16)
            for src, dst in ((a["g_xattn"], g["raw"][:, 0:2]), (a["g_ffn"], g["raw"][:, 2:4]),
                             (a["gamma"], g["raw"][:, 4:5])):
                sp.dma_start(dst, src.partition_broadcast(P)).then_inc(s_gate, 16)
            sp.dma_start(g["lut"][:, :], a["lut"].partition_broadcast(P)).then_inc(s_gate, 16)
            for b in range(BATCH):
                sp.dma_start(x_sb[:, b * SEQ_T:(b + 1) * SEQ_T, :],
                             a["x"][b * SEQ:(b + 1) * SEQ, :].rearrange("(i p) d -> p i d", p=P))\
                    .then_inc(s_x[b], 16)
            for n in range(BATCH):
                for t in range(n * GROUP, (n + 1) * GROUP):
                    sp.wait_ge(s_affc, t + 1)
                    sp.dma_start(a["aff"][t], affo[:, t % 2, :]).then_inc(s_affo[t % 2], 16)
                heads = slice(n * GROUP, (n + 1) * GROUP)
                sp.wait_ge(s_foldc, (n + 1) * 2 * GROUP)
                sp.dma_start(a["w1"][heads].rearrange("h p n -> p h n"), w1[:, heads, :]).then_inc(s_fout, 16)
                sp.dma_start(a["w2"][heads].rearrange("h p n -> p h n"), w2[:, heads, :]).then_inc(s_fout, 16)
            for j in range(2):
                sp.wait_ge(s_affo[j], 16 * TILES // 2)
            sp.wait_ge(s_fout, 32 * BATCH)

        @block.gpsimd
        def _(pool):
            pool.memset(half[:, :], -0.5).then_inc(s_half, 1)
            pool.wait_ge(s_half, 1)
            for b in range(BATCH):
                pool.wait_ge(s_var, b + 1)
                lo = b * SEQ_T
                pool.tensor_tensor(rstd[:, lo:lo + SEQ_T], ve[:, lo:lo + SEQ_T], half[:, :], ALU.pow)\
                    .then_inc(s_rstd, 1)

        @block.tensor
        def _(pe):
            pe.wait_ge(s_ctx, 48)
            for n in range(BATCH):
                for m, w in enumerate((wqa, wka)):
                    k = 2 * n + m
                    if k >= 4:
                        pe.wait_ge(s_qkc, k - 3)
                    pe.matmul(ps[4 + k % 4][:, :], w[:, :], ctxT[:, n * SEQ:(n + 1) * SEQ], start=True, stop=True)\
                        .then_inc(s_qk, 1)
            pe.wait_ge(s_qkc, 2 * BATCH)
            for n in range(BATCH):
                pe.wait_ge(s_win[n], 64)
                for h in range(n * GROUP, (n + 1) * GROUP):
                    j = h % 2
                    if h >= 2:
                        pe.wait_ge(s_foldc, 2 * h - 2)
                    for t in range(QT):
                        mm = pe.matmul(ps[2 * j][:, t * P:(t + 1) * P], w1[0:ROT, h, t * P:(t + 1) * P],
                                       wkrT[:, h, :], start=True, stop=True)
                    mm.then_inc(s_fold, 1)
                    pe.matmul(ps[2 * j + 1][:, :], wkc[:, h, :], w2[:, h, :], start=True, stop=True)\
                        .then_inc(s_fold, 1)
                    if h >= 2:
                        pe.wait_ge(s_affc, h - 1)
                    pe.matmul(ps[4 + j][:, :], qaT[:, h * P:(h + 1) * P], kaT[:, n * SEQ:(n + 1) * SEQ],
                              start=True, stop=True).then_inc(s_aff, 1)
                for t in range(n * SEQ_T, (n + 1) * SEQ_T):
                    pe.wait_ge(s_xn, t + 1)
                    if t >= 2:
                        pe.wait_ge(s_out, t - 1)
                    for k in range(KT):
                        tr = pe.transpose(ps[6 + t % 2][:, k * P:(k + 1) * P], xn[:, t % 4, k * P:(k + 1) * P],
                                          ident[:, :])
                    tr.then_inc(s_tr, 1)

        @block.scalar
        def _(act):
            for n in range(BATCH):
                heads = slice(n * GROUP, (n + 1) * GROUP)
                for src, dst in ((a["wqrT"], w1[0:ROT, heads, :]), (a["wkrT"], wkrT[:, heads, :]),
                                 (a["wkc"], wkc[:, heads, :]), (a["woT"], w2[:, heads, :])):
                    act.dma_start(dst, src[heads].rearrange("h p n -> p h n")).then_inc(s_win[n], 16)
            for k in range(2 * BATCH):
                act.wait_ge(s_qk, k + 1)
                n, dst = k // 2, (qaT, kaT)[k % 2]
                act.activation(dst[:, n * SEQ:(n + 1) * SEQ], ps[4 + k % 4][:, :], ACT.Copy).then_inc(s_qkc, 1)
            act.wait_ge(s_gate, 64)
            act.activation(g["th"][:, 0:4], g["raw"][:, 0:4], ACT.Tanh).then_inc(s_tanh, 1)
            act.activation(g["th"][:, 4:5], g["raw"][:, 4:5], ACT.Tanh, scale=0.5).then_inc(s_tanh, 1)
            act.wait_ge(s_tanh, 2)
            for n in range(BATCH):
                for h in range(n * GROUP, (n + 1) * GROUP):
                    act.wait_ge(s_fold, 2 * h + 1)
                    act.activation(w1[:, h, :], ps[2 * (h % 2)][:, 0:D_CQ], ACT.Copy).then_inc(s_foldc, 1)
                    act.wait_ge(s_fold, 2 * h + 2)
                    act.activation(w2[:, h, :], ps[2 * (h % 2) + 1][:, :], ACT.Copy, scale=g["th"][:, 0:1])\
                        .then_inc(s_foldc, 1)
                    act.wait_ge(s_aff, h + 1)
                    if h >= 2:
                        act.wait_ge(s_affo[h % 2], 16 * (h // 2))
                    act.activation(affo[:, h % 2, :], ps[4 + h % 2][:, :], ACT.Copy).then_inc(s_affc, 1)
                for t in range(n * SEQ_T, (n + 1) * SEQ_T):
                    act.wait_ge(s_tr, t + 1)
                    act.activation(xT[:, :, t * P:(t + 1) * P],
                                   ps[6 + t % 2][:, :].rearrange("p (k c) -> p k c", k=KT), ACT.Copy)\
                        .then_inc(s_out, 1)

        @block.vector
        def _(dve):
            dve.wait_ge(s_ctx, 48)
            dve.wait_ge(s_kvT, 48)
            for b in range(BATCH):
                c = slice(b * SEQ, (b + 1) * SEQ)
                dve.tensor_tensor(straight[:, c], ctxT[:, c], ktab[:, 0, :], ALU.mult)
                ins = dve.tensor_tensor(swapped[:, c], swapped[:, c], ktab[:, 1, :], ALU.mult)
            ins.then_inc(s_rope, 1)
            dve.wait_ge(s_rope, 1)
            dve.tensor_tensor(swapped[:, :], straight[:, :], swapped[:, :], ALU.add).then_inc(s_rope, 1)
            dve.wait_ge(s_rope, 2)
            dve.tensor_copy(kvT[:, 0, :], swapped[:, :]).then_inc(s_rope, 1)
            dve.wait_ge(s_rope, 3)
            dve.tensor_tensor(kvT[:, 1, :], swapped[:, :], kvT[:, 0, :], ALU.subtract).then_inc(s_rope, 1)
            H = D_C // 2
            dve.wait_ge(s_kv, 48)
            for b in range(BATCH):
                r = slice(b * SEQ_T, (b + 1) * SEQ_T)
                dve.tensor_tensor(kv[:, r, :], tok[:, r, :], ttab, ALU.mult)
                dve.tensor_tensor(tmp[:, r, 0:H], tok[:, r, H:], stab[:, :, 0:H], ALU.mult)
                ins = dve.tensor_tensor(tmp[:, r, H:], tok[:, r, 0:H], stab[:, :, H:], ALU.mult)
            ins.then_inc(s_rope, 1)
            dve.wait_ge(s_rope, 5)
            dve.tensor_tensor(kv[:, :, :], kv[:, :, :], tmp, ALU.add).then_inc(s_rope, 1)
            ch = Chain(dve, s_ch)
            for b in range(BATCH):
                dve.wait_ge(s_x[b], 16)
                lo = b * SEQ_T
                norm_stats(dve, ch, [x_sb[:, lo + j, :] for j in range(SEQ_T)], stats[:, lo:lo + SEQ_T, :],
                           mv[:, lo:lo + SEQ_T, :], ve[:, lo:lo + SEQ_T]).then_inc(s_var, 1)
                dve.wait_ge(s_rstd, b + 1)
                if b == 0:
                    dve.wait_ge(s_rope, 6)
                for t in range(lo, lo + SEQ_T):
                    if t >= 4:
                        dve.wait_ge(s_tr, t - 3)
                    dve.tensor_scalar(xn[:, t % 4, :], x_sb[:, t, :], mv[:, t, 0:1], rstd[:, t:t + 1],
                                      ALU.subtract, ALU.mult).then_inc(s_xn, 1)
            ch = Chain(dve, s_gsm)
            dve.wait_ge(s_tanh, 2)
            ch.link(dve.tensor_scalar(g["tmp"][:, 0:1], g["th"][:, 4:5], 0.5, 0.5, ALU.mult, ALU.add))
            ch.link(dve.tensor_scalar(g["tmp"][:, 1:2], g["tmp"][:, 0:1], -1.0, 1.0, ALU.mult, ALU.add))
            ch.add(dve.tensor_tensor(g["mix"][:, 0:1], g["tmp"][:, 1:2], g["th"][:, 1:2], ALU.mult))
            ch.link(dve.tensor_tensor(g["tmp"][:, 2:3], g["tmp"][:, 0:1], g["th"][:, 1:2], ALU.mult))
            ch.add(dve.tensor_scalar(g["mix"][:, 1:2], g["tmp"][:, 2:3], 0.25, None, ALU.mult))


def phase_attention(nc, a, x_sb, xT, kvT, kv, ident, g):
    with ExitStack() as stack:
        sb, banks, sem = scoped(nc, stack)
        rot = sb("rot", [P, 2 * QT, SEQ])
        wq = sb("wq", [P, KT, HK])
        wc_raw = sb("wc_raw", [P, 4 * P])
        w2_raw = sb("w2_raw", [P, DIM])
        wc = sb("wc", [P, 2, 4 * P], F32R)
        w1 = sb("w1", [P, D_CQ])
        w2 = sb("w2", [P, 2, DIM], F32R)
        qT = sb("qT", [P, 2, SEQ], F32R)
        prod = sb("prod", [P, 6, SEQ])
        qrot = sb("qrot", [P, QT, SEQ])
        qp = sb("qp", [P, 2, SEQ], F32R)
        attn = sb("attn", [P, 2, SEQ_T, SEQ])
        attnT = sb("attnT", [P, SEQ_T, SEQ])
        ctx_raw = sb("ctx_raw", [P, SEQ])
        ctx = sb("ctx", [P, 2, SEQ], F32R)
        nmax = sb("nmax", [P, 2, SEQ_T])
        esum = sb("esum", [P, 2, SEQ_T])
        rsum = sb("rsum", [P, 2, SEQ_T])
        aff = sb("affin", [P, SEQ])
        left = sb("left", [P, SEQ])
        tanh = sb("tanh", [P, SEQ])
        kept = sb("kept", [P, SEQ])
        top8 = sb("top8", [P, 8])
        idx = sb("idx", [P, LUT_CHUNK], I32)
        pick = sb("pick", [P, PICKS, LUT_CHUNK])
        wsum = sb("wsum", [P, LUT_CHUNK])

        ps_q, = banks("ps_q", 1)
        ps_r = banks("ps_r", 2)
        ps_s = banks("ps_s", 2)
        ps_t = banks("ps_t", 3)
        out_bank = (ps_t[2], ps_t[0], ps_t[1], ps_q)

        names = """rot_in
            wq_in wc_in w1_in w2_in aff_in idx_in
            q_full ab_full cc_full qp_full s_full t_full ctx_full o_full
            q_evac qp_evac exp_done t_evac ctx_evac tanh_done
            max_done a_mul b_mul cc_mul c_add o_add recip topk kept_made picked
            ab_add pick_added aff_out w_out
            wc_hi wc_lo w2_hi w2_lo q_lo qp_lo ctx_lo ctx_copied""".split()
        s = {n: sem("a_" + n) for n in names}
        block = stack.enter_context(nc.Block())
        TOPK_OPS = 2 * ROUNDS + 2
        SHARES = (((0, 0), (0, 6)), ((0, 1), (6, 10)), ((1, 2), (10, 11))), \
                 (((2, 4), (11, 15)), ((4, 7), (15, 19)), ((7, 7), (19, 21))), \
                 (((7, 9), (21, 25)), ((9, 12), (25, 29)), ((12, 12), (29, 31))), \
                 (((12, 14), (31, 35)), ((14, 16), (35, 39)), ((16, 16), (39, 2 * ROUNDS + 3)))

        def loop(eng, body):
            body(0)
            with eng.Fori(1, HEADS - 1) as i:
                body(i)
            body(HEADS - 1)

        @block.sync
        def _(sp):
            def load(dst, src, h, what):
                sp.dma_start(dst, src[bass.ds(h, 1), :, :].rearrange("o p n -> p (o n)"))\
                    .then_inc(s[what], 16)

            wq_f = wq[:, :, :].rearrange("p k n -> p (k n)")

            def weights(h):
                need(sp, s["q_full"], h * 4)
                load(wq_f, a["wq"], h, "wq_in")
                need(sp, s["wc_hi"], h)
                need(sp, s["wc_lo"], h)
                load(wc_raw[:, :], a["wc"], h, "wc_in")
                if isinstance(h, int) and h == 0:
                    sp.dma_start(rot[:, :, :], a["rot"]).then_inc(s["rot_in"], 16)
                need(sp, s["w2_hi"], h)
                need(sp, s["w2_lo"], h)
                load(w2_raw[:, :], a["w2"], h, "w2_in")
                need(sp, s["qp_full"], h * 4)
                load(w1[:, :], a["w1"], h, "w1_in")
                need(sp, s["picked"], h * LUT)
                load(idx[:, :], a["idx"], h, "idx_in")
                need(sp, s["kept_made"], h)
                need(sp, s["tanh_done"], h)
                load(aff[:, :], a["aff"], h, "aff_in")

            def body(h):
                weights(h)

            loop(sp, body)

        @block.gpsimd
        def _(pool):
            def ab_add(u):
                need(pool, s["qp_full"], u)
                for t in range(2):
                    pool.wait_ge(s["b_mul"], u * 2 + t + 1)
                    pool.tensor_tensor(qrot[:, t, :], prod[:, 2 * t, :], prod[:, 2 * t + 1, :], ALU.add)\
                        .then_inc(s["ab_add"], 1)

            def c_add(u):
                pool.wait_ge(s["cc_mul"], u + 1)
                pool.tensor_tensor(qrot[:, 2, :], prod[:, 4, :], prod[:, 5, :], ALU.add).then_inc(s["c_add"], 1)

            def pick_add(h, k):
                pool.wait_ge(s["picked"], h * LUT + k + 1)
                if k == 0:
                    need(pool, s["w_out"], h * 16)
                    stand(pool)
                    pool.tensor_copy(wsum[:, :], pick[:, 0, :]).then_inc(s["pick_added"], 1)
                else:
                    pool.wait_ge(s["pick_added"], h * LUT + k)
                    pool.tensor_tensor(wsum[:, :], wsum[:, :], pick[:, k % PICKS, :], ALU.add)\
                        .then_inc(s["pick_added"], 1)

            def low_part(w, raw, name, h):
                pool.wait_ge(s[name + "_in"], h * 16 + 16)
                pool.wait_ge(s[name + "_hi"], h + 1)
                pool.tensor_tensor(w[:, 1, :], raw[:, :], w[:, 0, :], ALU.subtract).then_inc(s[name + "_lo"], 1)

            def ctx_low(u):
                pool.wait_ge(s["ctx_evac"], u + 1)
                pool.wait_ge(s["ctx_copied"], u + 1)
                pool.tensor_tensor(ctx[:, 1, :], ctx_raw[:, :], ctx[:, 0, :], ALU.subtract).then_inc(s["ctx_lo"], 1)

            low_part(wc, wc_raw, "wc", 0)
            ab_add(0)
            c_add(0)

            def body(h):
                for b in range(BATCH):
                    u = h * 4 + b
                    if b == 1:
                        low_part(w2, w2_raw, "w2", h)
                    if b == 3 and not (isinstance(h, int) and h == HEADS - 1):
                        low_part(wc, wc_raw, "wc", h + 1)
                    (k0, _), (_, k1) = SHARES[b][0][0], SHARES[b][2][0]
                    between = k0 if b == 0 else k0 + 2
                    for k in range(k0, between):
                        pick_add(h, k)
                    if not (isinstance(h, int) and u == 0):
                        ctx_low(u - 1)
                    for k in range(between, min(k1, k0 + 4)):
                        pick_add(h, k)
                    if not (isinstance(h, int) and u == UNITS - 1):
                        ab_add(u + 1)
                        c_add(u + 1)
                    for k in range(k0 + 4, k1):
                        pick_add(h, k)

            loop(pool, body)
            ctx_low(UNITS - 1)

        @block.scalar
        def _(act):
            def evac_q(u):
                act.wait_ge(s["q_full"], u + 1)
                need(act, s["cc_full"], u * 2)
                act.activation(qT[:, 0, :], ps_q[:, :], ACT.Copy).then_inc(s["q_evac"], 1)

            def evac_qp(u):
                act.wait_ge(s["qp_full"], u + 1)
                act.activation(qp[:, 0, :], ps_q[:, :], ACT.Copy).then_inc(s["qp_evac"], 1)

            def exps(u, b, js):
                for j in js:
                    act.wait_ge(s["max_done"], u * 4 + j + 1)
                    if j == 0:
                        need(act, s["t_full"], u * 4 - 4)
                    act.activation(attn[:, b % 2, j, :], ps_s[j % 2][:, :], ACT.Exp, bias=nmax[:, b % 2, j:j + 1],
                                   accum_out=esum[:, b % 2, j:j + 1]).then_inc(s["exp_done"], 1)

            def evac_back(u):
                for j in range(SEQ_T):
                    act.wait_ge(s["t_full"], u * 4 + j + 1)
                    if j == 0:
                        need(act, s["ctx_full"], u)
                    act.activation(attnT[:, :, j * P:(j + 1) * P],
                                   ps_t[j % 3][:, :].rearrange("p (l c) -> p l c", l=SEQ_T), ACT.Copy)\
                        .then_inc(s["t_evac"], 1)

            def evac_ctx(u):
                act.wait_ge(s["ctx_full"], u + 1)
                need(act, s["o_full"], u * 4)
                act.activation(ctx_raw[:, :], ps_t[1][:, :], ACT.Copy).then_inc(s["ctx_copied"], 1)
                act.activation(ctx[:, 0, :], ps_t[1][:, :], ACT.Copy).then_inc(s["ctx_evac"], 1)

            def store(h):
                act.wait_ge(s["kept_made"], h + 1)
                act.dma_start(a["kept"][bass.ds(h, 1), :, :].rearrange("o p n -> p (o n)"), kept[:, :])\
                    .then_inc(s["aff_out"], 16)
                act.wait_ge(s["pick_added"], h * LUT + LUT)
                act.dma_start(a["lutw"][:, bass.ds(h * LUT_CHUNK, LUT_CHUNK)], wsum[:, :])\
                    .then_inc(s["w_out"], 16)

            def high_part(w, raw, name, h, last_read, n):
                act.wait_ge(s[name + "_in"], h * 16 + 16)
                need(act, s[last_read], n)
                act.activation(w[:, 0, :], raw[:, :], ACT.Copy).then_inc(s[name + "_hi"], 1)

            high_part(wc, wc_raw, "wc", 0, "cc_full", 0)
            evac_q(0)

            def body(h):
                for b in range(BATCH):
                    u = h * 4 + b
                    first = isinstance(h, int) and u == 0
                    last = isinstance(h, int) and u == UNITS - 1
                    if b == 1:
                        high_part(w2, w2_raw, "w2", h, "o_full", h * 16)
                    if b == 3 and not last:
                        high_part(wc, wc_raw, "wc", h + 1, "cc_full", h * 8 + 8)
                    if not first:
                        evac_back(u - 1)
                    evac_qp(u)
                    if not first:
                        evac_ctx(u - 1)
                    exps(u, b, (0, 1))
                    if not last:
                        evac_q(u + 1)
                    exps(u, b, (2, 3))
                    if b == 1:
                        act.wait_ge(s["aff_in"], h * 16 + 16)
                        need(act, s["kept_made"], h)
                        act.activation(tanh[:, :], aff[:, :], ACT.Tanh, scale=0.5 * AFF_SCALE)\
                            .then_inc(s["tanh_done"], 1)
                    if b == 3:
                        store(h)

            loop(act, body)
            evac_back(UNITS - 1)
            evac_ctx(UNITS - 1)
            act.wait_ge(s["aff_out"], 16 * HEADS)
            act.wait_ge(s["w_out"], 16 * HEADS)

        @block.tensor
        def _(pe):
            def q_heads(u, b, h):
                if b == 0:
                    pe.wait_ge(s["wq_in"], h * 16 + 16)
                need(pe, s["qp_evac"], u)
                for k in range(KT):
                    mm = pe.matmul(ps_q[:, :], wq[:, k, :], xT[:, k, b * SEQ:(b + 1) * SEQ],
                                   start=(k == 0), stop=(k == KT - 1))
                mm.then_inc(s["q_full"], 1)

            def latent(u, b, h, which, rs=(0, 1)):
                if which == 0 and 0 in rs:
                    if b == 0:
                        pe.wait_ge(s["wc_hi"], h + 1)
                        pe.wait_ge(s["wc_lo"], h + 1)
                    pe.wait_ge(s["q_evac"], u + 1)
                    need(pe, s["cc_mul"], u)
                for r in rs:
                    if which == 1:
                        if r == 0:
                            pe.wait_ge(s["a_mul"], u + 1)
                        else:
                            pe.wait_ge(s["b_mul"], u * 2 + 2)
                    c = (2 * which + r) * P
                    low = (lambda: pe.wait_ge(s["q_lo"], u + 1)) if which == 0 and r == 0 else None
                    mm = split_product(pe, ps_r[r][:, :], (wc[:, 0, c:c + P], wc[:, 1, c:c + P]),
                                       (qT[:, 0, :], qT[:, 1, :]), True, True, low)
                    mm.then_inc(s["ab_full" if which == 0 else "cc_full"], 1)

            def query(u, b, h):
                if b == 0:
                    pe.wait_ge(s["w1_in"], h * 16 + 16)
                need(pe, s["o_add"], u * 4 - 4)
                for t in range(QT):
                    if t < 2:
                        pe.wait_ge(s["ab_add"], u * 2 + t + 1)
                    else:
                        pe.wait_ge(s["c_add"], u + 1)
                    mm = pe.matmul(ps_q[:, :], w1[:, t * P:(t + 1) * P], qrot[:, t, :],
                                   start=(t == 0), stop=(t == QT - 1))
                mm.then_inc(s["qp_full"], 1)

            def scores(u, b, j):
                if j == 0:
                    pe.wait_ge(s["qp_lo"], u + 1)
                need(pe, s["exp_done"], u * 4 + j - 1)
                q, k = slice(j * P, (j + 1) * P), slice(b * SEQ, (b + 1) * SEQ)
                split_product(pe, ps_s[j % 2][:, :], (qp[:, 0, q], qp[:, 1, q]), (kvT[:, 0, k], kvT[:, 1, k]),
                              True, True).then_inc(s["s_full"], 1)

            def turn(u, b, j):
                pe.wait_ge(s["exp_done"], u * 4 + j + 1)
                if j < 3:
                    need(pe, s["o_add"], u * 4 - 4 + (2, 3, 1)[j])
                else:
                    pe.wait_ge(s["t_evac"], u * 4 + 1)
                for l in range(SEQ_T):
                    tr = pe.transpose(ps_t[j % 3][:, l * P:(l + 1) * P], attn[:, b % 2, j, l * P:(l + 1) * P],
                                      ident[:, :])
                tr.then_inc(s["t_full"], 1)

            def context(u, b):
                pe.wait_ge(s["t_evac"], u * 4 + 4)
                for l in range(SEQ_T):
                    mm = pe.matmul(ps_t[1][:, :], kv[:, b * SEQ_T + l, :], attnT[:, l, :],
                                   start=(l == 0), stop=(l == SEQ_T - 1))
                mm.then_inc(s["ctx_full"], 1)

            def output(u, b, h, j):
                if j == 0:
                    if b == 0:
                        pe.wait_ge(s["w2_hi"], h + 1)
                        pe.wait_ge(s["w2_lo"], h + 1)
                    pe.wait_ge(s["ctx_lo"], u + 1)
                if j == 3:
                    need(pe, s["o_add"], u * 4)
                q = slice(j * P, (j + 1) * P)
                split_product(pe, out_bank[j][:, :], (ctx[:, 0, q], ctx[:, 1, q]), (w2[:, 0, :], w2[:, 1, :]),
                              True, True)\
                    .then_inc(s["o_full"], 1)

            q_heads(0, 0, 0)
            latent(0, 0, 0, 0)
            latent(0, 0, 0, 1)

            def body(h):
                for b in range(BATCH):
                    u = h * 4 + b
                    first = isinstance(h, int) and u == 0
                    last = isinstance(h, int) and u == UNITS - 1
                    pb, ph = (b - 1) % 4, h if b else h - 1
                    nb, nh = (b + 1) % 4, h if b < 3 else h + 1
                    if not first:
                        for j in range(SEQ_T):
                            turn(u - 1, pb, j)
                    query(u, b, h)
                    if not first:
                        context(u - 1, pb)
                    scores(u, b, 0)
                    scores(u, b, 1)
                    if not last:
                        q_heads(u + 1, nb, nh)
                    scores(u, b, 2)
                    if not first:
                        output(u - 1, pb, ph, 0)
                    if not last:
                        latent(u + 1, nb, nh, 0)
                    scores(u, b, 3)
                    if not first:
                        output(u - 1, pb, ph, 1)
                        output(u - 1, pb, ph, 2)
                    if not last:
                        latent(u + 1, nb, nh, 1, (0,))
                    if not first:
                        output(u - 1, pb, ph, 3)
                    if not last:
                        latent(u + 1, nb, nh, 1, (1,))

            loop(pe, body)
            for j in range(SEQ_T):
                turn(UNITS - 1, 3, j)
            context(UNITS - 1, 3)
            for j in range(SEQ_T):
                output(UNITS - 1, 3, HEADS - 1, j)

        @block.vector
        def _(dve):
            def rope_ab(u, r):
                dve.wait_ge(s["ab_full"], u * 2 + r + 1)
                need(dve, s["ab_add"], u * 2)
                for t, tab in (((0, 0), (3, QT + 1)), ((1, QT), (2, 1)))[r]:
                    ins = dve.tensor_tensor(prod[:, t, :], ps_r[r][:, :], rot[:, tab, :], ALU.mult)
                    if r == 1:
                        ins.then_inc(s["b_mul"], 1)
                if r == 0:
                    ins.then_inc(s["a_mul"], 1)

            def rope_c(u):
                need(dve, s["c_add"], u)
                for t in range(2):
                    dve.wait_ge(s["cc_full"], u * 2 + t + 1)
                    ins = dve.tensor_tensor(prod[:, 4 + t, :], ps_r[t][:, :], rot[:, 2 + QT * t, :], ALU.mult)
                ins.then_inc(s["cc_mul"], 1)

            def maxes(u, b, js):
                for j in js:
                    dve.wait_ge(s["s_full"], u * 4 + j + 1)
                    dve.tensor_reduce(nmax[:, b % 2, j:j + 1], ps_s[j % 2][:, :], AX, ALU.max, negate=True)\
                        .then_inc(s["max_done"], 1)

            def add_out(u, b, js):
                dve.wait_ge(s["recip"], u + 1)
                for j in js:
                    dve.wait_ge(s["o_full"], u * 4 + j + 1)
                    need(dve, s["o_add"], u * 4 - 12)
                    xt = x_sb[:, b * SEQ_T + j, :]
                    dve.scalar_tensor_tensor(xt, out_bank[j][:, :], rsum[:, b % 2, j:j + 1], xt, ALU.mult, ALU.add)\
                        .then_inc(s["o_add"], 1)

            def sums(u, b):
                dve.wait_ge(s["exp_done"], u * 4 + 4)
                dve.reciprocal(rsum[:, b % 2, :], esum[:, b % 2, :]).then_inc(s["recip"], 1)

            def topk(h, n):
                base = h * TOPK_OPS
                src = aff if n < 2 else left
                if n == 0:
                    dve.wait_ge(s["aff_in"], h * 16 + 16)
                    need(dve, s["kept_made"], h)
                if n < 2 * ROUNDS + 2:
                    need(dve, s["topk"], base + n)
                if n <= 2 * ROUNDS:
                    stand(dve)
                if n <= 2 * ROUNDS and n % 2 == 0:
                    dve.max(top8[:, :], src[:, :]).then_inc(s["topk"], 1)
                elif n < 2 * ROUNDS:
                    dve.match_replace(left[:, :], top8[:, :], src[:, :], LOWEST).then_inc(s["topk"], 1)
                elif n == 2 * ROUNDS + 1:
                    k = TOP - 8 * ROUNDS - 1
                    dve.tensor_scalar(left[:, :], aff[:, :], top8[:, k:k + 1], None, ALU.is_ge)\
                        .then_inc(s["topk"], 1)
                else:
                    dve.wait_ge(s["topk"], base + TOPK_OPS)
                    dve.wait_ge(s["tanh_done"], h + 1)
                    need(dve, s["aff_out"], h * 16)
                    dve.scalar_tensor_tensor(kept[:, :], tanh[:, :], 1.0, left[:, :], ALU.add, ALU.mult)\
                        .then_inc(s["kept_made"], 1)

            def pick_entry(h, k):
                if k == 0:
                    dve.wait_ge(s["idx_in"], h * 16 + 16)
                need(dve, s["pick_added"], h * LUT + k + 1 - PICKS)
                dve.tensor_scalar(pick[:, k % PICKS, :], idx[:, :], float(k), g["lut"][:, k:k + 1], ALU.is_equal,
                                  ALU.mult).then_inc(s["picked"], 1)

            def background(h, share):
                (k, k_end), (n, n_end) = share
                while k < k_end or n < n_end:
                    if n < n_end:
                        topk(h, n)
                        n += 1
                    if k < k_end:
                        pick_entry(h, k)
                        k += 1

            def low_part(pair, ps, name, u):
                dve.wait_ge(s[name + "_evac"], u + 1)
                dve.tensor_tensor(pair[:, 1, :], ps[:, :], pair[:, 0, :], ALU.subtract).then_inc(s[name + "_lo"], 1)

            low_part(qT, ps_q, "q", 0)
            dve.wait_ge(s["rot_in"], 16)
            rope_ab(0, 0)
            rope_ab(0, 1)
            rope_c(0)

            def body(h):
                for b in range(BATCH):
                    u = h * 4 + b
                    first = isinstance(h, int) and u == 0
                    last = isinstance(h, int) and u == UNITS - 1
                    background(h, SHARES[b][0])
                    low_part(qp, ps_q, "qp", u)
                    background(h, SHARES[b][1])
                    maxes(u, b, (0, 1))
                    background(h, SHARES[b][2])
                    if not last:
                        low_part(qT, ps_q, "q", u + 1)
                    maxes(u, b, (2,))
                    if not first:
                        add_out(u - 1, (b - 1) % 4, (0,))
                    if not last:
                        rope_ab(u + 1, 0)
                    maxes(u, b, (3,))
                    if not last:
                        rope_ab(u + 1, 1)
                    sums(u, b)
                    if not first:
                        add_out(u - 1, (b - 1) % 4, (1, 2, 3))
                    if not last:
                        rope_c(u + 1)

            loop(dve, body)
            add_out(UNITS - 1, 3, range(SEQ_T))


def phase_swiglu_mix(nc, a, x_sb, ident, g, r):
    with ExitStack() as stack:
        sb, banks, sem = scoped(nc, stack)
        lw = sb("lw", [P, FT, F_W])
        xT = sb("xT2", [P, 2, KT, SEQ], F32R)
        gu = sb("gu", [P, 2, 2, GU_W], F32R)
        dn = sb("dn", [P, 2, 2, DIM], F32R)
        hcut = sb("hcut2", [P, 2, 2, SEQ], F32R)
        th = sb("th2", [P, SEQ])
        u = sb("u2", [P, SEQ])
        h = sb("h2", [P, SEQ])
        xn = sb("xn2", [P, SEQ_T, DIM])
        stats = sb("stats2", [P, SEQ_T, 6])
        mv = sb("mv2", [P, SEQ_T, 2])
        ve = sb("ve2", [P, SEQ_T])
        half = sb("half2", [P, SEQ_T])
        rstd = sb("rstd2", [P, SEQ_T])
        kept = sb("kept_m", [P, SEQ_T, SEQ])
        stats3 = sb("stats3", [P, SEQ_T, 6])
        mv3 = sb("mv3", [P, SEQ_T, 2])
        ve3 = sb("ve3", [P, SEQ_T])
        rstd3 = sb("rstd3", [P, SEQ_T])
        scl = sb("scl", [P, SEQ_T])
        shift = sb("shift", [P, SEQ_T])
        xnT = sb("xnT", [P, SEQ_T, DIM])
        gw = sb("gw", [P, KT, EXPERTS])
        logit = sb("logit", [P, SEQ_T, EXPERTS])
        rest = sb("rest", [P, SEQ_T, EXPERTS])
        top8 = sb("rtop8", [P, SEQ_T, 8])
        nmax = sb("rnmax", [P, SEQ_T])
        prob = sb("prob", [P, SEQ_T, EXPERTS])
        psum_e = sb("psum_e", [P, SEQ_T])
        rden = sb("rden", [P, SEQ_T])
        sel = sb("sel", [P, SEQ_T, EXPERTS])
        selb = sb("selb", [P, SEQ_T, EXPERTS], BF16)
        valid = sb("valid", [P, SEQ_T, EXPERTS])
        taken = sb("taken", [P, EXPERTS])
        takenb = sb("takenb", [P, EXPERTS], BF16)
        count = sb("count", [P, EXPERTS])
        posp = sb("posp", [P, SEQ_T, EXPERTS])
        w = sb("rw", [P, SEQ_T, EXPERTS])
        before = sb("before", [P, P], BF16)
        ones = sb("ones", [P, P], BF16)
        zeros = sb("zeros", [P, DIM])

        ps_g, ps_u = banks("ps_gu", 2)
        ps_o = banks("ps_o", SEQ_T)
        ps_m = banks("ps_m", 2)
        ps_x = (ps_m[0], ps_m[1], ps_g, ps_u)
        w_group = (range(0, 1), range(1, 2), range(2, 5), range(5, FT))
        s_w = [sem(f"f_w{i}") for i in range(len(w_group))]
        s = {n: sem("f_" + n) for n in """half ch var rstd xn_made xt_full xt_evac x_lo gu_hi gu_lo d_hi d_lo
            g_full u_full tanh_done u_made h_made h_hi h_lo down o_add
            kept_in gw_in const a_full a_used m_var m_rstd m_ch x_new m_xn xn_out acc_out m_xt_full m_xt_evac
            l_full nmax prob_done selb_made p_full routed""".split()}
        block = stack.enter_context(nc.Block())
        STATS = 2 * SEQ_T

        def loop(eng, body):
            body(0)
            with eng.Fori(1, BATCH - 1) as b:
                body(b)
            body(BATCH - 1)

        def last(b):
            return isinstance(b, int) and b == BATCH - 1

        @block.sync
        def _(sp):
            for i, tiles in enumerate(w_group):
                for f in tiles:
                    sp.dma_start(lw[:, f, :], a["lutw"][:, f * F_W:(f + 1) * F_W]).then_inc(s_w[i], 16)
            sp.dma_start(gw[:, :, :], a["gw"]).then_inc(s["gw_in"], 16)
            sp.wait_ge(s["const"], 4)
            for k in range(HALVES):
                sp.dma_start(a["acc"][T + k * P:T + (k + 1) * P, :], zeros[:, :]).then_inc(s["acc_out"], 16)
            for m in range(BATCH):
                need(sp, s["x_new"], m * SEQ_T)
                sp.dma_start(kept[:, :, :], a["kept"][m * SEQ_T:(m + 1) * SEQ_T].rearrange("i p n -> p i n"))\
                    .then_inc(s["kept_in"], 16)
                rows = slice(m * SEQ, (m + 1) * SEQ)
                sp.wait_ge(s["x_new"], (m + 1) * SEQ_T)
                sp.dma_start(a["acc"][rows].rearrange("(i p) d -> p i d", p=P), x_sb[:, m * SEQ_T:(m + 1) * SEQ_T, :])\
                    .then_inc(s["acc_out"], 16)
                sp.wait_ge(s["m_xn"], (m + 1) * SEQ_T)
                sp.dma_start(a["xn"][rows].rearrange("(i p) d -> p i d", p=P), xn[:, :, :]).then_inc(s["xn_out"], 16)
            sp.wait_ge(s["acc_out"], 16 * (HALVES + BATCH))
            sp.wait_ge(s["xn_out"], 16 * BATCH)

        @block.tensor
        def _(pe):
            def turn(b, js):
                for j in js:
                    pe.wait_ge(s["xn_made"], b * SEQ_T + j + 1)
                    need(pe, s["routed"] if j < 2 else s["h_made"], b - 1 if j < 2 else b * FT)
                    for k in range(KT):
                        tr = pe.transpose(ps_x[j][:, k * P:(k + 1) * P], xn[:, j, k * P:(k + 1) * P], ident[:, :])
                    tr.then_inc(s["xt_full"], 1)

            def gate_up(b, f):
                n = b * FT + f
                if f == 0:
                    pe.wait_ge(s["x_lo"], b * SEQ_T + SEQ_T)
                pe.wait_ge(s["gu_lo"], n + 1)
                for m, (ps, full, used) in enumerate(((ps_g, "g_full", "u_made"), (ps_u, "u_full", "h_made"))):
                    need(pe, s[used], n)
                    for k in range(KT):
                        cols = slice((m * KT + k) * P, (m * KT + k + 1) * P)
                        mm = split_product(pe, ps[:, :], (gu[:, f % 2, 0, cols], gu[:, f % 2, 1, cols]),
                                           (xT[:, 0, k, :], xT[:, 1, k, :]), k == 0, k == KT - 1)
                    mm.then_inc(s[full], 1)

            def down(b, f):
                n = b * FT + f
                pe.wait_ge(s["h_lo"], n + 1)
                pe.wait_ge(s["d_lo"], n + 1)
                if f == 0:
                    need(pe, s["o_add"], b * SEQ_T)
                for j in range(SEQ_T):
                    q = slice(j * P, (j + 1) * P)
                    mm = split_product(pe, ps_o[j][:, :], (hcut[:, f % 2, 0, q], hcut[:, f % 2, 1, q]),
                                       (dn[:, f % 2, 0, :], dn[:, f % 2, 1, :]), f == 0, f == FT - 1)
                mm.then_inc(s["down"], 1)

            def turn_kept(m, js):
                pe.wait_ge(s["kept_in"], m * 16 + 16)
                for j in js:
                    if j >= 2:
                        pe.wait_ge(s["a_used"], m * SEQ_T + j - 1)
                    for k in range(SEQ_T):
                        tr = pe.transpose(ps_m[j % 2][:, k * P:(k + 1) * P], kept[:, k, j * P:(j + 1) * P], ident[:, :])
                    tr.then_inc(s["a_full"], 1)

            def turn_mixed(m, js):
                for j in js:
                    pe.wait_ge(s["m_xn"], m * SEQ_T + j + 1)
                    if j < 2:
                        pe.wait_ge(s["a_used"], m * SEQ_T + j + 3)
                    else:
                        pe.wait_ge(s["m_xt_evac"], m * SEQ_T + j - 1)
                    for k in range(KT):
                        tr = pe.transpose(ps_m[j % 2][:, k * P:(k + 1) * P], xn[:, j, k * P:(k + 1) * P], ident[:, :])
                    tr.then_inc(s["m_xt_full"], 1)

            def logits(m):
                pe.wait_ge(s["gw_in"], 16)
                pe.wait_ge(s["m_xt_evac"], m * SEQ_T + SEQ_T)
                for j in range(SEQ_T):
                    for k in range(KT):
                        mm = pe.matmul(ps_m[0][:, j * EXPERTS:(j + 1) * EXPERTS], xnT[:, j, k * P:(k + 1) * P],
                                       gw[:, k, :], start=(k == 0), stop=(k == KT - 1))
                mm.then_inc(s["l_full"], 1)

            def places(m):
                pe.wait_ge(s["const"], 5)
                pe.wait_ge(s["selb_made"], m + 1)
                for j in range(SEQ_T):
                    out = ps_m[1][:, j * EXPERTS:(j + 1) * EXPERTS]
                    pe.matmul(out, before[:, :], selb[:, j, :], start=True, stop=False)
                    for k in range(j):
                        pe.matmul(out, ones[:, :], selb[:, k, :], start=False, stop=False)
                    mm = pe.matmul(out, ones[:, :], takenb[:, :], start=False, stop=True)
                mm.then_inc(s["p_full"], 1)

            turn(0, range(SEQ_T))

            def body(b):
                mix = not (isinstance(b, int) and b == 0)
                for f in range(FT):
                    gate_up(b, f)
                    if mix and f == 1:
                        turn_kept(b - 1, (0, 1))
                    if mix and f == 7:
                        turn_mixed(b - 1, (0, 1))
                    if mix and f == 8:
                        logits(b - 1)
                    if mix and f == 9:
                        places(b - 1)
                    if f == FT - 1 and not last(b):
                        turn(b + 1, (0, 1))
                    if f > 0:
                        down(b, f - 1)
                    if mix and f == 3:
                        turn_kept(b - 1, (2, 3))
                    if mix and f == 7:
                        turn_mixed(b - 1, (2, 3))
                if not last(b):
                    turn(b + 1, (2, 3))
                down(b, FT - 1)

            loop(pe, body)
            m = BATCH - 1
            turn_kept(m, range(SEQ_T))
            turn_mixed(m, range(SEQ_T))
            logits(m)
            places(m)

        @block.scalar
        def _(act):
            def high_gu(b, f):
                n = b * FT + f
                i = [f in tiles for tiles in w_group].index(True)
                act.wait_ge(s_w[i], 16 * len(w_group[i]))
                need(act, s["u_full"], n if f == 0 else n - 1)
                act.activation(gu[:, f % 2, 0, :], lw[:, f, 0:GU_W], ACT.Copy).then_inc(s["gu_hi"], 1)

            def high_d(b, f):
                n = b * FT + f
                need(act, s["down"], n if f == 0 else n - 1)
                act.activation(dn[:, f % 2, 0, :], lw[:, f, GU_W:], ACT.Copy).then_inc(s["d_hi"], 1)

            def evac_x(b):
                for j in range(SEQ_T):
                    act.wait_ge(s["xt_full"], b * SEQ_T + j + 1)
                    act.activation(xT[:, 0, :, j * P:(j + 1) * P],
                                   ps_x[j][:, :].rearrange("p (k c) -> p k c", k=KT), ACT.Copy)\
                        .then_inc(s["xt_evac"], 1)

            high_gu(0, 0)
            high_d(0, 0)
            evac_x(0)

            def evac_mixed(m, js):
                for j in js:
                    act.wait_ge(s["m_xt_full"], m * SEQ_T + j + 1)
                    act.activation(xnT[:, j, :], ps_m[j % 2][:, :], ACT.Copy).then_inc(s["m_xt_evac"], 1)

            def exps(m):
                act.wait_ge(s["nmax"], m + 1)
                for j in range(SEQ_T):
                    act.activation(prob[:, j, :], logit[:, j, :], ACT.Exp, bias=nmax[:, j:j + 1],
                                   accum_out=psum_e[:, j:j + 1]).then_inc(s["prob_done"], 1)

            def body(b):
                mix = not (isinstance(b, int) and b == 0)
                for f in range(FT):
                    n = b * FT + f
                    if mix and f == 9:
                        exps(b - 1)
                    if f < FT - 1:
                        high_gu(b, f + 1)
                    act.wait_ge(s["g_full"], n + 1)
                    need(act, s["u_made"], n)
                    act.activation(th[:, :], ps_g[:, :], ACT.Tanh, scale=0.5)\
                        .then_inc(s["tanh_done"], 1)
                    if f == FT - 1 and not last(b):
                        high_gu(b + 1, 0)
                    act.wait_ge(s["h_made"], n + 1)
                    need(act, s["down"], n if f == 0 else n - 1)
                    act.activation(hcut[:, f % 2, 0, :], h[:, :], ACT.Copy).then_inc(s["h_hi"], 1)
                    if mix and f == 7:
                        evac_mixed(b - 1, (0, 1))
                    if f < FT - 1:
                        high_d(b, f + 1)
                    if mix and f == 7:
                        evac_mixed(b - 1, (2, 3))
                if not last(b):
                    evac_x(b + 1)
                    high_d(b + 1, 0)

            loop(act, body)
            evac_mixed(BATCH - 1, range(SEQ_T))
            exps(BATCH - 1)

        @block.gpsimd
        def _(pool):
            def inverse_root(b):
                pool.wait_ge(s["var"], b + 1)
                pool.tensor_tensor(rstd[:, :], ve[:, :], half[:, :], ALU.pow).then_inc(s["rstd"], 1)

            def low_parts(b, f):
                n = b * FT + f
                pool.wait_ge(s["gu_hi"], n + 1)
                pool.tensor_tensor(gu[:, f % 2, 1, :], lw[:, f, 0:GU_W], gu[:, f % 2, 0, :], ALU.subtract)\
                    .then_inc(s["gu_lo"], 1)
                pool.wait_ge(s["d_hi"], n + 1)
                pool.tensor_tensor(dn[:, f % 2, 1, :], lw[:, f, GU_W:], dn[:, f % 2, 0, :], ALU.subtract)\
                    .then_inc(s["d_lo"], 1)

            def inverse_root_mixed(n):
                pool.wait_ge(s["m_var"], n + 1)
                pool.tensor_tensor(rstd3[:, :], ve3[:, :], half[:, :], ALU.pow).then_inc(s["m_rstd"], 1)

            pool.memset(half[:, :], -0.5).then_inc(s["half"], 1)
            pool.wait_ge(s["half"], 1)
            inverse_root(0)
            low_parts(0, 0)
            pool.memset(zeros[:, :], 0.0).then_inc(s["const"], 1)
            pool.memset(ones[:, :], 1.0).then_inc(s["const"], 1)
            pool.memset(takenb[:, :], 0.0).then_inc(s["const"], 1)
            pool.memset(taken[:, :], 0.0).then_inc(s["const"], 1)
            pool.wait_ge(s["const"], 4)
            pool.affine_select(out=before[:, :], in_=ones[:, :], compare_op=ALU.is_gt, fill=0.0, base=0,
                               pattern=[[1, P]], channel_multiplier=-1).then_inc(s["const"], 1)

            def body(b):
                mix = not (isinstance(b, int) and b == 0)
                for f in range(FT):
                    if f < FT - 1:
                        low_parts(b, f + 1)
                    if mix and f == 0:
                        inverse_root_mixed(b * 2 - 2)
                    if mix and f == 5:
                        inverse_root_mixed(b * 2 - 1)
                    if f == 7 and not last(b):
                        inverse_root(b + 1)
                if not last(b):
                    low_parts(b + 1, 0)

            loop(pool, body)
            inverse_root_mixed(BATCH * 2 - 2)
            inverse_root_mixed(BATCH * 2 - 1)

        @block.vector
        def _(dve):
            def x_tile(b, j):
                return x_sb[:, bass.ds(b * SEQ_T + j, 1), :].rearrange("p o d -> p (o d)")

            def variance(b):
                ch = Chain(dve, s["ch"], b * STATS)
                norm_stats(dve, ch, [x_tile(b, j) for j in range(SEQ_T)], stats, mv, ve).then_inc(s["var"], 1)
                assert ch.n == STATS

            def normed(b):
                dve.wait_ge(s["rstd"], b + 1)
                need(dve, s["xn_out"], b * 16 - 16)
                need(dve, s["m_xt_full"], b * SEQ_T - SEQ_T)
                for j in range(SEQ_T):
                    dve.tensor_scalar(xn[:, j, :], x_tile(b, j), mv[:, j, 0:1], rstd[:, j:j + 1],
                                      ALU.subtract, ALU.mult).then_inc(s["xn_made"], 1)

            def low_x(b):
                for j in range(SEQ_T):
                    dve.wait_ge(s["xt_evac"], b * SEQ_T + j + 1)
                    part = slice(j * P, (j + 1) * P)
                    dve.tensor_tensor(xT[:, 1, :, part], ps_x[j][:, :].rearrange("p (k c) -> p k c", k=KT),
                                      xT[:, 0, :, part], ALU.subtract).then_inc(s["x_lo"], 1)

            variance(0)
            normed(0)
            low_x(0)

            SCALE, VAR2, SELECT, PLACE, ROUTE_OPS = 8, 15, 23, 34, 49

            def chain(m, at):
                return Chain(dve, s["m_ch"], m * ROUTE_OPS + at)

            def add_columns(m, js):
                for j in js:
                    dve.wait_ge(s["a_full"], m * SEQ_T + j + 1)
                    dve.scalar_tensor_tensor(x_tile(m, j), ps_m[j % 2][:, :], g["mix"][:, 1:2], x_tile(m, j),
                                             ALU.mult, ALU.add).then_inc(s["a_used"], 1)

            def add_rows(m, js):
                for j in js:
                    dve.wait_ge(s["a_used"], m * SEQ_T + j + 1)
                    dve.scalar_tensor_tensor(x_tile(m, j), kept[:, j, :], g["mix"][:, 1:2], x_tile(m, j),
                                             ALU.mult, ALU.add).then_inc(s["x_new"], 1)

            def mixing(m, step):
                tiles = [x_tile(m, j) for j in range(SEQ_T)]
                if step == 0:
                    dve.wait_ge(s["o_add"], m * SEQ_T + SEQ_T)
                    stand(dve)
                    ch = chain(m, 0)
                    norm_stats(dve, ch, tiles, stats3, mv3, ve3).then_inc(s["m_var"], 1)
                    assert ch.n == SCALE
                if step == 1:
                    ch = chain(m, SCALE)
                    dve.wait_ge(s["m_rstd"], m * 2 + 1)
                    ch.link(dve.tensor_scalar(shift[:, :], rstd3[:, :], g["mix"][:, 0:1], None, ALU.mult))
                    ch.link(dve.tensor_scalar(scl[:, :], shift[:, :], 1.0, None, ALU.add))
                    ch.link(dve.scalar_tensor_tensor(shift[:, :], shift[:, :], -1.0, mv3[:, :, 0], ALU.mult, ALU.mult))
                    for j in range(SEQ_T):
                        ch.add(dve.tensor_scalar(tiles[j], tiles[j], scl[:, j:j + 1], shift[:, j:j + 1],
                                                 ALU.mult, ALU.add))
                    ch.now()
                    assert ch.n == VAR2 - SCALE
                if step == 2:
                    add_columns(m, (0, 1))
                if step == 3:
                    add_rows(m, (0, 1))
                if step == 4:
                    add_columns(m, (2, 3))
                    add_rows(m, (2, 3))
                if step == 5:
                    dve.wait_ge(s["x_new"], m * SEQ_T + SEQ_T)
                    stand(dve)
                    ch = chain(m, VAR2)
                    norm_stats(dve, ch, tiles, stats3, mv3, ve3).then_inc(s["m_var"], 1)
                    assert ch.n == SELECT - VAR2
                if step == 6:
                    dve.wait_ge(s["m_rstd"], m * 2 + 2)
                    if isinstance(m, int):
                        need(dve, s["xn_out"], m * 16)
                    for j in range(SEQ_T):
                        dve.tensor_scalar(xn[:, j, :], tiles[j], mv3[:, j, 0:1], rstd3[:, j:j + 1],
                                          ALU.subtract, ALU.mult).then_inc(s["m_xn"], 1)

            def routing(m, step):
                if step == 8:
                    ch = chain(m, SELECT)
                    dve.wait_ge(s["l_full"], m + 1)
                    ch.link(dve.tensor_copy(logit[:, :, :], ps_m[0][:, 0:SEQ_T * EXPERTS]
                                            .rearrange("p (j e) -> p j e", j=SEQ_T)))
                    stand(dve)
                    for j in range(SEQ_T):
                        ch.add(dve.max(top8[:, j, :], logit[:, j, :]))
                    ch.now()
                    dve.tensor_scalar(nmax[:, :], top8[:, :, 0], -1.0, None, ALU.mult).then_inc(s["nmax"], 1)
                    for j in range(SEQ_T):
                        ch.add(dve.match_replace(rest[:, j, :], top8[:, j, :], logit[:, j, :], LOWEST))
                    ch.now()
                    ch.link(dve.tensor_tensor(sel[:, :, :], rest[:, :, :], logit[:, :, :], ALU.not_equal))
                    dve.tensor_copy(selb[:, :, :], sel[:, :, :]).then_inc(s["selb_made"], 1)
                    ch.link(dve.tensor_reduce(count[:, :], sel[:, :, :].rearrange("p j e -> p e j"), AX, ALU.add))
                    assert ch.n == PLACE - SELECT
                if step == 9:
                    ch = chain(m, PLACE)
                    dve.wait_ge(s["const"], 5)
                    dve.wait_ge(s["p_full"], m + 1)
                    places = ps_m[1][:, 0:SEQ_T * EXPERTS].rearrange("p (j e) -> p j e", j=SEQ_T)
                    ch.link(dve.scalar_tensor_tensor(valid[:, :, :], places, float(CAP), sel[:, :, :],
                                                     ALU.is_lt, ALU.mult))
                    dve.scalar_tensor_tensor(posp[:, :, :], places, 1.0, valid[:, :, :], ALU.add, ALU.mult)\
                        .then_inc(s["routed"], 1)
                    dve.wait_ge(s["routed"], m + 1)
                    ch.add(dve.tensor_scalar(r["place"][:, bass.ds(m * SEQ_T, SEQ_T), :], posp[:, :, :], -1.0, None,
                                             ALU.add))
                    ch.link(dve.tensor_tensor(taken[:, :], taken[:, :], count[:, :], ALU.add))
                    ch.add(dve.tensor_copy(takenb[:, :], taken[:, :]))
                    dve.wait_ge(s["prob_done"], m * SEQ_T + SEQ_T)
                    ch.link(dve.reciprocal(rden[:, :], psum_e[:, :]))
                    ch.link(dve.tensor_scalar(rden[:, :], rden[:, :], g["th"][:, 3:4], None, ALU.mult))
                    for j in range(SEQ_T):
                        ch.add(dve.scalar_tensor_tensor(w[:, j, :], prob[:, j, :], rden[:, j:j + 1], valid[:, j, :],
                                                        ALU.mult, ALU.mult))
                    ch.now()
                    for part in range(3):
                        dst = r["parts"][:, bass.ds(m * SEQ_T, SEQ_T), part, :]
                        ch.link(dve.tensor_copy(dst, w[:, :, :]))
                        if part < 2:
                            ch.link(dve.tensor_tensor(w[:, :, :], w[:, :, :], dst, ALU.subtract))
                    assert ch.n == ROUTE_OPS - PLACE

            def body(b):
                mix = not (isinstance(b, int) and b == 0)
                for f in range(FT):
                    n = b * FT + f
                    dve.wait_ge(s["tanh_done"], n + 1)
                    dve.scalar_tensor_tensor(u[:, :], th[:, :], 1.0, ps_g[:, :], ALU.add, ALU.mult)\
                        .then_inc(s["u_made"], 1)
                    dve.wait_ge(s["u_full"], n + 1)
                    dve.wait_ge(s["u_made"], n + 1)
                    dve.scalar_tensor_tensor(h[:, :], u[:, :], 0.5, ps_u[:, :], ALU.mult, ALU.mult)\
                        .then_inc(s["h_made"], 1)
                    dve.wait_ge(s["h_hi"], n + 1)
                    dve.tensor_tensor(hcut[:, f % 2, 1, :], h[:, :], hcut[:, f % 2, 0, :], ALU.subtract)\
                        .then_inc(s["h_lo"], 1)
                    if mix:
                        mixing(b - 1, f)
                    if f == 7 and not last(b):
                        variance(b + 1)
                    if f == 8 and not last(b):
                        normed(b + 1)
                    if mix:
                        routing(b - 1, f)
                if not last(b):
                    low_x(b + 1)
                dve.wait_ge(s["down"], b * FT + FT)
                for j in range(SEQ_T):
                    dve.scalar_tensor_tensor(x_tile(b, j), ps_o[j][:, :], g["th"][:, 2:3], x_tile(b, j),
                                             ALU.mult, ALU.add).then_inc(s["o_add"], 1)

            loop(dve, body)
            for step in range(FT):
                mixing(BATCH - 1, step)
                routing(BATCH - 1, step)


def phase_experts(nc, a, ident, g, r):
    with ExitStack() as stack:
        sb, banks, sem = scoped(nc, stack)
        GROUP = 4
        raw = {w: sb("raw_" + w, [P, 2, KT * FE]) for w in "gud"}
        cut = {w: sb("cut_" + w, [P, 2, 2, KT * FE], F32R) for w in "gud"}
        slots = sb("slots", [P, CAP])
        slotsb = sb("slotsb", [P, CAP], BF16)
        spare = sb("spare", [P, HALVES])
        cur = sb("cur", [P, 2, TILES])
        pick = sb("pick_e", [P, 2, TILES, CAP], BF16)
        vals = sb("vals", [P, 2, TILES, 6], BF16)
        table = sb("table", [P, HALVES, 6])
        wsum = sb("wsum_e", [P, HALVES])
        weight = sb("weight", [P, GROUP, HALVES])
        tokf = sb("tokf", [P, HALVES])
        empty = sb("empty", [P, HALVES])
        src_row = sb("src_row", [P, GROUP, HALVES], U32)
        dst_row = sb("dst_row", [P, GROUP, HALVES], U32)
        xg = sb("xg", [P, 2, HALVES, DIM])
        xgT = sb("xgT", [P, 2, KT, CAP], F32R)
        th = sb("th_e", [P, FET * CAP])
        u = sb("u_e", [P, FET * CAP])
        hT = sb("hT_e", [P, FET * CAP])
        hcut = sb("hcut", [P, 2, FET * CAP], F32R)
        y = sb("y_e", [P, 2, HALVES, DIM])
        ps_tab, ps_g, ps_u = banks("ps_tgu", 3)
        ps_x = banks("ps_xg", 2)
        ps_y = banks("ps_y", 2)
        s_w = [sem(f"e_w{j}") for j in range(2)]
        s_gat = [sem(f"e_gat{j}") for j in range(2)]
        s = {n: sem("e_" + n) for n in """const slots cur_made pick_made tab_full tab_read ch tabled xt_full xt_evac
            gu_full tanh_done u_made h_made y_full y_evac scat g_hi g_lo u_hi u_lo d_hi d_lo h_hi h_lo x_lo""".split()}
        block = stack.enter_context(nc.Block())

        def loop(eng, body):
            body(0)
            with eng.Fori(1, EXPERTS // GROUP - 1) as i:
                body(i)
            body(EXPERTS // GROUP - 1)

        def last_group(i):
            return isinstance(i, int) and i > 0

        def count2(i, q, ahead=0):
            return i * (GROUP // 2) + (q + ahead) // 2 + 1

        @block.sync
        def _(sp):
            def body(i):
                for q in range(GROUP):
                    e, k = i * GROUP + q, q % 2
                    one = bass.ds(e, 1)
                    for w, name, n in (("g", "w_gate", KT), ("u", "w_up", KT), ("d", "w_down", FET)):
                        need(sp, s[w + "_hi"], e - 1)
                        need(sp, s[w + "_lo"], e - 1)
                        sp.dma_start(raw[w][:, k, :].rearrange("p (k f) -> p k f", k=n),
                                     a[name][one, :, :].rearrange("o (k p) f -> p (o k) f", p=P)).then_inc(s_w[k], 16)

            loop(sp, body)
            sp.wait_ge(s["scat"], 32 * EXPERTS)

        @block.gpsimd
        def _(pool):
            pool.iota(slots[:, :], pattern=[[1, CAP]], base=0, channel_multiplier=0,
                      allow_small_or_imprecise_dtypes=True).then_inc(s["const"], 1)
            pool.iota(spare[:, :], pattern=[[P, HALVES]], base=T, channel_multiplier=1,
                      allow_small_or_imprecise_dtypes=True).then_inc(s["const"], 1)
            for k in range(2):
                pool.iota(vals[:, k, :, 3], pattern=[[1, TILES]], base=0, channel_multiplier=0,
                          allow_small_or_imprecise_dtypes=True).then_inc(s["const"], 1)
                pool.iota(vals[:, k, :, 4], pattern=[[0, TILES]], base=0, channel_multiplier=1,
                          allow_small_or_imprecise_dtypes=True).then_inc(s["const"], 1)
                pool.memset(vals[:, k, :, 5], 1.0).then_inc(s["const"], 1)

            def gather(i, q, ahead):
                e = i * GROUP + q + ahead
                qq = (q + ahead) % GROUP
                pool.wait_ge(s["tabled"], e + 1)
                need(pool, s["xt_full"], e * 2 - 2)
                stand(pool)
                for n in range(HALVES):
                    pool.indirect_dma_start(xg[:, qq % 2, n, :], None, a["xn"][:, :],
                                            bass.IndirectOffsetOnAxis(ap=src_row[:, qq, n:n + 1], axis=0))\
                        .then_inc(s_gat[qq % 2], 16)

            def scatter(i, q, back):
                e = i * GROUP + q - back
                qq = (q - back) % GROUP
                pool.wait_ge(s["y_evac"], e * 2 + 2)
                need(pool, s["scat"], e * 32)
                stand(pool)
                for n in range(HALVES):
                    pool.indirect_dma_start(a["acc"][:, :], bass.IndirectOffsetOnAxis(ap=dst_row[:, qq, n:n + 1], axis=0),
                                            y[:, qq % 2, n, :], None, compute_op=ALU.add)\
                        .then_inc(s["scat"], 16)

            def low_part(w, i, q, ahead):
                e, k = i * GROUP + q + ahead, (q + ahead) % 2
                pool.wait_ge(s[w + "_hi"], e + 1)
                pool.tensor_tensor(cut[w][:, k, 1, :], raw[w][:, k, :], cut[w][:, k, 0, :], ALU.subtract)\
                    .then_inc(s[w + "_lo"], 1)

            gather(0, 0, 0)
            low_part("g", 0, 0, 0)
            low_part("u", 0, 0, 0)
            gather(0, 1, 0)

            def body(i):
                for q in range(GROUP):
                    if not (isinstance(i, int) and i == 0 and q == 0):
                        scatter(i, q, 1)
                    if not (last_group(i) and q == GROUP - 1):
                        low_part("g", i, q, 1)
                        low_part("u", i, q, 1)
                    if not (last_group(i) and q >= GROUP - 2):
                        gather(i, q, 2)

            loop(pool, body)
            scatter(EXPERTS // GROUP - 1, GROUP, 1)

        @block.tensor
        def _(pe):
            def tabulate(i, q, ahead):
                e, k = i * GROUP + q + ahead, (q + ahead) % 2
                pe.wait_ge(s["pick_made"], e + 1)
                need(pe, s["tab_read"], e)
                for n in range(HALVES):
                    for t in range(TILES):
                        mm = pe.matmul(ps_tab[:, n * 6:(n + 1) * 6], pick[:, k, t, n * P:(n + 1) * P],
                                       vals[:, k, t, :], start=(t == 0), stop=(t == TILES - 1))
                mm.then_inc(s["tab_full"], 1)

            def turn(i, q, ahead):
                e, k = i * GROUP + q + ahead, (q + ahead) % 2
                pe.wait_ge(s_gat[k], count2(i, q, ahead) * 32)
                for n in range(HALVES):
                    need(pe, s["xt_evac"], e * 2 - 1 + n)
                    for c in range(KT):
                        tr = pe.transpose(ps_x[n][:, c * P:(c + 1) * P], xg[:, k, n, c * P:(c + 1) * P], ident[:, :])
                    tr.then_inc(s["xt_full"], 1)

            def gate_up(i, q):
                e, k = i * GROUP + q, q % 2
                pe.wait_ge(s["xt_evac"], e * 2 + 2)
                need(pe, s["h_made"], e)
                for w, ps in (("g", ps_g), ("u", ps_u)):
                    pe.wait_ge(s[w + "_lo"], e + 1)
                    for f in range(FET):
                        for c in range(KT):
                            cols = slice(c * FE + f * P, c * FE + (f + 1) * P)
                            low = (lambda: pe.wait_ge(s["x_lo"], e + 1)) if w == "g" and f == c == 0 else None
                            mm = split_product(pe, ps[:, f * CAP:(f + 1) * CAP],
                                               (cut[w][:, k, 0, cols], cut[w][:, k, 1, cols]),
                                               (xgT[:, 0, c, :], xgT[:, 1, c, :]), c == 0, c == KT - 1, low)
                    mm.then_inc(s["gu_full"], 1)

            def down(i, q):
                e, k = i * GROUP + q, q % 2
                pe.wait_ge(s["h_hi"], e + 1)
                pe.wait_ge(s["d_lo"], e + 1)
                high, low = cut["d"][:, k, 0, :], cut["d"][:, k, 1, :]
                for n in range(HALVES):
                    need(pe, s["y_evac"], e * 2 - 1 + n)
                    for f in range(FET):
                        slots_n, cols = slice(f * CAP + n * P, f * CAP + (n + 1) * P), slice(f * DIM, (f + 1) * DIM)
                        pe.matmul(ps_y[n][:, :], hcut[:, 0, slots_n], high[:, cols], start=(f == 0), stop=False)
                        pe.matmul(ps_y[n][:, :], hcut[:, 0, slots_n], low[:, cols], start=False, stop=False)
                    if n == 0:
                        pe.wait_ge(s["h_lo"], e + 1)
                    for f in range(FET):
                        slots_n, cols = slice(f * CAP + n * P, f * CAP + (n + 1) * P), slice(f * DIM, (f + 1) * DIM)
                        mm = pe.matmul(ps_y[n][:, :], hcut[:, 1, slots_n], high[:, cols], start=False,
                                       stop=(f == FET - 1))
                    mm.then_inc(s["y_full"], 1)

            tabulate(0, 0, 0)
            tabulate(0, 1, 0)
            turn(0, 0, 0)

            def body(i):
                for q in range(GROUP):
                    gate_up(i, q)
                    if not (last_group(i) and q >= GROUP - 2):
                        tabulate(i, q, 2)
                    if not (last_group(i) and q == GROUP - 1):
                        turn(i, q, 1)
                    down(i, q)

            loop(pe, body)

        @block.scalar
        def _(act):
            def evac_x(i, q, ahead):
                e = i * GROUP + q + ahead
                for n in range(HALVES):
                    act.wait_ge(s["xt_full"], e * 2 + n + 1)
                    act.activation(xgT[:, 0, :, n * P:(n + 1) * P], ps_x[n][:, :].rearrange("p (k c) -> p k c", k=KT),
                                   ACT.Copy).then_inc(s["xt_evac"], 1)

            def high_part(w, i, q, ahead):
                e, k = i * GROUP + q + ahead, (q + ahead) % 2
                act.wait_ge(s_w[k], count2(i, q, ahead) * 48)
                need(act, s["y_full"], e * 2 - 2)
                act.activation(cut[w][:, k, 0, :], raw[w][:, k, :], ACT.Copy).then_inc(s[w + "_hi"], 1)

            for w in "gud":
                high_part(w, 0, 0, 0)
            evac_x(0, 0, 0)

            def body(i):
                for q in range(GROUP):
                    e = i * GROUP + q
                    ahead = not (last_group(i) and q == GROUP - 1)
                    if ahead:
                        high_part("g", i, q, 1)
                        high_part("u", i, q, 1)
                    act.wait_ge(s["gu_full"], e * 2 + 1)
                    need(act, s["u_made"], e)
                    act.activation(th[:, :], ps_g[:, :], ACT.Tanh, scale=0.5).then_inc(s["tanh_done"], 1)
                    if ahead:
                        high_part("d", i, q, 1)
                    act.wait_ge(s["h_made"], e + 1)
                    need(act, s["y_full"], e * 2)
                    act.activation(hcut[:, 0, :], hT[:, :], ACT.Copy).then_inc(s["h_hi"], 1)
                    if ahead:
                        evac_x(i, q, 1)
                    need(act, s["scat"], e * 32 - 32)
                    for n in range(HALVES):
                        act.wait_ge(s["y_full"], e * 2 + n + 1)
                        act.activation(y[:, q % 2, n, :], ps_y[n][:, :], ACT.Copy, scale=weight[:, q, n:n + 1])\
                            .then_inc(s["y_evac"], 1)

            loop(act, body)

        @block.vector
        def _(dve):
            def make_pick(i, q, ahead):
                e, k = i * GROUP + q + ahead, (q + ahead) % 2
                need(dve, s["tab_full"], e - 1)
                one = bass.ds(e, 1)
                dve.tensor_copy(cur[:, k, :], r["place"][:, :, one].rearrange("p t o -> p (t o)"))\
                    .then_inc(s["cur_made"], 1)
                dve.tensor_copy(vals[:, k, :, 0:3], r["parts"][:, :, :, one].rearrange("p t c o -> p t (c o)"))\
                    .then_inc(s["cur_made"], 1)
                dve.wait_ge(s["cur_made"], e * 2 + 2)
                for t in range(TILES):
                    ins = dve.tensor_scalar(pick[:, k, t, :], slotsb[:, :], cur[:, k, t:t + 1], None, ALU.is_equal)
                ins.then_inc(s["pick_made"], 1)

            PER = 5

            def make_table(i, q, ahead):
                e, qq = i * GROUP + q + ahead, (q + ahead) % GROUP
                dve.wait_ge(s["tab_full"], e + 1)
                need(dve, s["tabled"], e)
                dve.tensor_copy(table[:, :, :], ps_tab[:, 0:HALVES * 6].rearrange("p (n c) -> p n c", n=HALVES))\
                    .then_inc(s["tab_read"], 1)
                dve.wait_ge(s["tab_read"], e + 1)
                need(dve, s["scat"], e * 32 - 96)
                ch = Chain(dve, s["ch"], e * PER)
                ch.add(dve.tensor_tensor(wsum[:, :], table[:, :, 2], table[:, :, 1], ALU.add))
                ch.add(dve.scalar_tensor_tensor(tokf[:, :], table[:, :, 3], float(P), table[:, :, 4],
                                                ALU.mult, ALU.add))
                ch.link(dve.tensor_tensor(empty[:, :], table[:, :, 5], spare[:, :], ALU.mult))
                ch.add(dve.tensor_tensor(weight[:, qq, :], wsum[:, :], table[:, :, 0], ALU.add))
                ch.link(dve.tensor_tensor(empty[:, :], spare[:, :], empty[:, :], ALU.subtract))
                dve.tensor_copy(src_row[:, qq, :], tokf[:, :])
                dve.tensor_tensor(dst_row[:, qq, :], tokf[:, :], empty[:, :], ALU.add).then_inc(s["tabled"], 1)
                assert ch.n == PER

            def low_part_d(i, q, ahead):
                e, k = i * GROUP + q + ahead, (q + ahead) % 2
                dve.wait_ge(s["d_hi"], e + 1)
                dve.tensor_tensor(cut["d"][:, k, 1, :], raw["d"][:, k, :], cut["d"][:, k, 0, :], ALU.subtract)\
                    .then_inc(s["d_lo"], 1)

            def low_part_x(i, q, ahead):
                e = i * GROUP + q + ahead
                dve.wait_ge(s["xt_evac"], e * 2 + 2)
                for n in range(HALVES):
                    half = slice(n * P, (n + 1) * P)
                    ins = dve.tensor_tensor(xgT[:, 1, :, half], ps_x[n][:, :].rearrange("p (k c) -> p k c", k=KT),
                                            xgT[:, 0, :, half], ALU.subtract)
                ins.then_inc(s["x_lo"], 1)

            dve.wait_ge(s["const"], 8)
            dve.tensor_copy(slotsb[:, :], slots[:, :]).then_inc(s["slots"], 1)
            dve.wait_ge(s["slots"], 1)
            make_pick(0, 0, 0)
            make_table(0, 0, 0)
            make_pick(0, 1, 0)
            make_table(0, 1, 0)
            low_part_x(0, 0, 0)
            low_part_d(0, 0, 0)
            make_pick(0, 2, 0)

            def body(i):
                for q in range(GROUP):
                    e = i * GROUP + q
                    dve.wait_ge(s["tanh_done"], e + 1)
                    dve.scalar_tensor_tensor(u[:, :], th[:, :], 1.0, ps_g[:, :], ALU.add, ALU.mult)\
                        .then_inc(s["u_made"], 1)
                    dve.wait_ge(s["gu_full"], e * 2 + 2)
                    dve.wait_ge(s["u_made"], e + 1)
                    dve.scalar_tensor_tensor(hT[:, :], u[:, :], 0.5, ps_u[:, :], ALU.mult, ALU.mult)\
                        .then_inc(s["h_made"], 1)
                    if not (last_group(i) and q >= GROUP - 2):
                        make_table(i, q, 2)
                    dve.wait_ge(s["h_hi"], e + 1)
                    dve.tensor_tensor(hcut[:, 1, :], hT[:, :], hcut[:, 0, :], ALU.subtract).then_inc(s["h_lo"], 1)
                    if not (last_group(i) and q == GROUP - 1):
                        low_part_x(i, q, 1)
                        low_part_d(i, q, 1)
                    if not (last_group(i) and q >= GROUP - 3):
                        make_pick(i, q, 3)

            loop(dve, body)


def build(nc, a):
    with ExitStack() as stack:
        def sb(name, shape, dt=F32):
            return stack.enter_context(nc.sbuf_tensor(name, shape, dt))

        ident = sb("ident", [P, P])
        g = {"raw": sb("g_raw", [P, 5]), "th": sb("g_th", [P, 5]), "tmp": sb("g_tmp", [P, 3]),
             "mix": sb("g_mix", [P, 2]), "lut": sb("g_lut", [P, LUT])}
        with nc.semaphore("s_ident") as s_ident, nc.Block() as block:
            @block.gpsimd
            def _(pool):
                pool.memset(ident[:, :], 0.0).then_inc(s_ident, 1)
                pool.wait_ge(s_ident, 1)
                pool.affine_select(out=ident[:, :], in_=ident[:, :], compare_op=ALU.not_equal, fill=1.0, base=0,
                                   pattern=[[-1, P]], channel_multiplier=1).then_inc(s_ident, 1)

        with nc.sbuf_tensor("x_sb", [P, TILES, DIM], F32) as x_sb:
            with nc.sbuf_tensor("xT", [P, KT, T], F32) as xT:
                with nc.sbuf_tensor("kvT", [P, 2, T], F32R) as kvT, nc.sbuf_tensor("kv", [P, TILES, D_C], F32) as kv:
                    phase_prepare(nc, a, x_sb, xT, kvT, kv, ident, g)
                    phase_attention(nc, a, x_sb, xT, kvT, kv, ident, g)
            with nc.sbuf_tensor("place", [P, TILES, EXPERTS], F32) as place, \
                    nc.sbuf_tensor("parts", [P, TILES, 3, EXPERTS], BF16) as parts:
                r = {"place": place, "parts": parts}
                phase_swiglu_mix(nc, a, x_sb, ident, g, r)
                phase_experts(nc, a, ident, g, r)


def rope(length, dim):
    inv = (1.0 / 10000.0 ** (np.arange(0, dim, 2, dtype=np.float32) / np.float32(dim))).astype(np.float32)
    f = np.arange(length, dtype=np.float32)[:, None] * inv[None, :]
    return np.repeat(np.sin(f), 2, axis=-1), np.repeat(np.cos(f), 2, axis=-1)


def tables():
    half = D_CQ // 2
    sin, cos = rope(SEQ, D_CQ)
    sign = np.where(np.arange(D_CQ) < half, -1.0, 1.0).astype(np.float32)
    cols = latent_columns()
    rot = np.stack([cos[:, c].T for c in cols[:3]] + [(sin * sign)[:, c].T for c in cols[:3]], 1)
    sin, cos = rope(SEQ, D_C)
    sin = sin * np.where(np.arange(D_C) < D_C // 2, -1.0, 1.0).astype(np.float32)
    by_token = [m.reshape(SEQ_T, P, D_C).transpose(1, 0, 2) for m in (cos, sin)]
    return {"rot": rot, "ktab": np.stack([cos.T, sin.T], 1), "ttab": by_token[0], "stab": by_token[1]}


def latent_columns():
    half = D_CQ // 2
    a, rest = np.arange(P), np.arange(P, half)
    return [a, a + half, np.concatenate([rest, rest + half]), np.concatenate([rest + half, rest])]


def kernel(**inputs):
    import concourse.bacc as bacc
    from concourse.bass_utils import run_bass_kernel_spmd

    v = {k: np.asarray(x) for k, x in inputs.items()}
    cols = latent_columns()
    pad = lambda m: np.concatenate([m, np.full((FT * P - INTER, m.shape[1]), LUT, m.dtype)])
    by_tile = lambda m: pad(m).reshape(FT, P, KT, P).transpose(3, 0, 2, 1).reshape(P, FT, KT * P)
    down = pad(v["L0_ffn_down_idx"].T).reshape(FT, P, DIM).transpose(1, 0, 2)
    idx = np.concatenate([by_tile(v["L0_ffn_gate_idx"]), by_tile(v["L0_ffn_up_idx"]), down], 2)
    ctx = v["ctx_512"].reshape(T, D_C)
    arrays = {
        "x": v["x"].reshape(T, DIM), "ctx": ctx, "ctxT": ctx.T,
        "g_xattn": v["g_xattn"], "g_ffn": v["g_ffn"], "gamma": v["L1_xattn_gamma_raw"].reshape(1),
        "lut": v["L0_ffn_lut"],
        "wqa": v["L1_xattn_Wq"].T, "wka": v["L1_xattn_Wk"].T,
        "wq": v["L0_xattn_Wq"].T.reshape(KT, P, HEADS, HK).transpose(2, 1, 0, 3).reshape(HEADS, P, KT * HK),
        "wc": v["L0_xattn_w_kc_q"][:, :, np.concatenate(cols)],
        "wqrT": v["L0_xattn_W_qr"][:, np.concatenate(cols[:3]), :].transpose(0, 2, 1),
        "wkrT": v["L0_xattn_W_kr"].transpose(0, 2, 1),
        "wkc": v["L0_xattn_w_kc_kv"],
        "woT": v["L0_xattn_Wo"].T.reshape(HEADS, HK, DIM),
        "idx": idx.reshape(P, HEADS, LUT_CHUNK).transpose(1, 0, 2),
        "gw": v["L1_ffn_gate_w"].T.reshape(KT, P, EXPERTS).transpose(1, 0, 2),
        "w_gate": v["L1_ffn_w_gate"], "w_up": v["L1_ffn_w_up"], "w_down": v["L1_ffn_w_down"],
        **tables(),
    }
    arrays = {"in_" + k: np.ascontiguousarray(x) for k, x in arrays.items()}
    nc = bacc.Bacc("TRN2", target_bir_lowering=False, num_devices=1)
    a = {k[3:]: nc.dram_tensor(k, x.shape, mybir.dt.from_np(x.dtype), kind="ExternalInput").ap()
         for k, x in arrays.items()}
    for name, shape in (("w1", (HEADS, P, D_CQ)), ("w2", (HEADS, P, DIM)), ("aff", (TILES, P, SEQ)),
                        ("kept", (TILES, P, SEQ)), ("lutw", (P, LUT_W)), ("xn", (T, DIM))):
        a[name] = nc.dram_tensor("via_" + name, shape, F32).ap()
    a["acc"] = nc.dram_tensor("out", (T + CAP, DIM), F32, kind="ExternalOutput").ap()
    build(nc, a)
    result = run_bass_kernel_spmd(nc, [arrays], core_ids=[0])
    return result.results[0]["out"][:T].reshape(BATCH, SEQ, DIM)
```
